# Optimizing a Trainium2 kernel written in Bass

```python
import numpy as np
import jax
import jax.numpy as jnp

def _softmax(x, axis=-1):
    return jax.nn.softmax(x, axis=axis)

def _gelu(x):
    return jax.nn.gelu(x, approximate=True)

def _silu(x):
    return jax.nn.silu(x)

def _sigmoid(x):
    return jax.nn.sigmoid(x)

def _layernorm(x, axis=-1, eps=1e-05):
    m = jnp.mean(x, axis=axis, keepdims=True)
    v = jnp.var(x, axis=axis, keepdims=True)
    return (x - m) / jnp.sqrt(v + eps)

def _scatter_add(tgt, idx, src, axis=0):
    return tgt.at[idx].add(src)

def _segment_sum(src, seg, n):
    return jax.ops.segment_sum(src, seg, n)
kernel_name = 'mk_gnn_resnorm_d4_gnn_r8_07f14a'

def setup_inputs(seed: int=0):
    np.random.seed(seed)
    _w = jnp.asarray

    def _rec_inputs():
        import jax
        import jax.numpy as jnp
        _gk = jax.random.key(seed)
        x = -0.0005121 + 1.001 * jax.random.normal(jax.random.fold_in(_gk, 1), (12500, 64), jnp.float32)
        src = jax.random.randint(jax.random.fold_in(_gk, 2), (200000,), 0, 12500, jnp.int32)
        dst = jnp.minimum((12500 * jax.random.uniform(jax.random.fold_in(_gk, 3), (200000,)) ** 2.0).astype(jnp.int32), 99999)
        _o = jnp.argsort(dst, stable=True)
        src = src[_o]
        dst = dst[_o]
        edge_weight = jax.random.uniform(jax.random.fold_in(_gk, 12), (200000,), jnp.float32, 0.0, 0.999998)
        edge_weight1 = jax.random.uniform(jax.random.fold_in(_gk, 13), (200000, 1), jnp.float32, 0.0, 0.999999)
        return (x, src, dst, edge_weight, edge_weight1)
    x, src, dst, edge_weight, edge_weight1 = _rec_inputs()

    def _L0_gnn_setup():
        import jax, jax.numpy as jnp
        import numpy as np
        N_NODES = 6250

        def _gcn_conv(x, W, b, src, dst, dinv, n):
            h = x @ W
            norm = dinv[src] * dinv[dst]
            msg = h[src] * norm[:, None]
            out = jax.ops.segment_sum(msg, dst, num_segments=n)
            return out + b
        key = jax.random.key(seed)
        ks = jax.random.split(key, 10)
        n, e, cin, chid = (N_NODES, 75000, 64, 128)
        x = jax.random.normal(ks[0], (n, cin), dtype=jnp.float32)
        edge_index = jax.random.randint(ks[1], (2, e), 0, n, dtype=jnp.int64)

        def glorot(k, fi, fo):
            s = jnp.sqrt(6.0 / (fi + fo)).astype(jnp.float32)
            return jax.random.uniform(k, (fi, fo), jnp.float32, -s, s)
        return {'x': x, 'edge_index': edge_index, 'W1': glorot(ks[2], cin, chid), 'b1': jnp.zeros((chid,), jnp.float32), 'W2': glorot(ks[3], chid, cin), 'b2': jnp.zeros((cin,), jnp.float32), 'W3': glorot(ks[4], cin, chid), 'b3': jnp.zeros((chid,), jnp.float32), 'W4': glorot(ks[5], chid, cin), 'b4': jnp.zeros((cin,), jnp.float32)}
    _L0_gnn_all = _L0_gnn_setup()
    _L0_gnn_in = {k: v for k, v in _L0_gnn_all.items() if k in ('W1', 'b1', 'W2', 'b2', 'W3', 'b3', 'W4', 'b4')}
    del _L0_gnn_all

    def _L1_gnn_setup():
        import jax, jax.numpy as jnp
        import numpy as np
        N_NODES = 6250
        N_EDGES = 100000
        D_FEAT = 64
        HIDDEN = 128

        def _ebm(edge_input, t, W1, b1, Wt, bt, W2, b2):
            t_emb = jax.nn.silu(t[:, None] * Wt + bt)
            h = jax.nn.silu(edge_input @ W1 + t_emb + b1)
            return h @ W2 + b2
        key = jax.random.key(seed)
        ks = jax.random.split(key, 8)
        x = jax.random.normal(ks[0], (N_NODES, D_FEAT), dtype=jnp.float32)
        edge_index = jax.random.randint(ks[1], (2, N_EDGES), 0, N_NODES, dtype=jnp.int64)
        t = jax.random.uniform(ks[2], (N_EDGES,), dtype=jnp.float32)
        s1 = 1.0 / np.sqrt(2 * D_FEAT)
        s2 = 1.0 / np.sqrt(HIDDEN)
        W1 = jax.random.normal(ks[3], (2 * D_FEAT, HIDDEN), dtype=jnp.float32) * s1
        b1 = jnp.zeros((HIDDEN,), dtype=jnp.float32)
        Wt = jax.random.normal(ks[4], (1, HIDDEN), dtype=jnp.float32)
        bt = jnp.zeros((HIDDEN,), dtype=jnp.float32)
        W2 = jax.random.normal(ks[5], (HIDDEN, 2 * D_FEAT), dtype=jnp.float32) * s2
        b2 = jnp.zeros((2 * D_FEAT,), dtype=jnp.float32)
        return {'x': x, 'edge_index': edge_index, 't': t, 'W1': W1, 'b1': b1, 'Wt': Wt, 'bt': bt, 'W2': W2, 'b2': b2}
    _L1_gnn_all = _L1_gnn_setup()
    _L1_gnn_in = {k: v for k, v in _L1_gnn_all.items() if k in ('W1', 'b1', 'Wt', 'bt', 'W2', 'b2')}
    del _L1_gnn_all

    def _L2_gnn_setup():
        import jax, jax.numpy as jnp
        import numpy as np
        N_NODES = 12500

        def _add_self_loops(edge_index, n):
            loop = jnp.arange(n, dtype=edge_index.dtype)
            src = jnp.concatenate([edge_index[0], loop])
            dst = jnp.concatenate([edge_index[1], loop])
            return (src, dst)

        def _gcn_conv(x, src, dst, n, W, b):
            h = x @ W
            deg = jnp.zeros((n,), h.dtype).at[dst].add(1.0)
            dinv = jnp.where(deg > 0, jax.lax.rsqrt(deg), 0.0)
            norm = dinv[src] * dinv[dst]
            msg = h[src] * norm[:, None]
            out = jax.ops.segment_sum(msg, dst, num_segments=n)
            return out + b
        key = jax.random.key(seed)
        ks = jax.random.split(key, 9)
        n, d_in, d_h, d_out = (N_NODES, 64, 64, 64)
        x = jax.random.normal(ks[0], (n, d_in), jnp.float32)
        edge_index = jax.random.randint(ks[1], (2, 150000), 0, n, jnp.int64)
        s = lambda k, sh: jax.random.normal(k, sh, jnp.float32) * (1.0 / np.sqrt(sh[0]))
        return {'x': x, 'edge_index': edge_index, 'W1': s(ks[2], (d_in, d_h)), 'b1': jnp.zeros((d_h,), jnp.float32), 'W2': s(ks[3], (d_h, d_out)), 'b2': jnp.zeros((d_out,), jnp.float32), 'Wl': s(ks[4], (d_out, d_out)), 'bl': jnp.zeros((d_out,), jnp.float32)}
    _L2_gnn_all = _L2_gnn_setup()
    _L2_gnn_in = {k: v for k, v in _L2_gnn_all.items() if k in ('W1', 'b1', 'W2', 'b2', 'Wl', 'bl')}
    del _L2_gnn_all

    def _L3_gnn_setup():
        import jax, jax.numpy as jnp
        import numpy as np
        N_NODES = 12500
        N_EDGES = 200000
        HID = 64
        N_LAYERS = 3
        BN_EPS = 1e-05
        key = jax.random.key(seed)
        ks = jax.random.split(key, 10)
        x = jax.random.normal(ks[0], (N_NODES, HID), dtype=jnp.float32)
        edge_index = jax.random.randint(ks[1], (2, N_EDGES), 0, N_NODES, dtype=jnp.int64)
        edge_atten = jax.random.uniform(ks[2], (N_EDGES, 1), dtype=jnp.float32)
        s = 1.0 / np.sqrt(HID)
        W1 = jax.random.normal(ks[3], (N_LAYERS, HID, HID), dtype=jnp.float32) * s
        b1 = jax.random.normal(ks[4], (N_LAYERS, HID), dtype=jnp.float32) * s
        gamma = jnp.ones((N_LAYERS, HID), dtype=jnp.float32)
        beta = jnp.zeros((N_LAYERS, HID), dtype=jnp.float32)
        W2 = jax.random.normal(ks[5], (N_LAYERS, HID, HID), dtype=jnp.float32) * s
        b2 = jax.random.normal(ks[6], (N_LAYERS, HID), dtype=jnp.float32) * s
        return {'x': x, 'edge_index': edge_index, 'edge_atten': edge_atten, 'W1': W1, 'b1': b1, 'gamma': gamma, 'beta': beta, 'W2': W2, 'b2': b2}
    _L3_gnn_all = _L3_gnn_setup()
    _L3_gnn_in = {k: v for k, v in _L3_gnn_all.items() if k in ('W1', 'b1', 'gamma', 'beta', 'W2', 'b2')}
    del _L3_gnn_all
    return {'x': x, 'src': src, 'dst': dst, 'edge_weight': edge_weight, 'edge_weight1': edge_weight1, 'L0_gnn_W1': _L0_gnn_in['W1'], 'L0_gnn_b1': _L0_gnn_in['b1'], 'L0_gnn_W2': _L0_gnn_in['W2'], 'L0_gnn_b2': _L0_gnn_in['b2'], 'L0_gnn_W3': _L0_gnn_in['W3'], 'L0_gnn_b3': _L0_gnn_in['b3'], 'L0_gnn_W4': _L0_gnn_in['W4'], 'L0_gnn_b4': _L0_gnn_in['b4'], 'L1_gnn_W1': _L1_gnn_in['W1'], 'L1_gnn_b1': _L1_gnn_in['b1'], 'L1_gnn_Wt': _L1_gnn_in['Wt'], 'L1_gnn_bt': _L1_gnn_in['bt'], 'L1_gnn_W2': _L1_gnn_in['W2'], 'L1_gnn_b2': _L1_gnn_in['b2'], 'L2_gnn_W1': _L2_gnn_in['W1'], 'L2_gnn_b1': _L2_gnn_in['b1'], 'L2_gnn_W2': _L2_gnn_in['W2'], 'L2_gnn_b2': _L2_gnn_in['b2'], 'L2_gnn_Wl': _L2_gnn_in['Wl'], 'L2_gnn_bl': _L2_gnn_in['bl'], 'L3_gnn_W1': _L3_gnn_in['W1'], 'L3_gnn_b1': _L3_gnn_in['b1'], 'L3_gnn_gamma': _L3_gnn_in['gamma'], 'L3_gnn_beta': _L3_gnn_in['beta'], 'L3_gnn_W2': _L3_gnn_in['W2'], 'L3_gnn_b2': _L3_gnn_in['b2']}

def reference(x, src, dst, edge_weight, edge_weight1, L0_gnn_W1, L0_gnn_b1, L0_gnn_W2, L0_gnn_b2, L0_gnn_W3, L0_gnn_b3, L0_gnn_W4, L0_gnn_b4, L1_gnn_W1, L1_gnn_b1, L1_gnn_Wt, L1_gnn_bt, L1_gnn_W2, L1_gnn_b2, L2_gnn_W1, L2_gnn_b1, L2_gnn_W2, L2_gnn_b2, L2_gnn_Wl, L2_gnn_bl, L3_gnn_W1, L3_gnn_b1, L3_gnn_gamma, L3_gnn_beta, L3_gnn_W2, L3_gnn_b2):
    import jax
    import jax.numpy as jnp

    def _L0_gnn_ref(x, edge_index, W1, b1, W2, b2, W3, b3, W4, b4):
        import jax, jax.numpy as jnp
        import numpy as np
        N_NODES = 6250

        def _gcn_conv(x, W, b, src, dst, dinv, n):
            h = x @ W
            norm = dinv[src] * dinv[dst]
            msg = h[src] * norm[:, None]
            out = jax.ops.segment_sum(msg, dst, num_segments=n)
            return out + b
        n = x.shape[0]
        loop = jnp.arange(n, dtype=edge_index.dtype)
        src = jnp.concatenate([edge_index[0], loop])
        dst = jnp.concatenate([edge_index[1], loop])
        deg = jax.ops.segment_sum(jnp.ones_like(dst, dtype=x.dtype), dst, num_segments=n)
        dinv = jnp.where(deg > 0, jax.lax.rsqrt(deg), 0.0)
        x_l1 = jax.nn.relu(_gcn_conv(x, W1, b1, src, dst, dinv, n))
        x_l2 = jax.nn.relu(_gcn_conv(x_l1, W2, b2, src, dst, dinv, n))
        x_l1_td = jax.nn.relu(_gcn_conv(x_l2, W3, b3, src, dst, dinv, n)) + x_l1
        x_out = jax.nn.relu(_gcn_conv(x_l1_td, W4, b4, src, dst, dinv, n)) + x
        return x_out

    def _L1_gnn_ref(x, edge_index, t, W1, b1, Wt, bt, W2, b2):
        import jax, jax.numpy as jnp
        import numpy as np
        N_NODES = 6250
        N_EDGES = 100000
        D_FEAT = 64
        HIDDEN = 128

        def _ebm(edge_input, t, W1, b1, Wt, bt, W2, b2):
            t_emb = jax.nn.silu(t[:, None] * Wt + bt)
            h = jax.nn.silu(edge_input @ W1 + t_emb + b1)
            return h @ W2 + b2
        row, col = (edge_index[0], edge_index[1])
        edge_input = jnp.concatenate([x[row], x[col]], axis=1)
        edge_output = _ebm(edge_input, t, W1, b1, Wt, bt, W2, b2)
        d = edge_output.shape[1] // 2
        src_update = edge_output[:, :d]
        tgt_update = edge_output[:, d:]
        update = jnp.concatenate([src_update, tgt_update], axis=0)
        idx = jnp.concatenate([row, col], axis=0)
        return jax.ops.segment_sum(update, idx, num_segments=x.shape[0])

    def _L2_gnn_ref(x, edge_index, W1, b1, W2, b2, Wl, bl):
        import jax, jax.numpy as jnp
        import numpy as np
        N_NODES = 12500

        def _add_self_loops(edge_index, n):
            loop = jnp.arange(n, dtype=edge_index.dtype)
            src = jnp.concatenate([edge_index[0], loop])
            dst = jnp.concatenate([edge_index[1], loop])
            return (src, dst)

        def _gcn_conv(x, src, dst, n, W, b):
            h = x @ W
            deg = jnp.zeros((n,), h.dtype).at[dst].add(1.0)
            dinv = jnp.where(deg > 0, jax.lax.rsqrt(deg), 0.0)
            norm = dinv[src] * dinv[dst]
            msg = h[src] * norm[:, None]
            out = jax.ops.segment_sum(msg, dst, num_segments=n)
            return out + b
        n = x.shape[0]
        src, dst = _add_self_loops(edge_index, n)
        h = _gcn_conv(x, src, dst, n, W1, b1)
        h = jax.nn.relu(h)
        h = _gcn_conv(h, src, dst, n, W2, b2)
        return h @ Wl + bl

    def _L3_gnn_ref(x, edge_index, edge_atten, W1, b1, gamma, beta, W2, b2):
        import jax, jax.numpy as jnp
        import numpy as np
        N_NODES = 12500
        N_EDGES = 200000
        HID = 64
        N_LAYERS = 3
        BN_EPS = 1e-05
        src = edge_index[0]
        dst = edge_index[1]
        n = x.shape[0]
        for i in range(N_LAYERS):
            msg = x[src] * edge_atten
            agg = jax.ops.segment_sum(msg, dst, num_segments=n)
            h = agg + x
            h = h @ W1[i] + b1[i]
            mu = jnp.mean(h, axis=0)
            var = jnp.var(h, axis=0)
            h = (h - mu) * jax.lax.rsqrt(var + BN_EPS) * gamma[i] + beta[i]
            h = jax.nn.relu(h)
            h = h @ W2[i] + b2[i]
            x = jax.nn.relu(h)
        return x
    edge_index = jnp.stack([src, dst])
    x = _layernorm(x + _L0_gnn_ref(x, edge_index, L0_gnn_W1, L0_gnn_b1, L0_gnn_W2, L0_gnn_b2, L0_gnn_W3, L0_gnn_b3, L0_gnn_W4, L0_gnn_b4), axis=-1)
    x = _layernorm(x + _L1_gnn_ref(x, edge_index, edge_weight, L1_gnn_W1, L1_gnn_b1, L1_gnn_Wt, L1_gnn_bt, L1_gnn_W2, L1_gnn_b2), axis=-1)
    x = _layernorm(x + _L2_gnn_ref(x, edge_index, L2_gnn_W1, L2_gnn_b1, L2_gnn_W2, L2_gnn_b2, L2_gnn_Wl, L2_gnn_bl), axis=-1)
    x = _layernorm(x + _L3_gnn_ref(x, edge_index, edge_weight1, L3_gnn_W1, L3_gnn_b1, L3_gnn_gamma, L3_gnn_beta, L3_gnn_W2, L3_gnn_b2), axis=-1)
    return x

_drawn_inputs = setup_inputs


def setup_inputs(seed=0):
    import zlib

    import numpy as np

    out = dict(_drawn_inputs(seed))
    spreads = {'L0_gnn_b1': (0.0, 0.1),
     'L0_gnn_b2': (0.0, 0.435),
     'L0_gnn_b3': (0.0, 0.1),
     'L0_gnn_b4': (0.0, 0.1),
     'L1_gnn_b1': (0.0, 0.1),
     'L1_gnn_bt': (0.0, 0.1),
     'L1_gnn_b2': (0.0, 0.1),
     'L2_gnn_b1': (0.0, 0.1),
     'L2_gnn_b2': (0.0, 0.1),
     'L2_gnn_bl': (0.0, 0.1),
     'L3_gnn_gamma': (1.0, 0.2),
     'L3_gnn_beta': (0.0, 0.1)}
    factors = {'L0_gnn_W1': 3.525, 'L3_gnn_b1': 8.0}
    for name, (base, spread) in spreads.items():
        noise = np.random.default_rng([zlib.crc32(name.encode()), seed]).standard_normal(out[name].shape)
        drawn = base * np.exp(spread * noise) if base else spread * noise
        out[name] = jnp.asarray(drawn.astype(out[name].dtype))
    for name, factor in factors.items():
        out[name] = (out[name] * factor).astype(out[name].dtype)
    return out
```

```python
from contextlib import ExitStack

import concourse.bass as bass
from concourse import mybir

ALU = mybir.AluOpType
ACT = mybir.ActivationFunctionType
AX = mybir.AxisListType
F32 = mybir.dt.float32
BF16 = mybir.dt.bfloat16
I32 = mybir.dt.int32
U32 = mybir.dt.uint32

P = 128
N = 12500
E = 200000
F = 64
H = 128
J = -(-N // P)
NPAD = J * P
U = 16
T = -(-E // (P * 2 * U)) * 2 * U
G = T // U
EPAD = T * P
PAD_NODE = NPAD - 1
C = 7
NC = J // C
ZERO_ROW = P * T
BN_PARTS = 25
BN_LEN = N // BN_PARTS
LN_EPS = 1e-5
BN_EPS = 1e-5
assert BN_PARTS * BN_LEN == N and BN_LEN <= 512
assert NC * C == J and NC % 2 == 0 and G % 2 == 0 and PAD_NODE >= N


class Tally:

    def __init__(self, sem):
        self.sem, self.base, self.n = sem, 0, 0

    def up(self, ins, by=1):
        ins.then_inc(self.sem, by)
        self.n += by
        return ins

    def value(self):
        return self.base + self.n

    def enter(self, i, per_turn):
        self.start, self.per_turn = self.base + self.n, per_turn
        self.base, self.n = self.start + i * per_turn, 0

    def leave(self, turns):
        assert self.n == self.per_turn, (self.n, self.per_turn)
        self.base, self.n = self.start + turns * self.per_turn, 0


def gnn_program(nc, x_nodes, src_cols, dst_cols, weight_cols, dst_rows, tile_first, tile_last, time_row, src_row,
                weights, out, layers=4):
    PHASES = {1: 4, 2: 4, 3: 6, 4: 9}[layers]
    TURNS = G // 2
    CTURNS = NC // 2
    U1, TURNS1 = U // 2, G
    CW = C * P // 2
    LN_AFTER = [3, 5, 8]
    NORM = {3: 1, 5: 3, 8: 4}
    KIND = ["wide", "narrow", "wide_skip", "residual", "conv", "conv_out", "gin", "gin", "gin"]

    with ExitStack() as ctx:
        def sb(name, shape, dt=F32):
            return ctx.enter_context(nc.sbuf_tensor(name, shape, dt))[:]

        def psum(name, shape):
            return ctx.enter_context(nc.psum_tensor(name, shape, F32))[:]

        def sem(name):
            return ctx.enter_context(nc.semaphore(name))

        table = nc.dram_tensor("table", (NPAD, F), F32).ap()
        partial = nc.dram_tensor("partial", (P * T + P, F), F32).ap()
        table_v = table.rearrange("(p j) f -> p (j f)", p=P)
        partial_v = partial[0:P * T, :].rearrange("(p t) f -> p (t f)", p=P)

        table_s = nc.dram_tensor("table_s", (NPAD, H), F32).ap()
        table_t = nc.dram_tensor("table_t", (NPAD, H), F32).ap()
        partial1 = nc.dram_tensor("partial1", (P * T + P, H), F32).ap()
        partial1_v = partial1[0:P * T, :].rearrange("(p t) f -> p (t f)", p=P)
        by_src = [nc.dram_tensor("by_src%d" % u, (NPAD, H), F32).ap() for u in range(U1)]
        by_src_v = [a.rearrange("(p j) f -> p (j f)", p=P) for a in by_src]

        ps_main = psum("ps_main", [P, 4, 512])
        ps_out = psum("ps_out", [P, 2, 512])
        ps_last = psum("ps_last", [P, 2, 512])

        x_cur = sb("x_cur", [P, J * F])
        own = sb("own", [P, J * F])
        big = sb("big", [P, NPAD])
        rank = sb("rank", [P, T])
        edge_w = sb("edge_w", [P, T])
        src_idx = sb("src_idx", [P, T], U32)
        chained = sb("chained", [P, T])
        cont = sb("cont", [P, T])
        tile_sum = sb("tile_sum", [P, T])
        run_sum = sb("run_sum", [P, T])
        rows = sb("rows", [P, 2, U * F])
        pick = sb("pick", [P, 2, U, P])
        stage = sb("stage", [P, 2, U * F])
        idx = sb("idx", [P, 2, U], U32)
        rank_g = sb("rank_g", [P, 2, U])
        w_g = sb("w_g", [P, 2, U])
        node_idx = sb("node_idx", [P, J + 2 * C], U32)
        nidx = sb("nidx", [P, 2, C], U32)
        agg = sb("agg", [P, 2, C * F])
        z = sb("z", [P, 2, C * F])
        tmp = sb("tmp", [P, C * F])
        zT = sb("zT", [F, C * P])
        hT = sb("hT", [P, C * P])
        carry_rows = pick[:, 0].rearrange("p u c -> p (u c)")[:, 0:U * F]
        zeros = hT
        carry_idx = sb("carry_idx", [P, U], U32)
        deg_dst = sb("deg_dst", [P, J])
        deg_src = sb("deg_src", [P, J])
        dinv = sb("dinv", [P, J])
        iota_f = sb("iota_f", [P, P])
        iota_h = sb("iota_h", [P, P], BF16)
        iota_i = sb("iota_i", [P, P], I32)
        part_i = sb("part_i", [P, 1], I32)
        part_f = sb("part_f", [P, 1])
        ident = sb("ident", [P, P])
        tri = sb("tri", [P, P])
        ones = sb("ones", [P, P])
        hot_zero = sb("hot_zero", [P, 2 * J], BF16)
        low = sb("low", [P, P])
        src_c = sb("src_c", [P, 2, U1], I32)
        earlier = sb("earlier", [P, 2, U1])
        add_idx = sb("add_idx", [P, 2, U1], U32)
        stats = sb("stats", [F, BN_PARTS * 6])
        bn = sb("bn", [F, 8])
        small = sb("small", [P, 8, J])
        tid_i = sb("tid_i", [P, U], I32)
        next_first = sb("next_first", [P, U], I32)

        W1G = U1 * H
        rows_s = rows
        rows_t = big[:, 0:2 * W1G].rearrange("p (h c) -> p h c", h=2)
        pick1, same = pick[:, :, 0:U1], pick[:, :, U1:2 * U1]
        hid = big[:, 2 * W1G:4 * W1G].rearrange("p (h c) -> p h c", h=2)
        merged = big[:, 4 * W1G:6 * W1G].rearrange("p (h c) -> p h c", h=2)
        src_b = big[:, 6 * W1G:8 * W1G].bitcast(I32).rearrange("p (h c) -> p h c", h=2)
        t_emb = big[:, 8 * W1G:9 * W1G]
        arg = big[:, 9 * W1G:10 * W1G]
        scratch = big[:, 6 * W1G:8 * W1G].rearrange("p (h c) -> p h c", h=2)
        times = big[0:2, 10 * W1G:12 * W1G].rearrange("p (h c) -> p h c", h=2)
        carry_rows1 = big[:, 0:U * H]
        parts_s = big[:, 2 * W1G:2 * W1G + U1 * C * H].rearrange("p (k c) -> p k c", k=U1)
        agg1 = big[:, 9 * W1G:9 * W1G + 2 * C * H].rearrange("p (h c) -> p h c", h=2)
        dT = big[:, 11 * W1G:11 * W1G + C * P]
        new_s = big[:, 0:C * H]
        new_t = big[:, C * H:2 * C * H]
        dst_idx = edge_w[:].bitcast(U32)

        keys = big[:, 0:5 * T].rearrange("p (g q u) -> p g q u", q=5, u=U)
        hot_w = big[:, 5 * T:7 * T].bitcast(BF16).rearrange("p (h u c) -> p h u c", h=2, u=U)
        hot_s = big[:, 7 * T:8 * T].bitcast(BF16).rearrange("p (h u c) -> p h u c", h=2, u=U)
        hot_lo = pick[:].rearrange("p h u c -> p (h u c)").bitcast(BF16).rearrange("p (k h u c) -> p k h u c", k=2, h=2, u=U)
        row_dst = own[0:G, 0:U * P].bitcast(I32)
        row_chg = own[0:G, U * P:2 * U * P]
        row_pre = own[0:G, 2 * U * P:3 * U * P]
        row_rank = pick[0:G, 0].rearrange("p u c -> p (u c)")
        row_val = pick[0:G, 1].rearrange("p u c -> p (u c)")
        col_i = rows[:].rearrange("p h c -> p (h c)").bitcast(I32)[:, 0:T]
        dst_i = run_sum[:].bitcast(I32)
        src_i = tile_sum[:].bitcast(I32)
        first_b = chained
        last_b = stage[:].rearrange("p h c -> p (h c)")[:, 0:T]

        W = {}
        for name, (ap, shape, kind) in weights.items():
            W[name] = (sb("w_" + name, shape), ap, kind)

        inputs_in = sem("inputs_in")
        zero_in = sem("zero_in")
        zero_made = sem("zero_made")
        consts = sem("consts")
        v_step = Tally(sem("v_step"))
        a_step = Tally(sem("a_step"))
        ranks_out = sem("ranks_out")
        ranks_in = sem("ranks_in")
        keys_ready = sem("keys_ready")
        hot_ready = sem("hot_ready")
        hot_used = sem("hot_used")
        counted = sem("counted")
        deg_ready = sem("deg_ready")
        cum_ready = sem("cum_ready")
        root_ready = sem("root_ready")
        root_in = sem("root_in")
        own_ready = sem("own_ready")
        table_out = sem("table_out")
        idx_ready = sem("idx_ready")
        pool_go = sem("pool_go")
        rows_in = [[sem("rows_in%d_%d" % (s, h)) for h in range(2)] for s in range(-(-PHASES // 3))]
        pick_ready = sem("pick_ready")
        group_done = sem("group_done")
        sums_out = sem("sums_out")
        stored = [sem("stored0"), sem("stored1")]
        stage_free = sem("stage_free")
        carry_ready = sem("carry_ready")
        carry_turned = sem("carry_turned")
        carry_in = sem("carry_in")
        carry_added = sem("carry_added")
        nidx_ready = sem("nidx_ready")
        agg_in = [sem("agg_in0"), sem("agg_in1")]
        z_ready = sem("z_ready")
        z_turned = sem("z_turned")
        zT_ready = sem("zT_ready")
        h_done = sem("h_done")
        hT_ready = sem("hT_ready")
        bn_var, bn_root, bn_ready, o_taken = sem("bn_var"), sem("bn_root"), sem("bn_ready"), sem("o_taken")
        v_go, pe_go, act_go = sem("v_go"), sem("pe_go"), sem("act_go")
        o_done = sem("o_done")
        skip_ready = sem("skip_ready")
        stats_ready = sem("stats_ready")
        ln_var = sem("ln_var")
        ln_root = sem("ln_root")
        result_ready = sem("result_ready")
        result_out = sem("result_out")
        zeroed = sem("zeroed")
        x_ready, x_turned, xT_ready = sem("x_ready"), sem("x_turned"), sem("xT_ready")
        st_done, st_ready, st_out = sem("st_done"), sem("st_ready"), sem("st_out")
        edge_in = [sem("edge_in0"), sem("edge_in1")]
        idx1_ready, pick1_ready, add_idx_ready = sem("idx1_ready"), sem("pick1_ready"), sem("add_idx_ready")
        rows1_in = [sem("rows1_in0"), sem("rows1_in1")]
        t_done, t_ready, arg_ready, hid_ready = sem("t_done"), sem("t_ready"), sem("arg_ready"), sem("hid_ready")
        group1_done, sums1_out, stage1_free = sem("group1_done"), sem("sums1_out"), sem("stage1_free")
        stored1 = [sem("stored1_0"), sem("stored1_1")]
        added, added_free = sem("added"), sem("added_free")
        carry1_ready, carry1_turned, carry1_in, carry1_added = sem("carry1_ready"), sem("carry1_turned"), sem("carry1_in"), sem("carry1_added")
        nidx1_ready, parts_in, parts_free = sem("nidx1_ready"), sem("parts_in"), sem("parts_free")
        agg1_in = [sem("agg1_in0"), sem("agg1_in1")]
        sd_turned, sd_ready, o1_done, o1_taken = sem("sd_turned"), sem("sd_ready"), sem("o1_done"), sem("o1_taken")
        tmp_sum = sem("tmp_sum")
        weights_in = sem("weights_in")
        block = ctx.enter_context(nc.Block())

        def dyn(t, j0, width, per=1):
            return t[:, bass.ds(j0 * per, width * per)]

        MATS = {0: (W["W1"][0], W["b1"][0], W["W2"][0]), 2: (W["W3"][0], W["b3"][0], W["W4"][0])}
        if PHASES > 4:
            MATS[4] = (W["cW1"][0], W["cb1"][0], ident[0:F, 0:F])
            MATS[5] = (W["cW2"][0], W["cb2"][0], W["cWl"][0])
        for l in range(PHASES - 6):
            MATS[6 + l] = (W["gW1"][0][:, l], W["gb1"][0][:, l:l + 1], W["gW2"][0][:, l])
        TURNED = sorted(MATS)
        HT_EXTRA = {k: NC * max(0, k - 6) for k in TURNED}
        O_EXTRA = {k: 0 for k in TURNED}

        LOADS = []
        LOADS += [(x_cur[:], x_nodes), (dst_i, dst_cols), (src_i, src_cols),
                  (row_dst, dst_rows), (first_b[:].bitcast(I32), tile_first[0:T].partition_broadcast(P)),
                  (last_b.bitcast(I32), tile_last.partition_broadcast(P)),
                  (next_first[0:G, :], tile_first[1:T + 1].rearrange("(g u) -> g u", u=U))]
        for name, (t, ap, kind) in W.items():
            if kind == "rows":
                LOADS += [(t[r:r + 1, :], a) for r, a in enumerate(ap)]
            else:
                LOADS.append((t[:], ap.partition_broadcast(P) if kind == "row" else ap))

        @block.sync
        def _(sp):
            for dst, source in LOADS:
                sp.dma_start(dst, source).then_inc(inputs_in, 16)
            sp.wait_ge(zero_made, 1)
            sp.dma_start(partial[P * T:P * T + P, :], zeros[:, 0:F]).then_inc(zero_in, 16)
            sp.dma_start(partial1[P * T:P * T + P, :], zeros[:, 0:H]).then_inc(zero_in, 16)

            sp.sem_inc(stage_free, 2)

            def store_table(k):
                with sp.Fori(0, NC) as c:
                    sp.wait_ge(own_ready, c + NC * k + 1)
                    sp.dma_start(table_v[:, bass.ds(c * (C * F), C * F)], own[:, bass.ds(c * (C * F), C * F)]).then_inc(table_out, 16)

            def layer1():
                with sp.Fori(0, NC) as c:
                    at = bass.ds(c * (C * H), C * H)
                    sp.wait_ge(st_ready, c + 1)
                    sp.dma_start(table_s.rearrange("(p j) f -> p (j f)", p=P)[:, at], new_s).then_inc(st_out, 16)
                    sp.dma_start(table_t.rearrange("(p j) f -> p (j f)", p=P)[:, at], new_t).then_inc(st_out, 16)
                sp.wait_ge(st_out, 32 * NC)
                sp.sem_inc(stage1_free, 2)
                with sp.Fori(0, TURNS1) as i:
                    for h in range(2):
                        m = i * 2 + h
                        edges = bass.ds(m * (U1 * P), U1 * P)
                        sp.wait_ge(group1_done, m + 1)
                        sp.dma_start(times[0:1, h, :], time_row[:, edges]).then_inc(edge_in[h], 16)
                        sp.dma_start(src_b[:, h, :], src_row[0, edges].partition_broadcast(P)).then_inc(edge_in[h], 16)
                        sp.dma_start(src_c[:, h, :], src_cols[:, bass.ds(m * U1, U1)]).then_inc(edge_in[h], 16)
                    for h in range(2):
                        m = i * 2 + h
                        sp.wait_ge(sums1_out, m + 3)
                        sp.dma_start(partial1_v[:, bass.ds(m * W1G, W1G)], stage[:, h, :]).then_inc(stored1[h], 16)
                    for h in range(2):
                        sp.wait_ge(stored1[h], i * 16 + 16)
                        sp.sem_inc(stage1_free, 1)
                sp.wait_ge(added, 16 * U1 * 2 * TURNS1)
                with sp.Fori(0, NC) as c:
                    at = bass.ds(c * (C * H), C * H)
                    sp.wait_ge(parts_free, c + 1)
                    for u in range(U1):
                        sp.dma_start(parts_s[:, u, :], by_src_v[u][:, at]).then_inc(parts_in, 16)

            with sp.Fori(0, NC) as c:
                for u in range(U1):
                    sp.dma_start(by_src_v[u][:, bass.ds(c * (C * H), C * H)], zeros[:, 0:C * H]).then_inc(zeroed, 16)

            for k in range(PHASES):
                if k == 4:
                    layer1()
                if k == 6:
                    sp.wait_ge(own_ready, NC * 6 + 1)
                    sp.dma_start(edge_w[:], weight_cols).then_inc(weights_in, 16)
                store_table(k)
                with sp.Fori(0, TURNS) as i:
                    n = i + TURNS * k
                    for h in range(2):
                        sp.wait_ge(sums_out, n * 2 + h + 3)
                        sp.dma_start(partial_v[:, bass.ds((i * 2 + h) * (U * F), U * F)], stage[:, h, :]).then_inc(stored[h], 16)
                    for h in range(2):
                        sp.wait_ge(stored[h], n * 16 + 16)
                        sp.sem_inc(stage_free, 1)
            if layers == 2:
                layer1()
            sp.wait_ge(result_ready, 1)
            sp.dma_start(out, x_cur[:]).then_inc(result_out, 16)
            sp.wait_ge(result_out, 16)
            sp.wait_ge(inputs_in, 16 * len(LOADS))
            sp.wait_ge(zero_in, 32)
            sp.wait_ge(zeroed, 16 * NC * U1)
            sp.wait_ge(table_out, 16 * NC * PHASES)
            for h in range(2):
                sp.wait_ge(stored[h], 16 * TURNS * PHASES)

        @block.gpsimd
        def _(pool):
            nc.gpsimd.iota(iota_i[:], pattern=[[1, P]], base=0, channel_multiplier=0).then_inc(consts, 1)
            nc.gpsimd.iota(part_i[:], pattern=[[0, 1]], base=0, channel_multiplier=1).then_inc(consts, 1)
            nc.gpsimd.iota(tid_i[:], pattern=[[1, U]], base=0, channel_multiplier=U).then_inc(consts, 1)

            def gather_edges(k):
                pool.wait_ge(table_out, 16 * NC * (k + 1))
                with pool.Fori(0, TURNS) as i:
                    for h in range(2):
                        pool.wait_ge(idx_ready, (i + TURNS * k) * 2 + h + 1)
                        pool.sem_inc(pool_go, 1)
                        for u in range(U):
                            pool.indirect_dma_start(
                                out=rows[:, h, u * F:(u + 1) * F], out_offset=None, in_=table,
                                in_offset=bass.IndirectOffsetOnAxis(ap=idx[:, h, u:u + 1], axis=0),
                            ).then_inc(rows_in[k // 3][h], 16)

            def add_carries(k):
                for h in range(2):
                    pool.wait_ge(stored[h], 16 * TURNS * (k + 1))
                pool.wait_ge(zero_in, 32)
                pool.wait_ge(zeroed, 16 * NC * U1)
                pool.wait_ge(carry_in, k + 1)
                for u in range(U):
                    pool.indirect_dma_start(
                        out=partial, out_offset=bass.IndirectOffsetOnAxis(ap=carry_idx[0:G, u:u + 1], axis=0),
                        in_=carry_rows[0:G, u * F:(u + 1) * F], in_offset=None, compute_op=ALU.add,
                    ).then_inc(carry_added, 16)
                pool.wait_ge(carry_added, 16 * U * (k + 1))

            def gather_nodes(k):
                with pool.Fori(0, CTURNS) as i:
                    for h in range(2):
                        pool.wait_ge(nidx_ready, (i + (CTURNS + 1) * k) * 2 + h + 1)
                        pool.sem_inc(pool_go, 1)
                        for c in range(C):
                            pool.indirect_dma_start(
                                out=agg[:, h, c * F:(c + 1) * F], out_offset=None, in_=partial,
                                in_offset=bass.IndirectOffsetOnAxis(ap=nidx[:, h, c:c + 1], axis=0),
                            ).then_inc(agg_in[h], 16)

            def layer1():
                def gather(m, h):
                    pool.wait_ge(idx1_ready, m + 1)
                    pool.sem_inc(pool_go, 1)
                    for source, target, first in ((table_s, rows_s, 0), (table_t, rows_t, U1)):
                        for u in range(U1):
                            pool.indirect_dma_start(
                                out=target[:, h, u * H:(u + 1) * H], out_offset=None, in_=source,
                                in_offset=bass.IndirectOffsetOnAxis(ap=idx[:, h, first + u:first + u + 1], axis=0),
                            ).then_inc(rows1_in[h], 16)

                def add(m, h, begun=True):
                    pool.wait_ge(sums1_out, m + 3)
                    pool.wait_ge(add_idx_ready, m + 1)
                    if begun:
                        pool.wait_ge(added, m * (16 * U1))
                        pool.sem_inc(added_free, 1)
                    for u in range(U1):
                        pool.indirect_dma_start(
                            out=by_src[u], out_offset=bass.IndirectOffsetOnAxis(ap=add_idx[:, h, u:u + 1], axis=0),
                            in_=merged[:, h, u * H:(u + 1) * H], in_offset=None, compute_op=ALU.add,
                            bounds_check=NPAD - 1, oob_is_err=False,
                        ).then_inc(added, 16)

                pool.wait_ge(st_out, 32 * NC)
                pool.sem_inc(added_free, 2)
                last = 2 * TURNS1 - 1
                gather(0, 0)
                gather(1, 1)
                add(0, 0, begun=False)
                with pool.Fori(0, TURNS1 - 1) as i:
                    gather(i * 2 + 2, 0)
                    add(i * 2 + 1, 1)
                    gather(i * 2 + 3, 1)
                    add(i * 2 + 2, 0)
                add(last, 1)
                for h in range(2):
                    pool.wait_ge(stored1[h], 16 * TURNS1)
                pool.wait_ge(carry1_in, 1)
                for u in range(U):
                    pool.indirect_dma_start(
                        out=partial1, out_offset=bass.IndirectOffsetOnAxis(ap=carry_idx[0:G, u:u + 1], axis=0),
                        in_=carry_rows1[0:G, u * H:(u + 1) * H], in_offset=None, compute_op=ALU.add,
                    ).then_inc(carry1_added, 16)
                pool.wait_ge(carry1_added, 16 * U)
                with pool.Fori(0, CTURNS) as i:
                    for h in range(2):
                        pool.wait_ge(nidx1_ready, i * 2 + h + 1)
                        pool.sem_inc(pool_go, 1)
                        for c in range(C):
                            pool.indirect_dma_start(
                                out=agg1[:, h, c * H:(c + 1) * H], out_offset=None, in_=partial1,
                                in_offset=bass.IndirectOffsetOnAxis(ap=nidx[:, h, c:c + 1], axis=0),
                            ).then_inc(agg1_in[h], 16)

            for k in range(PHASES):
                gather_edges(k)
                add_carries(k)
                gather_nodes(k)
                if k == 3 and layers > 1:
                    layer1()

        @block.tensor
        def _(pe):
            def turn_rows(source, ready, n):
                pe.wait_ge(ready, n)
                for u in range(U):
                    ins = pe.transpose(ps_main[:, u // 4, (u % 4) * P:(u % 4) * P + G],
                                       source[:, u * P:(u + 1) * P], ident[0:G, 0:G])
                ins.then_inc(ranks_out, 1)

            turn_rows(row_rank, keys_ready, 1)
            pe.wait_ge(ranks_in, 4)
            turn_rows(row_val, keys_ready, 1)

            pe.wait_ge(hot_ready, 1)
            zero_lo, zero_hi = hot_zero[:, 0:P], hot_zero[:, 0:2 * J]
            pe.matmul(ps_out[:, 0, 0:2 * J], zero_lo, zero_hi, start=True, stop=False, skip_group_check=True)
            pe.matmul(ps_out[:, 1, 0:J], zero_lo, zero_hi[:, 0:J], start=True, stop=False, skip_group_check=True)
            pe.sem_inc(hot_used, 2)
            with pe.Fori(0, TURNS) as i:
                for h in range(2):
                    pe.wait_ge(hot_ready, i * 2 + h + 2)
                    for u in range(U):
                        pe.matmul(ps_out[:, 0, 0:2 * J], hot_lo[:, 0, h, u], hot_w[:, h, u],
                                  start=False, stop=False, skip_group_check=True)
                        ins = pe.matmul(ps_out[:, 1, 0:J], hot_lo[:, 1, h, u], hot_s[:, h, u],
                                        start=False, stop=False, skip_group_check=True)
                    ins.then_inc(hot_used, 1)
            pe.matmul(ps_out[:, 0, 0:2 * J], zero_lo, zero_hi, start=False, stop=True, skip_group_check=True)
            pe.matmul(ps_out[:, 1, 0:J], zero_lo, zero_hi[:, 0:J], start=False, stop=True,
                      skip_group_check=True).then_inc(counted, 1)

            pe.wait_ge(deg_ready, 1)
            pe.matmul(ps_last[:, 1, 0:J], tri[:], deg_dst[:], start=True, stop=True)
            pe.matmul(ps_last[:, 1, P:P + J], ones[:], deg_dst[:], start=True, stop=True).then_inc(cum_ready, 1)

            pe.sem_inc(group_done, 2)

            def sum_runs(k):
                with pe.Fori(0, TURNS) as i:
                    for h in range(2):
                        n = i + TURNS * k
                        pe.wait_ge(rows_in[k // 3][h], (i + TURNS * (k % 3)) * (16 * U) + 16 * U)
                        pe.wait_ge(pick_ready, n * 2 + h + 1)
                        pe.wait_ge(sums_out, n * 2 + h + 1)
                        for u in range(U):
                            got = rows[:, h, u * F:(u + 1) * F]
                            pe.matmul(ps_main[:, h * 2 + u // 8, (u % 8) * F:(u % 8 + 1) * F], pick[:, h, u], got,
                                      start=True, stop=True)
                            ins = pe.matmul(ps_last[0:F, h, u:u + 1], got, pick[:, h, u, 0:1],
                                            start=True, stop=True)
                        ins.then_inc(group_done, 1)

            def turn_carries(k):
                pe.wait_ge(carry_ready, k + 1)
                for u in range(U):
                    ins = pe.transpose(ps_main[0:G, u // 8, (u % 8) * F:(u % 8 + 1) * F],
                                       tile_sum[0:F, u:T:U], ident[0:F, 0:F])
                ins.then_inc(carry_turned, 1)

            def transform_nodes(k):
                first, _, second = MATS[k]
                wide = first.shape[1]
                gin = KIND[k] == "gin"
                with pe.Fori(0, CTURNS) as i:
                    for h in range(2):
                        m = (i + CTURNS * TURNED.index(k)) * 2 + h + 1
                        pe.wait_ge(z_ready, m)
                        pe.sem_inc(pe_go, 1)
                        for c in range(C):
                            ins = pe.transpose(ps_main[0:F, c // 4, (c % 4) * P:(c % 4 + 1) * P],
                                               z[:, h, c * F:(c + 1) * F], ident[:])
                        ins.then_inc(z_turned, 1)
                        pe.wait_ge(zT_ready, m)
                        pe.sem_inc(pe_go, 1)
                        for b in range(2):
                            ins = pe.matmul(ps_main[0:wide, 2 + b, 0:CW], first, zT[:, b * CW:(b + 1) * CW],
                                            start=True, stop=True)
                        ins.then_inc(h_done, 1)
                        if gin:
                            pe.wait_ge(hT_ready, m + HT_EXTRA[k])
                            pe.sem_inc(pe_go, 1)
                            continue
                        if KIND[k] == "wide_skip":
                            pe.wait_ge(skip_ready, i * 2 + h + 1)
                            pe.sem_inc(pe_go, 1)
                        else:
                            pe.wait_ge(hT_ready, m + HT_EXTRA[k])
                            pe.sem_inc(pe_go, 1)
                        for c in range(C):
                            ins = pe.matmul(ps_out[:, 0, c * F:(c + 1) * F], hT[0:wide, c * P:(c + 1) * P], second,
                                            start=True, stop=True)
                        ins.then_inc(o_done, 1)
                if gin:
                    with pe.Fori(0, NC) as c:
                        pe.wait_ge(hT_ready, c + (NC * (TURNED.index(k) + 1) + HT_EXTRA[k] + 1))
                        pe.wait_ge(o_taken, c + (NC * (k - 6) + 1))
                        pe.sem_inc(pe_go, 1)
                        for t in range(C):
                            ins = pe.matmul(ps_out[:, 0, t * F:(t + 1) * F], hT[0:F, t * P:(t + 1) * P], second,
                                            start=True, stop=True)
                        ins.then_inc(o_done, 1)

            def layer1():
                with pe.Fori(0, CTURNS) as i:
                    for h in range(2):
                        m = i * 2 + h + 1
                        pe.wait_ge(x_ready, m)
                        pe.sem_inc(pe_go, 1)
                        for c in range(C):
                            ins = pe.transpose(ps_out[0:F, c // 4, (c % 4) * P:(c % 4 + 1) * P],
                                               z[:, h, c * F:(c + 1) * F], ident[:])
                        ins.then_inc(x_turned, 1)
                        pe.wait_ge(xT_ready, m)
                        pe.sem_inc(pe_go, 1)
                        for c in range(C):
                            ins = pe.matmul(ps_main[:, c // 2, (c % 2) * 2 * H:(c % 2 + 1) * 2 * H],
                                            zT[:, c * P:(c + 1) * P], W["eW1"][0].rearrange("k s m -> k (s m)"), start=True, stop=True)
                        ins.then_inc(st_done, 1)
                pe.wait_ge(st_ready, NC)
                pe.sem_inc(group1_done, 2)
                with pe.Fori(0, TURNS1) as i:
                    for h in range(2):
                        m = i * 2 + h
                        pe.wait_ge(edge_in[h], i * 48 + 48)
                        pe.wait_ge(t_ready, m + 1)
                        pe.sem_inc(pe_go, 1)
                        for u in range(U1):
                            ins = pe.matmul(ps_out[:, u // 4, (u % 4) * H:(u % 4 + 1) * H], times[:, h, u * P:(u + 1) * P],
                                            W["eWt"][0], start=True, stop=True)
                        ins.then_inc(t_done, 1)
                        pe.wait_ge(hid_ready, m + 1)
                        pe.wait_ge(pick1_ready, m + 1)
                        pe.wait_ge(sums1_out, m + 2)
                        pe.sem_inc(pe_go, 1)
                        for u in range(U1):
                            got = hid[:, h, u * H:(u + 1) * H]
                            at = slice((u % 4) * H, (u % 4 + 1) * H)
                            pe.matmul(ps_main[:, u // 4, at], pick1[:, h, u], got, start=True, stop=True)
                            pe.matmul(ps_main[:, 2 + u // 4, at], same[:, h, u], got, start=True, stop=True)
                            ins = pe.matmul(ps_last[:, h, u:u + 1], got, pick1[:, h, u, 0:1], start=True, stop=True)
                        ins.then_inc(group1_done, 1)
                pe.wait_ge(carry1_ready, 1)
                for u in range(U):
                    ins = pe.transpose(ps_main[0:G, u // 4, (u % 4) * P:(u % 4 + 1) * P], tile_sum[:, u:T:U], ident[:])
                ins.then_inc(carry1_turned, 1)
                pe.wait_ge(carry1_in, 1)
                with pe.Fori(0, CTURNS) as i:
                    for h in range(2):
                        m = i * 2 + h + 1
                        pe.wait_ge(parts_in, m * (16 * U1))
                        pe.wait_ge(agg1_in[h], i * (16 * C) + 16 * C)
                        pe.sem_inc(pe_go, 1)
                        for c in range(C):
                            at = slice((c % 4) * P, (c % 4 + 1) * P)
                            for u in range(U1):
                                pe.matmul(ps_main[:, c // 4, at], parts_s[:, u, c * H:(c + 1) * H], ident[:],
                                          start=(u == 0), stop=(u == U1 - 1))
                            ins = pe.transpose(ps_main[:, 2 + c // 4, at], agg1[:, h, c * H:(c + 1) * H], ident[:])
                        ins.then_inc(sd_turned, 1)
                        pe.wait_ge(sd_ready, m)
                        pe.wait_ge(o1_taken, m)
                        pe.sem_inc(pe_go, 1)
                        for c in range(C):
                            at = slice(c * F, (c + 1) * F)
                            pe.matmul(ps_out[:, 0, at], hT[:, c * P:(c + 1) * P], W["eW2"][0][:, 0:F], start=True, stop=False)
                            ins = pe.matmul(ps_out[:, 0, at], dT[:, c * P:(c + 1) * P], W["eW2"][0][:, F:2 * F],
                                            start=False, stop=True)
                        ins.then_inc(o1_done, 1)

            for k in range(PHASES):
                sum_runs(k)
                turn_carries(k)
                if k in MATS:
                    transform_nodes(k)
                if k == 3 and layers > 1:
                    layer1()

        @block.scalar
        def _(act):
            def take_rows(target, n):
                act.wait_ge(ranks_out, n)
                for b in range(4):
                    ins = nc.scalar.copy(target(b), ps_main[:, b].rearrange("p (u g) -> p u g", u=4)[:, :, 0:G])
                ins.then_inc(ranks_in, 4)

            take_rows(lambda b: rank[:].rearrange("p (g u) -> p u g", u=U)[:, 4 * b:4 * b + 4], 1)
            take_rows(lambda b: keys[:, :, 2].rearrange("p g u -> p u g")[:, 4 * b:4 * b + 4], 2)

            act.wait_ge(root_ready, 1)
            nc.scalar.activation(dinv[:], small[:, 0], ACT.Sqrt).then_inc(root_in, 1)
            act.sem_inc(sums_out, 2)

            def take_sums(k):
                with act.Fori(0, TURNS) as i:
                    for h in range(2):
                        m = (i + TURNS * k) * 2 + h
                        act.wait_ge(group_done, m + 3)
                        act.wait_ge(stage_free, m + 1)
                        act.sem_inc(act_go, 1)
                        for b in range(2):
                            nc.scalar.copy(stage[:, h, b * 512:(b + 1) * 512], ps_main[:, h * 2 + b])
                        nc.scalar.copy(tile_sum[0:F, bass.ds((i * 2 + h) * U, U)],
                                       ps_last[0:F, h, 0:U]).then_inc(sums_out, 1)

            def take_carries(k):
                act.wait_ge(carry_turned, k + 1)
                for b in range(2):
                    ins = nc.scalar.copy(carry_rows[0:G, b * 512:(b + 1) * 512], ps_main[0:G, b])
                ins.then_inc(carry_in, 1)

            def bend_nodes(k):
                first, bias, _ = MATS[k]
                wide = first.shape[1]
                kind = KIND[k]
                bend = ACT.Identity if kind in ("conv_out", "gin") else ACT.Relu
                with act.Fori(0, CTURNS) as i:
                    for h in range(2):
                        m = (i + CTURNS * TURNED.index(k)) * 2 + h + 1
                        act.wait_ge(z_turned, m)
                        act.sem_inc(act_go, 1)
                        nc.scalar.copy(zT[:, 0:512], ps_main[0:F, 0])
                        nc.scalar.copy(zT[:, 512:C * P], ps_main[0:F, 1, 0:C * P - 512]).then_inc(zT_ready, 1)
                        act.wait_ge(h_done, m)
                        act.sem_inc(act_go, 1)
                        if kind in ("gin", "wide"):
                            for b in range(2):
                                ins = nc.scalar.activation(big[0:wide, bass.ds((i * 2 + h) * (C * P) + b * CW, CW)],
                                                           ps_main[0:wide, 2 + b, 0:CW], bend, bias=bias)
                        if kind != "gin":
                            for b in range(2):
                                ins = nc.scalar.activation(hT[0:wide, b * CW:(b + 1) * CW],
                                                           ps_main[0:wide, 2 + b, 0:CW], bend, bias=bias)
                        ins.then_inc(hT_ready, 1)
                if kind == "gin":
                    act.wait_ge(bn_var, k - 5)
                    nc.scalar.activation(bn[:, 3:4], bn[:, 2:3], ACT.Sqrt).then_inc(bn_root, 1)
                    act.wait_ge(bn_ready, k - 5)
                    with act.Fori(0, NC) as c:
                        act.wait_ge(o_done, c + NC * TURNED.index(k))
                        act.sem_inc(act_go, 1)
                        nc.scalar.activation(hT[0:F, :], big[0:F, bass.ds(c * (C * P), C * P)], ACT.Relu,
                                             bias=bn[:, 5:6], scale=bn[:, 4:5]).then_inc(hT_ready, 1)

            def root(n):
                act.wait_ge(ln_var, n)
                nc.scalar.activation(small[:, 3], small[:, 2], ACT.Sqrt).then_inc(ln_root, 1)

            def layer1():
                with act.Fori(0, CTURNS) as i:
                    for h in range(2):
                        m = i * 2 + h + 1
                        act.wait_ge(x_turned, m)
                        act.sem_inc(act_go, 1)
                        nc.scalar.copy(zT[:, 0:512], ps_out[0:F, 0])
                        nc.scalar.copy(zT[:, 512:C * P], ps_out[0:F, 1, 0:C * P - 512]).then_inc(xT_ready, 1)
                act.wait_ge(st_ready, NC)
                act.sem_inc(t_ready, 1)
                act.sem_inc(sums1_out, 2)
                with act.Fori(0, TURNS1) as i:
                    for h in range(2):
                        m = i * 2 + h
                        act.wait_ge(t_done, m + 1)
                        act.wait_ge(arg_ready, m + 1)
                        act.sem_inc(act_go, 1)
                        for b in range(2):
                            ins = nc.scalar.activation(t_emb[:, b * 512:(b + 1) * 512], ps_out[:, b], ACT.Silu)
                        ins.then_inc(t_ready, 1)
                        act.wait_ge(arg_ready, m + 2)
                        act.sem_inc(act_go, 1)
                        nc.scalar.activation(hid[:, h], arg, ACT.Silu).then_inc(hid_ready, 1)
                        act.wait_ge(group1_done, m + 3)
                        act.wait_ge(stage1_free, m + 1)
                        act.wait_ge(added_free, m + 1)
                        act.sem_inc(act_go, 1)
                        for b in range(2):
                            nc.scalar.copy(stage[:, h, b * 512:(b + 1) * 512], ps_main[:, b])
                            nc.scalar.copy(merged[:, h, b * 512:(b + 1) * 512], ps_main[:, 2 + b])
                        nc.scalar.copy(tile_sum[:, bass.ds(m * U1, U1)], ps_last[:, h, 0:U1]).then_inc(sums1_out, 1)
                act.wait_ge(carry1_turned, 1)
                for b in range(4):
                    ins = nc.scalar.copy(carry_rows1[0:G, b * 512:(b + 1) * 512], ps_main[0:G, b])
                ins.then_inc(carry1_in, 1)
                act.wait_ge(added, 16 * U1 * 2 * TURNS1)
                act.sem_inc(parts_free, 1)
                with act.Fori(0, NC) as c:
                    act.wait_ge(sd_turned, c + 1)
                    act.sem_inc(parts_free, 1)
                    for b, (start, end) in enumerate(((0, 512), (512, C * P))):
                        nc.scalar.copy(hT[:, start:end], ps_main[:, b, 0:end - start])
                        ins = nc.scalar.copy(dT[:, start:end], ps_main[:, 2 + b, 0:end - start])
                    ins.then_inc(sd_ready, 1)

            for k in range(PHASES):
                take_sums(k)
                take_carries(k)
                if k in MATS:
                    bend_nodes(k)
                if k in LN_AFTER:
                    root(NORM[k])
                if k == 3 and layers > 1:
                    layer1()
                    root(2)

        @block.vector
        def _(v):
            tt, ts = nc.vector.tensor_tensor, nc.vector.tensor_scalar
            step = v_step

            def settle():
                v.wait_ge(step.sem, step.value())

            def per_node(t, j0, n=C):
                return t[:, bass.ds(j0, n)].unsqueeze(2).to_broadcast([P, n, F])

            def split(t):
                return t.rearrange("p (j f) -> p j f", f=F)

            step.up(nc.vector.memset(zeros[:], 0.0))
            step.up(nc.vector.memset(hot_zero[:], 0.0))
            step.up(nc.vector.memset(ones[:], 1.0))
            step.up(nc.vector.memset(node_idx[:, J:J + 2 * C], 0))
            settle()
            nc.vector.memset(row_chg, 0.0).then_inc(zero_made, 1)
            v.wait_ge(consts, 3)
            step.up(nc.vector.tensor_copy(iota_f[:], iota_i[:]))
            step.up(nc.vector.tensor_copy(iota_h[:], iota_i[:]))
            step.up(nc.vector.tensor_copy(part_f[:], part_i[:]))
            settle()
            step.up(ts(ident[:], iota_f[:], part_f[:], None, ALU.is_equal))
            step.up(ts(tri[:], iota_f[:], part_f[:], None, ALU.is_ge))
            step.up(ts(low[:], iota_f[:], part_f[:], None, ALU.is_lt))
            v.wait_ge(inputs_in, 16 * len(LOADS))
            v.wait_ge(zero_made, 1)

            def tiles(t):
                return t.rearrange("g (u e) -> g u e", u=U)

            chg, pre = tiles(row_chg), tiles(row_pre)
            step.up(tt(chg[:, :, 1:P], tiles(row_dst)[:, :, 1:P], tiles(row_dst)[:, :, 0:P - 1], ALU.not_equal))
            step.up(nc.vector.memset(row_rank, 1.0))
            settle()
            step.up(nc.vector.memset(tiles(row_rank)[:, :, 0:1], 0.0))
            settle()
            step.up(nc.vector.tensor_tensor_scan(row_pre, row_rank, row_chg, 0.0, ALU.mult, ALU.add))
            settle()
            in_tile = pre[:, :, P - 1:P]
            step.up(tt(tiles(row_rank), in_tile.to_broadcast([G, U, P]), pre, ALU.subtract))
            step.up(nc.vector.tensor_copy(tiles(row_val)[:, :, 0:P - 1], chg[:, :, 1:P]))
            step.up(tt(tiles(row_val)[:, :, P - 1], tiles(row_dst)[:, :, P - 1], next_first[0:G], ALU.not_equal))
            step.up(nc.vector.tensor_copy(small[0:G, 1, 0:U], tid_i[0:G, :]))
            settle()
            step.up(nc.vector.scalar_tensor_tensor(carry_idx[0:G, :], pre[:, :, P - 1], float(T), small[0:G, 1, 0:U],
                                                   ALU.mult, ALU.add))
            nc.vector.scalar_tensor_tensor(row_val, row_rank, 1.0, row_val, ALU.add, ALU.mult).then_inc(keys_ready, 1)

            def parts(source, lo, hi):
                step.up(ts(col_i, source, P - 1, None, ALU.bitwise_and))
                settle()
                step.up(nc.vector.tensor_copy(keys[:, :, lo], col_i.rearrange("p (g u) -> p g u", u=U)))
                settle()
                step.up(ts(col_i, source, 7, None, ALU.logical_shift_right))
                settle()
                step.up(nc.vector.tensor_copy(keys[:, :, hi], col_i.rearrange("p (g u) -> p g u", u=U)))
                settle()

            parts(dst_i, 0, 1)
            parts(src_i, 3, 4)
            step.up(nc.vector.scalar_tensor_tensor(src_idx[:].rearrange("p (g u) -> p g u", u=U), keys[:, :, 3],
                                                   float(J), keys[:, :, 4], ALU.mult, ALU.add))
            step.up(nc.vector.scalar_tensor_tensor(dst_idx.rearrange("p (g u) -> p g u", u=U), keys[:, :, 0],
                                                   float(J), keys[:, :, 1], ALU.mult, ALU.add))
            first_i = first_b[:].bitcast(I32)
            last_i = last_b.bitcast(I32)
            step.up(nc.vector.memset(cont[:, 0:1], 0.0))
            step.up(tt(cont[:, 1:T], first_i[:, 1:T], last_i[:, 0:T - 1], ALU.is_equal))
            step.up(tt(run_sum[:], first_i, last_i, ALU.is_equal))
            settle()
            step.up(tt(chained[:], run_sum[:], cont[:], ALU.mult))

            v.wait_ge(ranks_in, 8)
            settle()
            v.sem_inc(hot_ready, 1)
            kg = small[:].rearrange("p a b -> p (a b)")[:, 4 * J:4 * J + 160].rearrange("p (h q u) -> p h q u", h=2, q=5)

            with v.Fori(0, TURNS) as i:
                step.enter(i, 2)
                for h in range(2):
                    v.wait_ge(hot_used, i * 2 + h + 1)
                    v.sem_inc(v_go, 1)
                    step.up(nc.vector.tensor_copy(kg[:, h].rearrange("p q u -> p (q u)"),
                                                  big[:, bass.ds((i * 2 + h) * (5 * U), 5 * U)]))
                    settle()
                    v.sem_inc(v_go, 1)
                    for u in range(U):
                        ts(hot_lo[:, 0, h, u], iota_h[:], kg[:, h, 0, u:u + 1], None, ALU.is_equal)
                        ts(hot_w[:, h, u, 0:J], iota_h[:, 0:J], kg[:, h, 1, u:u + 1], None, ALU.is_equal)
                        ts(hot_w[:, h, u, J:2 * J], iota_h[:, 0:J], kg[:, h, 1, u:u + 1], kg[:, h, 2, u:u + 1],
                           ALU.is_equal, ALU.mult)
                        ts(hot_lo[:, 1, h, u], iota_h[:], kg[:, h, 3, u:u + 1], None, ALU.is_equal)
                        ins = ts(hot_s[:, h, u, 0:J], iota_h[:, 0:J], kg[:, h, 4, u:u + 1], None, ALU.is_equal)
                    ins.then_inc(hot_ready, 1)
                step.leave(TURNS)

            v.wait_ge(counted, 1)
            step.up(nc.vector.tensor_copy(deg_src[:], ps_out[:, 1, 0:J]))
            step.up(nc.vector.tensor_copy(small[:, 1], ps_out[:, 0, J:2 * J]))
            step.up(ts(small[:, 0], ps_out[:, 0, 0:J], 1.0, None, ALU.add))
            step.up(nc.vector.tensor_copy(deg_dst[:], ps_out[:, 0, 0:J]))
            settle()
            v.sem_inc(deg_ready, 1)
            v.sem_inc(root_ready, 1)
            v.wait_ge(cum_ready, 1)
            step.up(nc.vector.memset(small[:, 2], 1.0))
            step.up(nc.vector.tensor_copy(small[:, 4], ps_last[:, 1, P:P + J]))
            settle()
            step.up(nc.vector.tensor_tensor_scan(small[:, 3], small[:, 2], small[:, 4], 0.0, ALU.mult, ALU.add))
            settle()
            step.up(tt(small[:, 3], small[:, 3], small[:, 4], ALU.subtract))
            settle()
            step.up(tt(small[:, 3], small[:, 3], ps_last[:, 1, 0:J], ALU.add))
            settle()
            cum_i = small[:, 5].bitcast(I32)
            tile_i = small[:, 6].bitcast(I32)
            step.up(ts(cum_i, small[:, 3], -1.0, 0.0, ALU.add, ALU.max))
            settle()
            step.up(ts(tile_i, cum_i, 7, None, ALU.logical_shift_right))
            settle()
            step.up(nc.vector.tensor_copy(small[:, 4], tile_i))
            step.up(ts(small[:, 2], small[:, 1], 0.0, None, ALU.is_gt))
            settle()
            step.up(nc.vector.scalar_tensor_tensor(small[:, 4], small[:, 1], float(T), small[:, 4], ALU.mult, ALU.add))
            settle()
            step.up(ts(small[:, 4], small[:, 4], float(-T - ZERO_ROW), None, ALU.add))
            settle()
            step.up(tt(small[:, 4], small[:, 4], small[:, 2], ALU.mult))
            settle()
            step.up(ts(node_idx[:, 0:J], small[:, 4], float(ZERO_ROW), None, ALU.add))
            v.wait_ge(root_in, 1)
            settle()
            step.up(nc.vector.reciprocal(small[:, 7], dinv[:]))
            settle()
            step.up(nc.vector.tensor_copy(dinv[:], small[:, 7]))
            settle()

            def make_table(scaled):
                if scaled:
                    tt(split(own[:]), split(x_cur[:]), per_node(dinv, 0, J), ALU.mult).then_inc(own_ready, NC)
                else:
                    nc.vector.tensor_copy(own[:], x_cur[:]).then_inc(own_ready, NC)

            def pick_slots(k, weighted):
                with v.Fori(0, TURNS) as i:
                    step.enter(i, 4)
                    for h in range(2):
                        m = (i + TURNS * k) * 2 + h
                        at = bass.ds((i * 2 + h) * U, U)
                        v.wait_ge(group_done, m + 1)
                        v.sem_inc(v_go, 1)
                        nc.vector.tensor_copy(idx[:, h], src_idx[:, at]).then_inc(idx_ready, 1)
                        step.up(nc.vector.tensor_copy(w_g[:, h], (edge_w if weighted else rank)[:, at]))
                        step.up(nc.vector.tensor_copy(rank_g[:, h], rank[:, at]))
                        settle()
                        v.sem_inc(v_go, 1)
                        for u in range(U):
                            if weighted:
                                ins = ts(pick[:, h, u], iota_f[:], rank_g[:, h, u:u + 1], w_g[:, h, u:u + 1],
                                         ALU.is_equal, ALU.mult)
                            else:
                                ins = ts(pick[:, h, u], iota_f[:], rank_g[:, h, u:u + 1], None, ALU.is_equal)
                        ins.then_inc(pick_ready, 1)
                    step.leave(TURNS)

            def carry_runs(k):
                v.wait_ge(sums_out, 2 * TURNS * (k + 1) + 2)
                step.up(nc.vector.tensor_tensor_scan(run_sum[0:F], chained[0:F], tile_sum[0:F], 0.0, ALU.mult, ALU.add))
                settle()
                step.up(nc.vector.memset(tile_sum[0:F, 0:1], 0.0))
                step.up(tt(tile_sum[0:F, 1:T], run_sum[0:F, 0:T - 1], cont[0:F, 1:T], ALU.mult))
                settle()
                v.sem_inc(carry_ready, 1)

            def finish_nodes(k):
                kind = KIND[k]
                per = {"wide": 1, "wide_skip": 1, "narrow": 3, "residual": 5, "conv": 1, "conv_out": 3, "gin": 0}[kind]
                for h in range(2):
                    nc.vector.tensor_copy(nidx[:, h], node_idx[:, h * C:(h + 1) * C]).then_inc(nidx_ready, 1)
                with v.Fori(0, CTURNS) as i:
                    step.enter(i, 2 * per)
                    for h in range(2):
                        c = i * 2 + h
                        chunk = bass.ds(c * (C * F), C * F)
                        if kind == "narrow":
                            v.wait_ge(own_ready, c + NC * (k + 1))
                        elif kind in ("residual", "conv_out"):
                            settle()
                        v.wait_ge(agg_in[h], (i + CTURNS * k) * (16 * C) + 16 * C)
                        v.sem_inc(v_go, 1)
                        if kind == "gin":
                            v.wait_ge(z_turned, c + (NC * TURNED.index(k) - 1))
                            v.sem_inc(v_go, 1)
                            tt(z[:, h], agg[:, h], own[:, chunk], ALU.add).then_inc(z_ready, 1)
                        else:
                            step.up(tt(tmp[:], agg[:, h], own[:, chunk], ALU.add))
                            settle()
                            v.sem_inc(v_go, 1)
                            ins = tt(split(z[:, h]), split(tmp[:]), per_node(dinv, c * C), ALU.mult)
                            if k in MATS:
                                ins.then_inc(z_ready, 1)
                            else:
                                step.up(ins)
                        nc.vector.tensor_copy(nidx[:, h], node_idx[:, bass.ds(c * C + 2 * C, C)]).then_inc(nidx_ready, 1)
                        if kind in ("narrow", "residual"):
                            bias = (W["b2"] if kind == "narrow" else W["b4"])[0][:]
                            settle()
                            v.sem_inc(v_go, 1)
                            step.up(tt(split(tmp[:]), split(z[:, h]), bias.unsqueeze(1).to_broadcast([P, C, F]), ALU.add))
                            settle()
                            v.sem_inc(v_go, 1)
                            if kind == "narrow":
                                nc.vector.scalar_tensor_tensor(split(own[:, chunk]), split(tmp[:]), 0.0,
                                                               per_node(dinv, c * C), ALU.max, ALU.mult).then_inc(own_ready, 1)
                            else:
                                step.up(nc.vector.scalar_tensor_tensor(z[:, h], tmp[:], 0.0, x_cur[:, chunk],
                                                                       ALU.max, ALU.add))
                                settle()
                                v.sem_inc(v_go, 1)
                                step.up(tt(x_cur[:, chunk], z[:, h], x_cur[:, chunk], ALU.add))
                            continue
                        m = (i + CTURNS * TURNED.index(k)) * 2 + h + 1
                        if kind == "gin":
                            continue
                        if kind == "wide_skip":
                            v.wait_ge(hT_ready, m + HT_EXTRA[k])
                            v.sem_inc(v_go, 1)
                            tt(hT[:], hT[:], big[:, bass.ds(c * (C * P), C * P)], ALU.add).then_inc(skip_ready, 1)
                        v.wait_ge(o_done, m + O_EXTRA[k])
                        v.sem_inc(v_go, 1)
                        product = ps_out[:, 0, 0:C * F]
                        if kind == "conv_out":
                            step.up(tt(split(tmp[:]), split(product), W["cbl"][0][:].unsqueeze(1).to_broadcast([P, C, F]), ALU.add))
                            settle()
                            v.sem_inc(v_go, 1)
                            step.up(tt(x_cur[:, chunk], tmp[:], x_cur[:, chunk], ALU.add))
                        else:
                            tt(split(own[:, chunk]), split(product), per_node(dinv, c * C), ALU.mult).then_inc(own_ready, 1)
                    step.leave(CTURNS)

            def norm_hidden(k):
                l = k - 6
                v.wait_ge(hT_ready, NC * (TURNED.index(k) + 1) + HT_EXTRA[k])
                for s in range(BN_PARTS):
                    ins = nc.vector.bn_stats(stats[:, s * 6:(s + 1) * 6], big[0:F, s * BN_LEN:(s + 1) * BN_LEN])
                step.up(ins)
                settle()
                step.up(nc.vector.bn_aggr(bn[:, 0:2], stats[:]))
                settle()
                ts(bn[:, 2:3], bn[:, 1:2], BN_EPS, None, ALU.add).then_inc(bn_var, 1)
                v.wait_ge(bn_root, l + 1)
                step.up(nc.vector.reciprocal(bn[:, 6:7], bn[:, 3:4]))
                settle()
                step.up(tt(bn[:, 4:5], bn[:, 6:7], W["gg"][0][:, l:l + 1], ALU.mult))
                settle()
                step.up(tt(bn[:, 7:8], bn[:, 0:1], bn[:, 4:5], ALU.mult))
                settle()
                tt(bn[:, 5:6], W["gbe"][0][:, l:l + 1], bn[:, 7:8], ALU.subtract).then_inc(bn_ready, 1)
                last = k == PHASES - 1
                with v.Fori(0, NC) as c:
                    step.enter(c, 1 if last else 0)
                    chunk = bass.ds(c * (C * F), C * F)
                    if last:
                        settle()
                    else:
                        v.wait_ge(own_ready, c + NC * (k + 1))
                    v.wait_ge(o_done, c + (NC * TURNED.index(k) + 1))
                    v.sem_inc(v_go, 1)
                    tt(split(tmp[:]), split(ps_out[:, 0, 0:C * F]), W["gb2"][0][:, l * F:(l + 1) * F].unsqueeze(1)
                       .to_broadcast([P, C, F]), ALU.add).then_inc(o_taken, 1)
                    v.wait_ge(o_taken, c + (NC * l + 2))
                    v.sem_inc(v_go, 1)
                    if last:
                        step.up(nc.vector.scalar_tensor_tensor(x_cur[:, chunk], tmp[:], 0.0, x_cur[:, chunk],
                                                               ALU.max, ALU.add))
                    else:
                        ts(own[:, chunk], tmp[:], 0.0, None, ALU.max).then_inc(own_ready, 1)
                    step.leave(NC)

            def norm_layer(last):
                xs, cs = split(x_cur[:]), split(own[:])
                settle()
                step.up(nc.vector.tensor_reduce(small[:, 0], xs, AX.X, ALU.add))
                settle()
                step.up(ts(small[:, 1], small[:, 0], 1.0 / F, None, ALU.mult))
                settle()
                step.up(tt(cs, xs, per_node(small[:, 1], 0, J), ALU.subtract))
                settle()
                step.up(tt(xs, cs, cs, ALU.mult))
                settle()
                step.up(nc.vector.tensor_reduce(small[:, 0], xs, AX.X, ALU.add))
                settle()
                ts(small[:, 2], small[:, 0], 1.0 / F, LN_EPS, ALU.mult, ALU.add).then_inc(ln_var, 1)
                norm_layer.n += 1
                v.wait_ge(ln_root, norm_layer.n)
                step.up(nc.vector.reciprocal(small[:, 4], small[:, 3]))
                settle()
                ins = tt(xs, cs, per_node(small[:, 4], 0, J), ALU.mult)
                if last:
                    ins.then_inc(result_ready, 1)
                else:
                    step.up(ins)
                    settle()
            norm_layer.n = 0

            def layer1():
                def spread(t, n=C):
                    return t.unsqueeze(1).to_broadcast([P, n, t.shape[1]])

                def settled():
                    settle()
                    v.sem_inc(v_go, 1)

                step.up(nc.vector.memset(times[:], 1.0))
                with v.Fori(0, CTURNS) as i:
                    for h in range(2):
                        c = i * 2 + h
                        nc.vector.tensor_copy(z[:, h], x_cur[:, bass.ds(c * (C * F), C * F)]).then_inc(x_ready, 1)
                        v.wait_ge(st_done, c + 1)
                        v.sem_inc(v_go, 1)
                        for t in range(C):
                            bank = ps_main[:, t // 2, (t % 2) * 2 * H:(t % 2 + 1) * 2 * H]
                            tt(new_s[:, t * H:(t + 1) * H], bank[:, 0:H], W["eb1"][0][:], ALU.add)
                            ins = nc.vector.tensor_copy(new_t[:, t * H:(t + 1) * H], bank[:, H:2 * H])
                        ins.then_inc(st_ready, 1)
                        v.wait_ge(st_out, c * 32 + 32)
                        v.sem_inc(v_go, 1)
                v.sem_inc(arg_ready, 1)
                with v.Fori(0, TURNS1) as i:
                    step.enter(i, 2 * 3)
                    for h in range(2):
                        m = i * 2 + h
                        at = bass.ds(m * U1, U1)
                        v.wait_ge(group1_done, m + 1)
                        v.sem_inc(v_go, 1)
                        nc.vector.tensor_copy(idx[:, h, 0:U1], src_idx[:, at])
                        nc.vector.tensor_copy(idx[:, h, U1:2 * U1], dst_idx[:, at]).then_inc(idx1_ready, 1)
                        step.up(nc.vector.tensor_copy(rank_g[:, h, 0:U1], rank[:, at]))
                        v.wait_ge(edge_in[h], i * 48 + 48)
                        settled()
                        for u in range(U1):
                            one = src_c[:, h, u:u + 1]
                            ts(pick1[:, h, u], iota_f[:], rank_g[:, h, u:u + 1], None, ALU.is_equal)
                            ins = ts(same[:, h, u], src_b[:, h, u * P:(u + 1) * P], one, None, ALU.is_equal)
                        step.up(ins)
                        settled()
                        for u in range(U1):
                            ins = nc.vector.tensor_tensor_reduce(scratch[:, h, u * P:(u + 1) * P], same[:, h, u], low[:], 1.0, 0.0, ALU.mult, ALU.add,
                                                                 earlier[:, h, u:u + 1])
                        ins.then_inc(pick1_ready, 1)
                        v.wait_ge(pick1_ready, m + 1)
                        v.wait_ge(added_free, m + 1)
                        v.sem_inc(v_go, 1)
                        nc.vector.scalar_tensor_tensor(add_idx[:, h], earlier[:, h], float(2 * NPAD), idx[:, h, 0:U1],
                                                       ALU.mult, ALU.add).then_inc(add_idx_ready, 1)
                        v.wait_ge(rows1_in[h], i * (32 * U1) + 32 * U1)
                        v.wait_ge(t_ready, m + 2)
                        v.sem_inc(v_go, 1)
                        step.up(tt(rows_s[:, h], rows_s[:, h], rows_t[:, h], ALU.add))
                        settled()
                        tt(arg, rows_s[:, h], t_emb, ALU.add).then_inc(arg_ready, 1)
                    step.leave(TURNS1)
                v.wait_ge(sums1_out, 2 * TURNS1 + 2)
                step.up(nc.vector.tensor_tensor_scan(run_sum[:], chained[:], tile_sum[:], 0.0, ALU.mult, ALU.add))
                settle()
                step.up(nc.vector.memset(tile_sum[:, 0:1], 0.0))
                step.up(tt(tile_sum[:, 1:T], run_sum[:, 0:T - 1], cont[:, 1:T], ALU.mult))
                settle()
                v.sem_inc(carry1_ready, 1)
                v.sem_inc(o1_taken, 1)
                for h in range(2):
                    nc.vector.tensor_copy(nidx[:, h], node_idx[:, h * C:(h + 1) * C]).then_inc(nidx1_ready, 1)
                with v.Fori(0, CTURNS) as i:
                    step.enter(i, 2 * 3)
                    for h in range(2):
                        c = i * 2 + h
                        chunk = bass.ds(c * (C * F), C * F)
                        settled()
                        step.up(tt(split(tmp[:]), spread(W["eb2"][0][:, 0:F]), per_node(deg_src, c * C), ALU.mult))
                        step.up(tt(split(z[:, h]), spread(W["eb2"][0][:, F:2 * F]), per_node(deg_dst, c * C), ALU.mult))
                        settled()
                        tt(tmp[:], tmp[:], z[:, h], ALU.add).then_inc(tmp_sum, 1)
                        v.wait_ge(sd_turned, c + 1)
                        v.sem_inc(v_go, 1)
                        nc.vector.tensor_copy(nidx[:, h], node_idx[:, bass.ds(c * C + 2 * C, C)]).then_inc(nidx1_ready, 1)
                        v.wait_ge(tmp_sum, c + 1)
                        v.wait_ge(o1_done, c + 1)
                        v.sem_inc(v_go, 1)
                        tt(z[:, h], tmp[:], ps_out[:, 0, 0:C * F], ALU.add).then_inc(o1_taken, 1)
                        v.wait_ge(o1_taken, c + 2)
                        v.sem_inc(v_go, 1)
                        step.up(tt(x_cur[:, chunk], z[:, h], x_cur[:, chunk], ALU.add))
                    step.leave(CTURNS)
                norm_layer(layers == 2)

            for k in range(PHASES):
                if k in (0, 4, 6):
                    make_table(scaled=k < 6)
                if k == 6:
                    v.sem_inc(o_taken, 1)
                    v.wait_ge(weights_in, 16)
                pick_slots(k, weighted=k >= 6)
                carry_runs(k)
                finish_nodes(k)
                if k >= 6:
                    norm_hidden(k)
                if k in LN_AFTER:
                    norm_layer(k == PHASES - 1 and layers != 2)
                if k == 3 and layers > 1:
                    layer1()


BY_HIDDEN = ("L3_gnn_b1", "L3_gnn_gamma", "L3_gnn_beta")


def kernel(x, src, dst, edge_weight, edge_weight1, **w):
    import numpy as np
    import concourse.bacc as bacc
    from concourse.bass_utils import run_bass_kernel_spmd as run

    def padded(a, n, value):
        a = np.asarray(a).reshape(len(a), -1)
        return np.concatenate([a, np.full((n - len(a), a.shape[1]), value, a.dtype)])

    def columns(a):
        return np.ascontiguousarray(a.reshape(T, P).T)

    nodes = padded(x, NPAD, 0).reshape(J, P, F).transpose(1, 0, 2).reshape(P, J * F)
    srcs = padded(src, EPAD, PAD_NODE).reshape(-1)
    dsts = padded(dst, EPAD, PAD_NODE).reshape(-1)
    times = padded(edge_weight, EPAD, 0).reshape(-1)
    ew = padded(edge_weight1, EPAD, 0).reshape(-1)
    by_tile = dsts.reshape(T, P)
    end = np.full(1, -1, dsts.dtype)
    arrays = {
        "x_nodes": np.ascontiguousarray(nodes),
        "src_cols": columns(srcs),
        "dst_cols": columns(dsts),
        "weight_cols": columns(ew),
        "dst_rows": np.ascontiguousarray(dsts.reshape(G, U * P)),
        "tile_first": np.concatenate([by_tile[:, 0], end]),
        "tile_last": np.ascontiguousarray(by_tile[:, -1]),
        "time_row": times.reshape(1, EPAD),
        "src_row": srcs.reshape(1, EPAD),
    }
    for name, a in w.items():
        arrays[name] = np.ascontiguousarray(np.asarray(a).T if name in BY_HIDDEN else np.asarray(a))
    nc = bacc.Bacc("TRN2", target_bir_lowering=False, num_devices=1)
    ap = {n: nc.dram_tensor("in_" + n, a.shape, mybir.dt.from_np(a.dtype), kind="ExternalInput").ap() for n, a in arrays.items()}

    def mat(name):
        return (ap[name], list(ap[name].shape), "mat")

    def row(name):
        return (ap[name], [P, ap[name].shape[0]], "row")

    def col(name):
        return (ap[name].rearrange("(p o) -> p o", o=1), [ap[name].shape[0], 1], "col")

    weights = {"W1": mat("L0_gnn_W1"), "b1": col("L0_gnn_b1"), "W2": mat("L0_gnn_W2"), "b2": row("L0_gnn_b2"),
               "W3": mat("L0_gnn_W3"), "b3": col("L0_gnn_b3"), "W4": mat("L0_gnn_W4"), "b4": row("L0_gnn_b4")}
    if 4 > 1:
        weights.update({"eW1": (ap["L1_gnn_W1"].rearrange("(s k) m -> k s m", s=2), [F, 2, H], "mat"),
                        "eb1": row("L1_gnn_b1"), "eWt": ((ap["L1_gnn_Wt"], ap["L1_gnn_bt"].rearrange("(o m) -> o m", o=1)), [2, H], "rows"),
                        "eW2": mat("L1_gnn_W2"), "eb2": row("L1_gnn_b2")})
    if 4 > 2:
        weights.update({"cW1": mat("L2_gnn_W1"), "cb1": col("L2_gnn_b1"), "cW2": mat("L2_gnn_W2"), "cb2": col("L2_gnn_b2"),
                        "cWl": mat("L2_gnn_Wl"), "cbl": row("L2_gnn_bl")})
    if 4 > 3:
        def layers_in(name):
            return (ap[name].rearrange("l k m -> k l m"), [F, 3, F], "mat")

        def layer_cols(name):
            return (ap[name], [F, 3], "mat")

        weights.update({"gW1": layers_in("L3_gnn_W1"), "gW2": layers_in("L3_gnn_W2"), "gb1": layer_cols("L3_gnn_b1"),
                        "gg": layer_cols("L3_gnn_gamma"), "gbe": layer_cols("L3_gnn_beta"),
                        "gb2": (ap["L3_gnn_b2"].rearrange("l k -> (l k)"), [P, 3 * F], "row")})
    out = nc.dram_tensor("out_0_dram", (P, J * F), F32, kind="ExternalOutput").ap()
    gnn_program(nc, ap["x_nodes"], ap["src_cols"], ap["dst_cols"], ap["weight_cols"], ap["dst_rows"], ap["tile_first"],
                ap["tile_last"], ap["time_row"], ap["src_row"], weights, out, layers=4)
    r = run(nc, [{"in_" + n: a for n, a in arrays.items()}], core_ids=[0])
    got = r.results[0]["out_0_dram"].reshape(P, J, F).transpose(1, 0, 2).reshape(NPAD, F)[:N]
    return np.ascontiguousarray(got)
```

```python
from contextlib import ExitStack

import concourse.bass as bass
from concourse import mybir

ALU = mybir.AluOpType
ACT = mybir.ActivationFunctionType
AX = mybir.AxisListType
F32 = mybir.dt.float32
BF16 = mybir.dt.bfloat16
I32 = mybir.dt.int32
U32 = mybir.dt.uint32

P = 128
N = 12500
E = 200000
F = 64
H = 128
J = -(-N // P)
NPAD = J * P
U = 16
T = -(-E // (P * 2 * U)) * 2 * U
G = T // U
EPAD = T * P
PAD_NODE = NPAD - 1
C = 7
NC = J // C
ZERO_ROW = P * T
HI_POOL = 7
BN_PARTS = 25
BN_LEN = N // BN_PARTS
LN_EPS = 1e-5
BN_EPS = 1e-5
assert BN_PARTS * BN_LEN == N and BN_LEN <= 512
assert NC * C == J and NC % 2 == 0 and G % 2 == 0 and PAD_NODE >= N


class Tally:

    def __init__(self, sem):
        self.sem, self.base, self.n = sem, 0, 0

    def up(self, ins, by=1):
        ins.then_inc(self.sem, by)
        self.n += by
        return ins

    def value(self):
        return self.base + self.n

    def enter(self, i, per_turn):
        self.start, self.per_turn = self.base + self.n, per_turn
        self.base, self.n = self.start + i * per_turn, 0

    def leave(self, turns):
        assert self.n == self.per_turn, (self.n, self.per_turn)
        self.base, self.n = self.start + turns * self.per_turn, 0


def gnn_program(nc, x_nodes, src_cols, dst_cols, weight_cols, dst_rows, tile_first, tile_last, time_row, time_cols, src_row,
                weights, out, layers=4):
    PHASES = {1: 4, 2: 4, 3: 6, 4: 9}[layers]
    TURNS = G // 2
    CTURNS = NC // 2
    U1, TURNS1 = U // 2, G
    CW = C * P // 2
    LN_AFTER = [3, 5, 8]
    NORM = {3: 1, 5: 3, 8: 4}
    KIND = ["wide", "narrow", "wide_skip", "residual", "conv", "conv_out", "gin", "gin", "gin"]

    with ExitStack() as ctx:
        def sb(name, shape, dt=F32):
            return ctx.enter_context(nc.sbuf_tensor(name, shape, dt))[:]

        def psum(name, shape):
            return ctx.enter_context(nc.psum_tensor(name, shape, F32))[:]

        def sem(name):
            return ctx.enter_context(nc.semaphore(name))

        table = nc.dram_tensor("table", (NPAD, F), F32).ap()
        partial = nc.dram_tensor("partial", (P * T + P, F), F32).ap()
        table_v = table.rearrange("(p j) f -> p (j f)", p=P)
        partial_v = partial[0:P * T, :].rearrange("(p t) f -> p (t f)", p=P)

        table_s = nc.dram_tensor("table_s", (NPAD, H), F32).ap()
        table_t = nc.dram_tensor("table_t", (NPAD, H), F32).ap()
        partial1 = nc.dram_tensor("partial1", (P * T + P, H), F32).ap()
        partial1_v = partial1[0:P * T, :].rearrange("(p t) f -> p (t f)", p=P)
        by_src = [nc.dram_tensor("by_src%d" % u, (NPAD, H), F32).ap() for u in range(U1)]
        by_src_v = [a.rearrange("(p j) f -> p (j f)", p=P) for a in by_src]

        in_order = {"src_cols": nc.dram_tensor("sorted_src_cols", (P, T), I32).ap(),
                    "weight_cols": nc.dram_tensor("sorted_weight_cols", (P, T), F32).ap(),
                    "src_row": nc.dram_tensor("sorted_src_row", (1, EPAD), I32).ap(),
                    "time_row": nc.dram_tensor("sorted_time_row", (1, EPAD), F32).ap()}
        dst_line = nc.dram_tensor("sorted_dst", (EPAD,), I32).ap()
        moved = [nc.dram_tensor("moved%d" % d, (EPAD, 4), F32).ap() for d in range(2)]

        ps_main = psum("ps_main", [P, 4, 512])
        ps_out = psum("ps_out", [P, 2, 512])
        ps_last = psum("ps_last", [P, 2, 512])

        x_cur = sb("x_cur", [P, J * F])
        own = sb("own", [P, J * F])
        big = sb("big", [P, NPAD])
        rank = sb("rank", [P, T])
        edge_w = sb("edge_w", [P, T])
        src_idx = sb("src_idx", [P, T], U32)
        chained = sb("chained", [P, T])
        cont = sb("cont", [P, T])
        tile_sum = sb("tile_sum", [P, T])
        run_sum = sb("run_sum", [P, T])
        rows = sb("rows", [P, 2, U * F])
        pick = sb("pick", [P, 2, U, P])
        stage = sb("stage", [P, 2, U * F])
        idx = sb("idx", [P, 2, U], U32)
        rank_g = sb("rank_g", [P, 2, U])
        w_g = sb("w_g", [P, 2, U])
        node_idx = sb("node_idx", [P, J + 2 * C], U32)
        nidx = sb("nidx", [P, 2, C], U32)
        agg = sb("agg", [P, 2, C * F])
        z = sb("z", [P, 2, C * F])
        tmp = sb("tmp", [P, C * F])
        zT = sb("zT", [F, C * P])
        hT = sb("hT", [P, C * P])
        carry_rows = pick[:, 0].rearrange("p u c -> p (u c)")[:, 0:U * F]
        zeros = hT
        carry_idx = sb("carry_idx", [P, U], U32)
        deg_dst = sb("deg_dst", [P, J])
        deg_src = sb("deg_src", [P, J])
        dinv = sb("dinv", [P, J])
        iota_f = sb("iota_f", [P, P])
        iota_h = sb("iota_h", [P, P], BF16)
        iota_i = sb("iota_i", [P, P], I32)
        part_i = sb("part_i", [P, 1], I32)
        part_f = sb("part_f", [P, 1])
        ident = sb("ident", [P, P])
        tri = sb("tri", [P, P])
        ones = sb("ones", [P, P])
        hot_zero = sb("hot_zero", [P, P], BF16)
        low = sb("low", [P, P])
        src_c = sb("src_c", [P, 2, U1], I32)
        src_lo = sb("src_lo", [P, 2, U1], I32)
        src_hi = sb("src_hi", [P, 2, U1], I32)
        earlier = sb("earlier", [P, 2, U1])
        add_idx = sb("add_idx", [P, 2, U1], U32)
        stats = sb("stats", [F, BN_PARTS * 6])
        bn = sb("bn", [F, 8])
        small = sb("small", [P, 8, J])
        tid_i = sb("tid_i", [P, U], I32)
        next_first = sb("next_first", [P, U], I32)

        W1G = U1 * H
        rows_s = rows
        rows_t = big[:, 0:2 * W1G].rearrange("p (h c) -> p h c", h=2)
        pick1, same = pick[:, :, 0:U1], pick[:, :, U1:2 * U1]
        hid = big[:, 2 * W1G:4 * W1G].rearrange("p (h c) -> p h c", h=2)
        merged = big[:, 4 * W1G:6 * W1G].rearrange("p (h c) -> p h c", h=2)
        src_b = big[:, 6 * W1G:8 * W1G].bitcast(I32).rearrange("p (h c) -> p h c", h=2)
        t_emb = big[:, 8 * W1G:9 * W1G]
        arg = big[:, 9 * W1G:10 * W1G]
        scratch = big[:, 6 * W1G:8 * W1G].rearrange("p (h c) -> p h c", h=2)
        times = big[0:2, 10 * W1G:12 * W1G].rearrange("p (h c) -> p h c", h=2)
        carry_rows1 = big[:, 0:U * H]
        parts_s = big[:, 2 * W1G:2 * W1G + U1 * C * H].rearrange("p (k c) -> p k c", k=U1)
        agg1 = big[:, 9 * W1G:9 * W1G + 2 * C * H].rearrange("p (h c) -> p h c", h=2)
        dT = big[:, 11 * W1G:11 * W1G + C * P]
        new_s = big[:, 0:C * H]
        new_t = big[:, C * H:2 * C * H]
        hot_src = own[:, 0:U1 * (P + J)].bitcast(BF16).rearrange("p (h u c) -> p h u c", h=2, u=U1)
        dst_idx = edge_w[:].bitcast(U32)

        keys = big[:, 0:5 * T].rearrange("p (g q u) -> p g q u", q=5, u=U)
        hot_lo = pick.rearrange("p h u c -> p (h u c)")[:, 0:U * P].bitcast(BF16).rearrange("p (h u c) -> p h u c", h=2, u=U)
        hot_hi = big[:, 5 * T:7 * T].bitcast(BF16)[:, 0:2 * U * J].rearrange("p (h u c) -> p h u c", h=2, u=U)
        hot_end = big[:, 5 * T:8 * T].bitcast(BF16)[:, 0:2 * U * (P + J)].rearrange("p (h u c) -> p h u c", h=2, u=U)
        kg = z[:, :, 0:5 * U]
        row_dst = own[0:G, 0:U * P].bitcast(I32)
        row_chg = own[0:G, U * P:2 * U * P]
        row_pre = own[0:G, 2 * U * P:3 * U * P]
        row_rank = pick[0:G, 0].rearrange("p u c -> p (u c)")
        row_val = pick[0:G, 1].rearrange("p u c -> p (u c)")
        col_i = rows[:].rearrange("p h c -> p (h c)").bitcast(I32)[:, 0:T]
        dst_i = run_sum[:].bitcast(I32)
        src_i = tile_sum[:].bitcast(I32)
        first_b = chained
        last_b = stage[:].rearrange("p h c -> p (h c)")[:, 0:T]

        edges = own.rearrange("p (t q) -> p t q", q=4)
        digit = chained
        digit_hot, digit_sum, digit_tmp, digit_base = (pick[:, 0, q] for q in range(4))
        digit_col, digit_rank = rank_g[:, 0, 0:1], rank_g[:, 0, 1:2]
        move_idx, moving = idx[:, 0, 0:1], agg[:, 0, 0:4]
        out_of_order = sb("out_of_order", [P, 2])
        sort_flag = sb("sort_flag", [1, 1], I32)

        W = {}
        for name, (ap, shape, kind) in weights.items():
            W[name] = (sb("w_" + name, shape), ap, kind)

        inputs_in = sem("inputs_in")
        zero_in = sem("zero_in")
        zero_made = sem("zero_made")
        consts = sem("consts")
        v_step = Tally(sem("v_step"))
        a_step = Tally(sem("a_step"))
        ranks_out = sem("ranks_out")
        ranks_in = sem("ranks_in")
        keys_ready = sem("keys_ready")
        hot_ready = sem("hot_ready")
        kg_ready, hi_ready = sem("kg_ready"), sem("hi_ready")
        count_ready, count_used, counted_all, src_counted = sem("count_ready"), sem("count_used"), sem("counted_all"), sem("src_counted")
        hot_used = sem("hot_used")
        counted = sem("counted")
        deg_ready = sem("deg_ready")
        cum_ready = sem("cum_ready")
        root_ready = sem("root_ready")
        root_in = sem("root_in")
        own_ready = sem("own_ready")
        table_out = sem("table_out")
        idx_ready = sem("idx_ready")
        pool_go = sem("pool_go")
        rows_in = [[sem("rows_in%d_%d" % (s, h)) for h in range(2)] for s in range(-(-PHASES // 3))]
        pick_ready = sem("pick_ready")
        group_done = sem("group_done")
        sums_out = sem("sums_out")
        stored = [sem("stored0"), sem("stored1")]
        stage_free = sem("stage_free")
        carry_ready = sem("carry_ready")
        carry_turned = sem("carry_turned")
        carry_in = sem("carry_in")
        carry_added = sem("carry_added")
        nidx_ready = sem("nidx_ready")
        agg_in = [sem("agg_in0"), sem("agg_in1")]
        z_ready = sem("z_ready")
        z_turned = sem("z_turned")
        zT_ready = sem("zT_ready")
        h_done = sem("h_done")
        hT_ready = sem("hT_ready")
        bn_var, bn_root, bn_ready, o_taken = sem("bn_var"), sem("bn_root"), sem("bn_ready"), sem("o_taken")
        v_go, pe_go, act_go = sem("v_go"), sem("pe_go"), sem("act_go")
        o_done = sem("o_done")
        skip_ready = sem("skip_ready")
        stats_ready = sem("stats_ready")
        ln_var = sem("ln_var")
        ln_root = sem("ln_root")
        result_ready = sem("result_ready")
        result_out = sem("result_out")
        order_summed, flag_ready, copies_in = sem("order_summed"), sem("flag_ready"), sem("copies_in")
        s_step = Tally(sem("s_step"))
        cols_in, edges_in, unpacked, lines_out, again_in = sem("cols_in"), sem("edges_in"), sem("unpacked"), sem("lines_out"), sem("again_in")
        digit_ready, digit_used, digit_counted, digit_zeroed = sem("digit_ready"), sem("digit_used"), sem("digit_counted"), sem("digit_zeroed")
        rank_ready, edge_moved, edge_free = sem("rank_ready"), sem("edge_moved"), sem("edge_free")

        zeroed = sem("zeroed")
        x_ready, x_turned, xT_ready = sem("x_ready"), sem("x_turned"), sem("xT_ready")
        st_done, st_ready, st_out = sem("st_done"), sem("st_ready"), sem("st_out")
        edge_in = [sem("edge_in0"), sem("edge_in1")]
        idx1_ready, pick1_ready, add_idx_ready = sem("idx1_ready"), sem("pick1_ready"), sem("add_idx_ready")
        rows1_in = [sem("rows1_in0"), sem("rows1_in1")]
        t_done, t_ready, arg_ready, hid_ready = sem("t_done"), sem("t_ready"), sem("arg_ready"), sem("hid_ready")
        group1_done, sums1_out, stage1_free = sem("group1_done"), sem("sums1_out"), sem("stage1_free")
        stored1 = [sem("stored1_0"), sem("stored1_1")]
        added, added_free = sem("added"), sem("added_free")
        carry1_ready, carry1_turned, carry1_in, carry1_added = sem("carry1_ready"), sem("carry1_turned"), sem("carry1_in"), sem("carry1_added")
        nidx1_ready, parts_in, parts_free = sem("nidx1_ready"), sem("parts_in"), sem("parts_free")
        agg1_in = [sem("agg1_in0"), sem("agg1_in1")]
        sd_turned, sd_ready, o1_done, o1_taken = sem("sd_turned"), sem("sd_ready"), sem("o1_done"), sem("o1_taken")
        tmp_sum = sem("tmp_sum")
        weights_in = sem("weights_in")
        block = ctx.enter_context(nc.Block())

        def dyn(t, j0, width, per=1):
            return t[:, bass.ds(j0 * per, width * per)]

        MATS = {0: (W["W1"][0], W["b1"][0], W["W2"][0]), 2: (W["W3"][0], W["b3"][0], W["W4"][0])}
        if PHASES > 4:
            MATS[4] = (W["cW1"][0], W["cb1"][0], ident[0:F, 0:F])
            MATS[5] = (W["cW2"][0], W["cb2"][0], W["cWl"][0])
        for l in range(PHASES - 6):
            MATS[6 + l] = (W["gW1"][0][:, l], W["gb1"][0][:, l:l + 1], W["gW2"][0][:, l])
        TURNED = sorted(MATS)
        HT_EXTRA = {k: NC * max(0, k - 6) for k in TURNED}
        O_EXTRA = {k: 0 for k in TURNED}

        LOADS = []
        LOADS += [(x_cur[:], x_nodes), (dst_i, dst_cols), (src_i, src_cols),
                  (row_dst, dst_rows), (first_b[:].bitcast(I32), tile_first[0:T].partition_broadcast(P)),
                  (last_b.bitcast(I32), tile_last.partition_broadcast(P)),
                  (next_first[0:G, :], tile_first[1:T + 1].rearrange("(g u) -> g u", u=U))]
        for name, (t, ap, kind) in W.items():
            if kind == "rows":
                LOADS += [(t[r:r + 1, :], a) for r, a in enumerate(ap)]
            else:
                LOADS.append((t[:], ap.partition_broadcast(P) if kind == "row" else ap))

        def if_unsorted(eng):
            eng.wait_ge(flag_ready, 1)
            return eng.If(eng.value_load(sort_flag[0:1, 0:1], min_val=0, max_val=1) > 0)

        @block.sync
        def _(sp):
            for dst, source in LOADS:
                sp.dma_start(dst, source).then_inc(inputs_in, 16)
            for name, source in (("src_cols", src_cols), ("weight_cols", weight_cols), ("src_row", src_row), ("time_row", time_row)):
                sp.dma_start(in_order[name], source).then_inc(copies_in, 16)
            with if_unsorted(sp):
                sp.dma_start(edge_w, weight_cols).then_inc(cols_in, 16)
                sp.dma_start(cont, time_cols).then_inc(cols_in, 16)
                for d in range(2):
                    sp.wait_ge(edge_moved, 16 * T * (d + 1))
                    sp.dma_start(edges, moved[d].rearrange("(t p) q -> p t q", p=P)).then_inc(edges_in, 16)
                sp.wait_ge(unpacked, 1)
                sp.wait_ge(copies_in, 64)
                with nc.allow_non_contiguous_dma(reason="only for inputs out of order"):
                    sp.dma_start(in_order["src_cols"], src_i).then_inc(lines_out, 16)
                    sp.dma_start(in_order["weight_cols"], edge_w).then_inc(lines_out, 16)
                    sp.dma_start(in_order["src_row"][0].rearrange("(t p) -> p t", p=P), src_i).then_inc(lines_out, 16)
                    sp.dma_start(in_order["time_row"][0].rearrange("(t p) -> p t", p=P), cont).then_inc(lines_out, 16)
                    sp.dma_start(dst_line.rearrange("(t p) -> p t", p=P), dst_i).then_inc(lines_out, 16)
                    sp.wait_ge(lines_out, 80)
                    ends = dst_line.rearrange("(t p) -> t p", p=P)
                    sp.dma_start(row_dst, dst_line.rearrange("(g e) -> g e", g=G)).then_inc(again_in, 16)
                    sp.dma_start(first_b.bitcast(I32), ends[:, 0].partition_broadcast(P)).then_inc(again_in, 16)
                    sp.dma_start(last_b.bitcast(I32), ends[:, P - 1].partition_broadcast(P)).then_inc(again_in, 16)
                    starts = ends[:, 0].rearrange("(g u) -> g u", u=U)
                    sp.dma_start(next_first[0:G, 0:U - 1], starts[:, 1:U]).then_inc(again_in, 16)
                    sp.dma_start(next_first[0:G - 1, U - 1:U], starts[1:G, 0:1]).then_inc(again_in, 16)
            sp.wait_ge(zero_made, 1)
            sp.dma_start(partial[P * T:P * T + P, :], zeros[:, 0:F]).then_inc(zero_in, 16)
            sp.dma_start(partial1[P * T:P * T + P, :], zeros[:, 0:H]).then_inc(zero_in, 16)

            sp.sem_inc(stage_free, 2)

            def store_table(k):
                with sp.Fori(0, NC) as c:
                    sp.wait_ge(own_ready, c + NC * k + 1)
                    sp.dma_start(table_v[:, bass.ds(c * (C * F), C * F)], own[:, bass.ds(c * (C * F), C * F)]).then_inc(table_out, 16)

            def layer1():
                sp.wait_ge(copies_in, 64)
                with sp.Fori(0, NC) as c:
                    at = bass.ds(c * (C * H), C * H)
                    sp.wait_ge(st_ready, c + 1)
                    sp.dma_start(table_s.rearrange("(p j) f -> p (j f)", p=P)[:, at], new_s).then_inc(st_out, 16)
                    sp.dma_start(table_t.rearrange("(p j) f -> p (j f)", p=P)[:, at], new_t).then_inc(st_out, 16)
                sp.wait_ge(st_out, 32 * NC)
                sp.sem_inc(stage1_free, 2)
                with sp.Fori(0, TURNS1) as i:
                    for h in range(2):
                        m = i * 2 + h
                        at = bass.ds(m * (U1 * P), U1 * P)
                        sp.wait_ge(group1_done, m + 1)
                        sp.dma_start(times[0:1, h, :], in_order["time_row"][:, at]).then_inc(edge_in[h], 16)
                        sp.dma_start(src_b[:, h, :], in_order["src_row"][0, at].partition_broadcast(P)).then_inc(edge_in[h], 16)
                        sp.dma_start(src_c[:, h, :], in_order["src_cols"][:, bass.ds(m * U1, U1)]).then_inc(edge_in[h], 16)
                    for h in range(2):
                        m = i * 2 + h
                        sp.wait_ge(sums1_out, m + 3)
                        sp.dma_start(partial1_v[:, bass.ds(m * W1G, W1G)], stage[:, h, :]).then_inc(stored1[h], 16)
                    for h in range(2):
                        sp.wait_ge(stored1[h], i * 16 + 16)
                        sp.sem_inc(stage1_free, 1)
                sp.wait_ge(added, 16 * U1 * 2 * TURNS1)
                with sp.Fori(0, NC) as c:
                    at = bass.ds(c * (C * H), C * H)
                    sp.wait_ge(parts_free, c + 1)
                    for u in range(U1):
                        sp.dma_start(parts_s[:, u, :], by_src_v[u][:, at]).then_inc(parts_in, 16)

            with sp.Fori(0, NC) as c:
                for u in range(U1):
                    sp.dma_start(by_src_v[u][:, bass.ds(c * (C * H), C * H)], zeros[:, 0:C * H]).then_inc(zeroed, 16)

            for k in range(PHASES):
                if k == 4:
                    layer1()
                if k == 6:
                    sp.wait_ge(own_ready, NC * 6 + 1)
                    sp.dma_start(edge_w[:], in_order["weight_cols"]).then_inc(weights_in, 16)
                store_table(k)
                with sp.Fori(0, TURNS) as i:
                    n = i + TURNS * k
                    for h in range(2):
                        sp.wait_ge(sums_out, n * 2 + h + 3)
                        sp.dma_start(partial_v[:, bass.ds((i * 2 + h) * (U * F), U * F)], stage[:, h, :]).then_inc(stored[h], 16)
                    for h in range(2):
                        sp.wait_ge(stored[h], n * 16 + 16)
                        sp.sem_inc(stage_free, 1)
            if layers == 2:
                layer1()
            sp.wait_ge(result_ready, 1)
            sp.dma_start(out, x_cur[:]).then_inc(result_out, 16)
            sp.wait_ge(result_out, 16)
            sp.wait_ge(inputs_in, 16 * len(LOADS))
            sp.wait_ge(zero_in, 32)
            sp.wait_ge(zeroed, 16 * NC * U1)
            sp.wait_ge(table_out, 16 * NC * PHASES)
            for h in range(2):
                sp.wait_ge(stored[h], 16 * TURNS * PHASES)

        @block.gpsimd
        def _(pool):
            nc.gpsimd.iota(iota_i[:], pattern=[[1, P]], base=0, channel_multiplier=0).then_inc(consts, 1)
            nc.gpsimd.iota(part_i[:], pattern=[[0, 1]], base=0, channel_multiplier=1).then_inc(consts, 1)
            nc.gpsimd.iota(tid_i[:], pattern=[[1, U]], base=0, channel_multiplier=U).then_inc(consts, 1)

            with if_unsorted(pool):
                pool.sem_inc(edge_free, 1)
                for d in range(2):
                    with pool.Fori(0, T) as t:
                        pool.wait_ge(rank_ready, t + (T * d + 1))
                        pool.sem_inc(pool_go, 1)
                        pool.indirect_dma_start(
                            out=moved[d], out_offset=bass.IndirectOffsetOnAxis(ap=move_idx, axis=0),
                            in_=moving, in_offset=None).then_inc(edge_moved, 16)
                        pool.wait_ge(edge_moved, t * 16 + (16 * T * d + 16))
                        pool.sem_inc(edge_free, 1)

            with pool.Fori(0, TURNS) as i:
                for h in range(2):
                    pool.wait_ge(kg_ready, i * 2 + h + 1)
                    pool.sem_inc(pool_go, 1)
                    for u in range(HI_POOL):
                        ins = nc.gpsimd.tensor_scalar(hot_hi[:, h, u], iota_h[:, 0:J], kg[:, h, U + u:U + u + 1], None, ALU.is_equal)
                    ins.then_inc(hi_ready, 1)

            def gather_edges(k):
                pool.wait_ge(table_out, 16 * NC * (k + 1))
                with pool.Fori(0, TURNS) as i:
                    for h in range(2):
                        pool.wait_ge(idx_ready, (i + TURNS * k) * 2 + h + 1)
                        pool.sem_inc(pool_go, 1)
                        for u in range(U):
                            pool.indirect_dma_start(
                                out=rows[:, h, u * F:(u + 1) * F], out_offset=None, in_=table,
                                in_offset=bass.IndirectOffsetOnAxis(ap=idx[:, h, u:u + 1], axis=0),
                            ).then_inc(rows_in[k // 3][h], 16)

            def add_carries(k):
                for h in range(2):
                    pool.wait_ge(stored[h], 16 * TURNS * (k + 1))
                pool.wait_ge(zero_in, 32)
                pool.wait_ge(zeroed, 16 * NC * U1)
                pool.wait_ge(carry_in, k + 1)
                for u in range(U):
                    pool.indirect_dma_start(
                        out=partial, out_offset=bass.IndirectOffsetOnAxis(ap=carry_idx[0:G, u:u + 1], axis=0),
                        in_=carry_rows[0:G, u * F:(u + 1) * F], in_offset=None, compute_op=ALU.add,
                    ).then_inc(carry_added, 16)
                pool.wait_ge(carry_added, 16 * U * (k + 1))

            def gather_nodes(k):
                with pool.Fori(0, CTURNS) as i:
                    for h in range(2):
                        pool.wait_ge(nidx_ready, (i + (CTURNS + 1) * k) * 2 + h + 1)
                        pool.sem_inc(pool_go, 1)
                        for c in range(C):
                            pool.indirect_dma_start(
                                out=agg[:, h, c * F:(c + 1) * F], out_offset=None, in_=partial,
                                in_offset=bass.IndirectOffsetOnAxis(ap=nidx[:, h, c:c + 1], axis=0),
                            ).then_inc(agg_in[h], 16)

            def layer1():
                def gather(m, h):
                    pool.wait_ge(idx1_ready, m + 1)
                    pool.sem_inc(pool_go, 1)
                    for source, target, first in ((table_s, rows_s, 0), (table_t, rows_t, U1)):
                        for u in range(U1):
                            pool.indirect_dma_start(
                                out=target[:, h, u * H:(u + 1) * H], out_offset=None, in_=source,
                                in_offset=bass.IndirectOffsetOnAxis(ap=idx[:, h, first + u:first + u + 1], axis=0),
                            ).then_inc(rows1_in[h], 16)

                def add(m, h, begun=True):
                    pool.wait_ge(sums1_out, m + 3)
                    pool.wait_ge(add_idx_ready, m + 1)
                    if begun:
                        pool.wait_ge(added, m * (16 * U1))
                        pool.sem_inc(added_free, 1)
                    for u in range(U1):
                        pool.indirect_dma_start(
                            out=by_src[u], out_offset=bass.IndirectOffsetOnAxis(ap=add_idx[:, h, u:u + 1], axis=0),
                            in_=merged[:, h, u * H:(u + 1) * H], in_offset=None, compute_op=ALU.add,
                            bounds_check=NPAD - 1, oob_is_err=False,
                        ).then_inc(added, 16)

                pool.wait_ge(st_out, 32 * NC)
                pool.sem_inc(added_free, 2)
                last = 2 * TURNS1 - 1
                gather(0, 0)
                gather(1, 1)
                add(0, 0, begun=False)
                with pool.Fori(0, TURNS1 - 1) as i:
                    gather(i * 2 + 2, 0)
                    add(i * 2 + 1, 1)
                    gather(i * 2 + 3, 1)
                    add(i * 2 + 2, 0)
                add(last, 1)
                for h in range(2):
                    pool.wait_ge(stored1[h], 16 * TURNS1)
                pool.wait_ge(carry1_in, 1)
                for u in range(U):
                    pool.indirect_dma_start(
                        out=partial1, out_offset=bass.IndirectOffsetOnAxis(ap=carry_idx[0:G, u:u + 1], axis=0),
                        in_=carry_rows1[0:G, u * H:(u + 1) * H], in_offset=None, compute_op=ALU.add,
                    ).then_inc(carry1_added, 16)
                pool.wait_ge(carry1_added, 16 * U)
                with pool.Fori(0, CTURNS) as i:
                    for h in range(2):
                        pool.wait_ge(nidx1_ready, i * 2 + h + 1)
                        pool.sem_inc(pool_go, 1)
                        for c in range(C):
                            pool.indirect_dma_start(
                                out=agg1[:, h, c * H:(c + 1) * H], out_offset=None, in_=partial1,
                                in_offset=bass.IndirectOffsetOnAxis(ap=nidx[:, h, c:c + 1], axis=0),
                            ).then_inc(agg1_in[h], 16)

            for k in range(PHASES):
                gather_edges(k)
                add_carries(k)
                gather_nodes(k)
                if k == 3 and layers > 1:
                    layer1()

        @block.tensor
        def _(pe):
            pe.wait_ge(order_summed, 1)
            pe.matmul(ps_last[0:1, 0, 0:1], out_of_order[0:G, 0:1], ones[0:G, 0:1], start=True, stop=True).then_inc(order_summed, 1)
            with if_unsorted(pe):
                for d in range(2):
                    pe.wait_ge(digit_zeroed, d + 1)
                    pe.matmul(ps_main[:, 0, 0:P], ones, digit_sum, start=True, stop=False, skip_group_check=True)
                    pe.sem_inc(digit_used, 1)
                    with pe.Fori(0, T) as t:
                        pe.wait_ge(digit_ready, t + (2 * T * d + 1))
                        pe.sem_inc(pe_go, 1)
                        pe.matmul(ps_main[:, 0, 0:P], ones, digit_hot, start=False, stop=False,
                                  skip_group_check=True).then_inc(digit_used, 1)
                    pe.matmul(ps_main[:, 0, 0:P], ones, digit_sum, start=False, stop=True,
                              skip_group_check=True).then_inc(digit_counted, 1)
                    with pe.Fori(0, T) as t:
                        pe.wait_ge(digit_ready, t + (2 * T * d + T + 1))
                        pe.sem_inc(pe_go, 1)
                        pe.matmul(ps_main[:, 1, 0:P], tri, digit_hot, start=True, stop=True)
                        pe.matmul(ps_main[:, 2, 0:P], ones, digit_hot, start=True, stop=True).then_inc(digit_counted, 1)

            def turn_rows(source, ready, n):
                pe.wait_ge(ready, n)
                for u in range(U):
                    ins = pe.transpose(ps_main[:, u // 4, (u % 4) * P:(u % 4) * P + G],
                                       source[:, u * P:(u + 1) * P], ident[0:G, 0:G])
                ins.then_inc(ranks_out, 1)

            turn_rows(row_rank, keys_ready, 1)
            pe.wait_ge(ranks_in, 4)
            turn_rows(row_val, keys_ready, 1)

            pe.wait_ge(hot_ready, 1)
            zero_lo, zero_hi = hot_zero[:, 0:P], hot_zero[:, 0:J]

            def clear(counts):
                pe.matmul(counts, zero_lo, zero_hi, start=True, stop=False, skip_group_check=True)

            def close(counts):
                return pe.matmul(counts, zero_lo, zero_hi, start=False, stop=True, skip_group_check=True)

            dst_counts, end_counts, src_counts = ps_out[:, 0, 0:J], ps_out[:, 1, 0:J], ps_last[:, 1, 0:J]
            clear(dst_counts)
            pe.sem_inc(hot_used, 2)
            with pe.Fori(0, TURNS) as i:
                for h in range(2):
                    pe.wait_ge(hot_ready, i * 2 + h + 2)
                    pe.wait_ge(hi_ready, i * 2 + h + 1)
                    pe.sem_inc(pe_go, 1)
                    for u in range(U):
                        ins = pe.matmul(dst_counts, hot_lo[:, h, u], hot_hi[:, h, u],
                                        start=False, stop=False, skip_group_check=True)
                    ins.then_inc(hot_used, 1)
            close(dst_counts).then_inc(counted, 1)

            pe.wait_ge(deg_ready, 1)
            pe.matmul(ps_last[:, 1, 0:J], tri[:], deg_dst[:], start=True, stop=True)
            pe.matmul(ps_last[:, 1, P:P + J], ones[:], deg_dst[:], start=True, stop=True).then_inc(cum_ready, 1)

            pe.sem_inc(group_done, 2)

            def sum_runs(k):
                if k == 0:
                    pe.wait_ge(deg_ready, 2)
                    clear(end_counts)
                    pe.sem_inc(count_used, 2)
                with pe.Fori(0, TURNS) as i:
                    for h in range(2):
                        n = i + TURNS * k
                        pe.wait_ge(rows_in[k // 3][h], (i + TURNS * (k % 3)) * (16 * U) + 16 * U)
                        pe.wait_ge(pick_ready, n * 2 + h + 1)
                        pe.wait_ge(sums_out, n * 2 + h + 1)
                        for u in range(U):
                            got = rows[:, h, u * F:(u + 1) * F]
                            pe.matmul(ps_main[:, h * 2 + u // 8, (u % 8) * F:(u % 8 + 1) * F], pick[:, h, u], got,
                                      start=True, stop=True)
                            ins = pe.matmul(ps_last[0:F, h, u:u + 1], got, pick[:, h, u, 0:1],
                                            start=True, stop=True)
                        ins.then_inc(group_done, 1)
                        if k == 0:
                            count_ends(n * 2, h)
                if k == 0:
                    close(end_counts).then_inc(counted_all, 1)

            def count_ends(m, h):
                pe.wait_ge(count_ready, m + h + 1)
                pe.sem_inc(pe_go, 1)
                for u in range(U):
                    ins = pe.matmul(end_counts, hot_end[:, h, u, 0:P], hot_end[:, h, u, P:P + J], start=False, stop=False,
                                    skip_group_check=True)
                ins.then_inc(count_used, 1)

            def turn_carries(k):
                pe.wait_ge(carry_ready, k + 1)
                for u in range(U):
                    ins = pe.transpose(ps_main[0:G, u // 8, (u % 8) * F:(u % 8 + 1) * F],
                                       tile_sum[0:F, u:T:U], ident[0:F, 0:F])
                ins.then_inc(carry_turned, 1)

            def transform_nodes(k):
                first, _, second = MATS[k]
                wide = first.shape[1]
                gin = KIND[k] == "gin"
                with pe.Fori(0, CTURNS) as i:
                    for h in range(2):
                        m = (i + CTURNS * TURNED.index(k)) * 2 + h + 1
                        pe.wait_ge(z_ready, m)
                        pe.sem_inc(pe_go, 1)
                        for c in range(C):
                            ins = pe.transpose(ps_main[0:F, c // 4, (c % 4) * P:(c % 4 + 1) * P],
                                               z[:, h, c * F:(c + 1) * F], ident[:])
                        ins.then_inc(z_turned, 1)
                        pe.wait_ge(zT_ready, m)
                        pe.sem_inc(pe_go, 1)
                        for b in range(2):
                            ins = pe.matmul(ps_main[0:wide, 2 + b, 0:CW], first, zT[:, b * CW:(b + 1) * CW],
                                            start=True, stop=True)
                        ins.then_inc(h_done, 1)
                        if gin:
                            pe.wait_ge(hT_ready, m + HT_EXTRA[k])
                            pe.sem_inc(pe_go, 1)
                            continue
                        if KIND[k] == "wide_skip":
                            pe.wait_ge(skip_ready, i * 2 + h + 1)
                            pe.sem_inc(pe_go, 1)
                        else:
                            pe.wait_ge(hT_ready, m + HT_EXTRA[k])
                            pe.sem_inc(pe_go, 1)
                        for c in range(C):
                            ins = pe.matmul(ps_out[:, 0, c * F:(c + 1) * F], hT[0:wide, c * P:(c + 1) * P], second,
                                            start=True, stop=True)
                        ins.then_inc(o_done, 1)
                if gin:
                    with pe.Fori(0, NC) as c:
                        pe.wait_ge(hT_ready, c + (NC * (TURNED.index(k) + 1) + HT_EXTRA[k] + 1))
                        pe.wait_ge(o_taken, c + (NC * (k - 6) + 1))
                        pe.sem_inc(pe_go, 1)
                        for t in range(C):
                            ins = pe.matmul(ps_out[:, 0, t * F:(t + 1) * F], hT[0:F, t * P:(t + 1) * P], second,
                                            start=True, stop=True)
                        ins.then_inc(o_done, 1)

            def layer1():
                with pe.Fori(0, CTURNS) as i:
                    for h in range(2):
                        m = i * 2 + h + 1
                        pe.wait_ge(x_ready, m)
                        pe.sem_inc(pe_go, 1)
                        for c in range(C):
                            ins = pe.transpose(ps_out[0:F, c // 4, (c % 4) * P:(c % 4 + 1) * P],
                                               z[:, h, c * F:(c + 1) * F], ident[:])
                        ins.then_inc(x_turned, 1)
                        pe.wait_ge(xT_ready, m)
                        pe.sem_inc(pe_go, 1)
                        for c in range(C):
                            ins = pe.matmul(ps_main[:, c // 2, (c % 2) * 2 * H:(c % 2 + 1) * 2 * H],
                                            zT[:, c * P:(c + 1) * P], W["eW1"][0].rearrange("k s m -> k (s m)"), start=True, stop=True)
                        ins.then_inc(st_done, 1)
                pe.wait_ge(st_ready, NC)
                clear(src_counts)
                pe.sem_inc(group1_done, 2)
                with pe.Fori(0, TURNS1) as i:
                    for h in range(2):
                        m = i * 2 + h
                        pe.wait_ge(edge_in[h], i * 48 + 48)
                        pe.wait_ge(t_ready, m + 1)
                        pe.sem_inc(pe_go, 1)
                        for u in range(U1):
                            ins = pe.matmul(ps_out[:, u // 4, (u % 4) * H:(u % 4 + 1) * H], times[:, h, u * P:(u + 1) * P],
                                            W["eWt"][0], start=True, stop=True)
                        ins.then_inc(t_done, 1)
                        pe.wait_ge(hid_ready, m + 1)
                        pe.wait_ge(pick1_ready, m + 1)
                        pe.wait_ge(sums1_out, m + 2)
                        pe.sem_inc(pe_go, 1)
                        for u in range(U1):
                            got = hid[:, h, u * H:(u + 1) * H]
                            at = slice((u % 4) * H, (u % 4 + 1) * H)
                            pe.matmul(ps_main[:, u // 4, at], pick1[:, h, u], got, start=True, stop=True)
                            pe.matmul(ps_main[:, 2 + u // 4, at], same[:, h, u], got, start=True, stop=True)
                            pe.matmul(ps_last[:, 0, u:u + 1], got, pick1[:, h, u, 0:1], start=True, stop=True)
                            ins = pe.matmul(src_counts, hot_src[:, h, u, 0:P], hot_src[:, h, u, P:P + J],
                                            start=False, stop=False, skip_group_check=True)
                        ins.then_inc(group1_done, 1)
                close(src_counts).then_inc(src_counted, 1)
                pe.wait_ge(carry1_ready, 1)
                for u in range(U):
                    ins = pe.transpose(ps_main[0:G, u // 4, (u % 4) * P:(u % 4 + 1) * P], tile_sum[:, u:T:U], ident[:])
                ins.then_inc(carry1_turned, 1)
                pe.wait_ge(carry1_in, 1)
                with pe.Fori(0, CTURNS) as i:
                    for h in range(2):
                        m = i * 2 + h + 1
                        pe.wait_ge(parts_in, m * (16 * U1))
                        pe.wait_ge(agg1_in[h], i * (16 * C) + 16 * C)
                        pe.sem_inc(pe_go, 1)
                        for c in range(C):
                            at = slice((c % 4) * P, (c % 4 + 1) * P)
                            for u in range(U1):
                                pe.matmul(ps_main[:, c // 4, at], parts_s[:, u, c * H:(c + 1) * H], ident[:],
                                          start=(u == 0), stop=(u == U1 - 1))
                            ins = pe.transpose(ps_main[:, 2 + c // 4, at], agg1[:, h, c * H:(c + 1) * H], ident[:])
                        ins.then_inc(sd_turned, 1)
                        pe.wait_ge(sd_ready, m)
                        pe.wait_ge(o1_taken, m)
                        pe.sem_inc(pe_go, 1)
                        for c in range(C):
                            at = slice(c * F, (c + 1) * F)
                            pe.matmul(ps_out[:, 0, at], hT[:, c * P:(c + 1) * P], W["eW2"][0][:, 0:F], start=True, stop=False)
                            ins = pe.matmul(ps_out[:, 0, at], dT[:, c * P:(c + 1) * P], W["eW2"][0][:, F:2 * F],
                                            start=False, stop=True)
                        ins.then_inc(o1_done, 1)

            for k in range(PHASES):
                sum_runs(k)
                turn_carries(k)
                if k in MATS:
                    transform_nodes(k)
                if k == 3 and layers > 1:
                    layer1()

        @block.scalar
        def _(act):
            with if_unsorted(act):
                act.sem_inc(act_go, 1)

            def take_rows(target, n):
                act.wait_ge(ranks_out, n)
                for b in range(4):
                    ins = nc.scalar.copy(target(b), ps_main[:, b].rearrange("p (u g) -> p u g", u=4)[:, :, 0:G])
                ins.then_inc(ranks_in, 4)

            take_rows(lambda b: rank[:].rearrange("p (g u) -> p u g", u=U)[:, 4 * b:4 * b + 4], 1)
            take_rows(lambda b: keys[:, :, 2].rearrange("p g u -> p u g")[:, 4 * b:4 * b + 4], 2)

            act.wait_ge(root_ready, 1)
            nc.scalar.activation(dinv[:], small[:, 0], ACT.Sqrt).then_inc(root_in, 1)
            act.sem_inc(sums_out, 2)

            def take_sums(k):
                with act.Fori(0, TURNS) as i:
                    for h in range(2):
                        m = (i + TURNS * k) * 2 + h
                        act.wait_ge(group_done, m + 3)
                        act.wait_ge(stage_free, m + 1)
                        act.sem_inc(act_go, 1)
                        for b in range(2):
                            nc.scalar.copy(stage[:, h, b * 512:(b + 1) * 512], ps_main[:, h * 2 + b])
                        nc.scalar.copy(tile_sum[0:F, bass.ds((i * 2 + h) * U, U)],
                                       ps_last[0:F, h, 0:U]).then_inc(sums_out, 1)

            def take_carries(k):
                act.wait_ge(carry_turned, k + 1)
                for b in range(2):
                    ins = nc.scalar.copy(carry_rows[0:G, b * 512:(b + 1) * 512], ps_main[0:G, b])
                ins.then_inc(carry_in, 1)

            def bend_nodes(k):
                first, bias, _ = MATS[k]
                wide = first.shape[1]
                kind = KIND[k]
                bend = ACT.Identity if kind in ("conv_out", "gin") else ACT.Relu
                with act.Fori(0, CTURNS) as i:
                    for h in range(2):
                        m = (i + CTURNS * TURNED.index(k)) * 2 + h + 1
                        act.wait_ge(z_turned, m)
                        act.sem_inc(act_go, 1)
                        nc.scalar.copy(zT[:, 0:512], ps_main[0:F, 0])
                        nc.scalar.copy(zT[:, 512:C * P], ps_main[0:F, 1, 0:C * P - 512]).then_inc(zT_ready, 1)
                        act.wait_ge(h_done, m)
                        act.sem_inc(act_go, 1)
                        if kind in ("gin", "wide"):
                            for b in range(2):
                                ins = nc.scalar.activation(big[0:wide, bass.ds((i * 2 + h) * (C * P) + b * CW, CW)],
                                                           ps_main[0:wide, 2 + b, 0:CW], bend, bias=bias)
                        if kind != "gin":
                            for b in range(2):
                                ins = nc.scalar.activation(hT[0:wide, b * CW:(b + 1) * CW],
                                                           ps_main[0:wide, 2 + b, 0:CW], bend, bias=bias)
                        ins.then_inc(hT_ready, 1)
                if kind == "gin":
                    act.wait_ge(bn_var, k - 5)
                    nc.scalar.activation(bn[:, 3:4], bn[:, 2:3], ACT.Sqrt).then_inc(bn_root, 1)
                    act.wait_ge(bn_ready, k - 5)
                    with act.Fori(0, NC) as c:
                        act.wait_ge(o_done, c + NC * TURNED.index(k))
                        act.sem_inc(act_go, 1)
                        nc.scalar.activation(hT[0:F, :], big[0:F, bass.ds(c * (C * P), C * P)], ACT.Relu,
                                             bias=bn[:, 5:6], scale=bn[:, 4:5]).then_inc(hT_ready, 1)

            def root(n):
                act.wait_ge(ln_var, n)
                nc.scalar.activation(small[:, 3], small[:, 2], ACT.Sqrt).then_inc(ln_root, 1)

            def layer1():
                with act.Fori(0, CTURNS) as i:
                    for h in range(2):
                        m = i * 2 + h + 1
                        act.wait_ge(x_turned, m)
                        act.sem_inc(act_go, 1)
                        nc.scalar.copy(zT[:, 0:512], ps_out[0:F, 0])
                        nc.scalar.copy(zT[:, 512:C * P], ps_out[0:F, 1, 0:C * P - 512]).then_inc(xT_ready, 1)
                act.wait_ge(st_ready, NC)
                act.sem_inc(t_ready, 1)
                act.sem_inc(sums1_out, 2)
                with act.Fori(0, TURNS1) as i:
                    for h in range(2):
                        m = i * 2 + h
                        act.wait_ge(t_done, m + 1)
                        act.wait_ge(arg_ready, m + 1)
                        act.sem_inc(act_go, 1)
                        for b in range(2):
                            ins = nc.scalar.activation(t_emb[:, b * 512:(b + 1) * 512], ps_out[:, b], ACT.Silu)
                        ins.then_inc(t_ready, 1)
                        act.wait_ge(arg_ready, m + 2)
                        act.sem_inc(act_go, 1)
                        nc.scalar.activation(hid[:, h], arg, ACT.Silu).then_inc(hid_ready, 1)
                        act.wait_ge(group1_done, m + 3)
                        act.wait_ge(stage1_free, m + 1)
                        act.wait_ge(added_free, m + 1)
                        act.sem_inc(act_go, 1)
                        for b in range(2):
                            nc.scalar.copy(stage[:, h, b * 512:(b + 1) * 512], ps_main[:, b])
                            nc.scalar.copy(merged[:, h, b * 512:(b + 1) * 512], ps_main[:, 2 + b])
                        nc.scalar.copy(tile_sum[:, bass.ds(m * U1, U1)], ps_last[:, 0, 0:U1]).then_inc(sums1_out, 1)
                act.wait_ge(carry1_turned, 1)
                for b in range(4):
                    ins = nc.scalar.copy(carry_rows1[0:G, b * 512:(b + 1) * 512], ps_main[0:G, b])
                ins.then_inc(carry1_in, 1)
                act.wait_ge(added, 16 * U1 * 2 * TURNS1)
                act.sem_inc(parts_free, 1)
                with act.Fori(0, NC) as c:
                    act.wait_ge(sd_turned, c + 1)
                    act.sem_inc(parts_free, 1)
                    for b, (start, end) in enumerate(((0, 512), (512, C * P))):
                        nc.scalar.copy(hT[:, start:end], ps_main[:, b, 0:end - start])
                        ins = nc.scalar.copy(dT[:, start:end], ps_main[:, 2 + b, 0:end - start])
                    ins.then_inc(sd_ready, 1)

            for k in range(PHASES):
                take_sums(k)
                take_carries(k)
                if k in MATS:
                    bend_nodes(k)
                if k in LN_AFTER:
                    root(NORM[k])
                if k == 3 and layers > 1:
                    layer1()
                    root(2)

        @block.vector
        def _(v):
            tt, ts = nc.vector.tensor_tensor, nc.vector.tensor_scalar
            step = v_step

            def settle():
                v.wait_ge(step.sem, step.value())

            def per_node(t, j0, n=C):
                return t[:, bass.ds(j0, n)].unsqueeze(2).to_broadcast([P, n, F])

            def split(t):
                return t.rearrange("p (j f) -> p j f", f=F)

            def sort_edges():
                def then(ins):
                    s_step.up(ins)
                    v.wait_ge(s_step.sem, s_step.value())

                def tile_hot(t):
                    v.wait_ge(digit_used, s_used[0])
                    v.sem_inc(v_go, 1)
                    then(nc.vector.tensor_copy(digit_col, digit[:, bass.ds(t, 1)]))
                    ts(digit_hot, iota_f, digit_col, None, ALU.is_equal).then_inc(digit_ready, 1)

                v.wait_ge(cols_in, 32)
                for q, source in enumerate((src_i, dst_i, edge_w, cont)):
                    then(nc.vector.tensor_copy(edges[:, :, q], source))
                for d in range(2):
                    then(nc.vector.tensor_copy(col_i, edges[:, :, 1]))
                    then(ts(col_i, col_i, *((P - 1, None, ALU.bitwise_and) if d == 0 else (7, None, ALU.logical_shift_right))))
                    then(nc.vector.tensor_copy(digit, col_i))
                    then(nc.vector.memset(digit_sum, 0.0))
                    v.sem_inc(digit_zeroed, 1)
                    used = (T + 1) * d
                    with v.Fori(0, T) as t:
                        s_step.enter(t, 1)
                        s_used = [t + (used + 1)]
                        tile_hot(t)
                        s_step.leave(T)
                    v.wait_ge(digit_counted, (T + 1) * d + 1)
                    then(nc.vector.tensor_copy(digit_sum, ps_main[:, 0, 0:P]))
                    then(nc.vector.memset(digit_tmp, 1.0))
                    then(nc.vector.tensor_tensor_scan(digit_base, digit_tmp, digit_sum, 0.0, ALU.mult, ALU.add))
                    then(tt(digit_base, digit_base, digit_sum, ALU.subtract))
                    then(ts(digit_base, digit_base, -1.0, None, ALU.add))
                    with v.Fori(0, T) as t:
                        s_step.enter(t, 5)
                        s_used = [used + T + 1]
                        tile_hot(t)
                        v.wait_ge(digit_counted, t + ((T + 1) * d + 2))
                        v.sem_inc(v_go, 1)
                        then(tt(digit_tmp, digit_base, ps_main[:, 1, 0:P], ALU.add))
                        then(nc.vector.tensor_tensor_reduce(digit_sum, digit_tmp, digit_hot, 1.0, 0.0, ALU.mult, ALU.add, digit_rank))
                        then(tt(digit_base, digit_base, ps_main[:, 2, 0:P], ALU.add))
                        v.wait_ge(edge_free, t + (T * d + 1))
                        v.sem_inc(v_go, 1)
                        then(nc.vector.tensor_copy(moving, edges[:, bass.ds(t, 1)].rearrange("p t q -> p (t q)")))
                        nc.vector.tensor_copy(move_idx, digit_rank).then_inc(rank_ready, 1)
                        v.wait_ge(rank_ready, t + (T * d + 1))
                        v.sem_inc(v_go, 1)
                        s_step.leave(T)
                    v.wait_ge(edges_in, 16 * (d + 1))
                for q, target in enumerate((src_i, dst_i, edge_w, cont)):
                    then(nc.vector.tensor_copy(target, edges[:, :, q]))
                v.sem_inc(unpacked, 1)
                v.wait_ge(again_in, 80)

            step.up(nc.vector.memset(zeros[:], 0.0))
            step.up(nc.vector.memset(hot_zero[:], 0.0))
            step.up(nc.vector.memset(ones[:], 1.0))
            step.up(nc.vector.memset(node_idx[:, J:J + 2 * C], 0))
            settle()
            nc.vector.memset(row_chg, 0.0).then_inc(zero_made, 1)
            v.wait_ge(consts, 3)
            step.up(nc.vector.tensor_copy(iota_f[:], iota_i[:]))
            step.up(nc.vector.tensor_copy(iota_h[:], iota_i[:]))
            step.up(nc.vector.tensor_copy(part_f[:], part_i[:]))
            settle()
            step.up(ts(ident[:], iota_f[:], part_f[:], None, ALU.is_equal))
            step.up(ts(tri[:], iota_f[:], part_f[:], None, ALU.is_ge))
            step.up(ts(low[:], iota_f[:], part_f[:], None, ALU.is_lt))
            v.wait_ge(inputs_in, 16 * len(LOADS))
            v.wait_ge(zero_made, 1)

            step.up(nc.vector.memset(out_of_order, 0.0))
            settle()
            step.up(tt(row_chg[:, 1:U * P], row_dst[:, 1:U * P], row_dst[:, 0:U * P - 1], ALU.is_lt))
            step.up(tt(out_of_order[0:G - 1, 1:2], next_first[0:G - 1, U - 1:U], row_dst[0:G - 1, U * P - 1:U * P], ALU.is_lt))
            settle()
            step.up(nc.vector.tensor_reduce(out_of_order[0:G, 0:1], row_chg, AX.X, ALU.add))
            settle()
            tt(out_of_order[:, 0:1], out_of_order[:, 0:1], out_of_order[:, 1:2], ALU.add).then_inc(order_summed, 1)
            v.wait_ge(order_summed, 2)
            ts(sort_flag, ps_last[0:1, 0, 0:1], 1.0, None, ALU.min).then_inc(flag_ready, 1)
            with if_unsorted(v):
                sort_edges()
            step.up(nc.vector.memset(row_chg, 0.0))
            settle()

            def tiles(t):
                return t.rearrange("g (u e) -> g u e", u=U)

            chg, pre = tiles(row_chg), tiles(row_pre)
            step.up(tt(chg[:, :, 1:P], tiles(row_dst)[:, :, 1:P], tiles(row_dst)[:, :, 0:P - 1], ALU.not_equal))
            step.up(nc.vector.memset(row_rank, 1.0))
            settle()
            step.up(nc.vector.memset(tiles(row_rank)[:, :, 0:1], 0.0))
            settle()
            step.up(nc.vector.tensor_tensor_scan(row_pre, row_rank, row_chg, 0.0, ALU.mult, ALU.add))
            settle()
            in_tile = pre[:, :, P - 1:P]
            step.up(tt(tiles(row_rank), in_tile.to_broadcast([G, U, P]), pre, ALU.subtract))
            step.up(nc.vector.tensor_copy(tiles(row_val)[:, :, 0:P - 1], chg[:, :, 1:P]))
            step.up(tt(tiles(row_val)[:, :, P - 1], tiles(row_dst)[:, :, P - 1], next_first[0:G], ALU.not_equal))
            step.up(nc.vector.tensor_copy(small[0:G, 1, 0:U], tid_i[0:G, :]))
            settle()
            step.up(nc.vector.scalar_tensor_tensor(carry_idx[0:G, :], pre[:, :, P - 1], float(T), small[0:G, 1, 0:U],
                                                   ALU.mult, ALU.add))
            nc.vector.scalar_tensor_tensor(row_val, row_rank, 1.0, row_val, ALU.add, ALU.mult).then_inc(keys_ready, 1)

            def parts(source, lo, hi):
                step.up(ts(col_i, source, P - 1, None, ALU.bitwise_and))
                settle()
                step.up(nc.vector.tensor_copy(keys[:, :, lo], col_i.rearrange("p (g u) -> p g u", u=U)))
                settle()
                step.up(ts(col_i, source, 7, None, ALU.logical_shift_right))
                settle()
                step.up(nc.vector.tensor_copy(keys[:, :, hi], col_i.rearrange("p (g u) -> p g u", u=U)))
                settle()

            parts(dst_i, 0, 1)
            parts(src_i, 3, 4)
            step.up(nc.vector.scalar_tensor_tensor(src_idx[:].rearrange("p (g u) -> p g u", u=U), keys[:, :, 3],
                                                   float(J), keys[:, :, 4], ALU.mult, ALU.add))
            step.up(nc.vector.scalar_tensor_tensor(dst_idx.rearrange("p (g u) -> p g u", u=U), keys[:, :, 0],
                                                   float(J), keys[:, :, 1], ALU.mult, ALU.add))
            first_i = first_b[:].bitcast(I32)
            last_i = last_b.bitcast(I32)
            step.up(nc.vector.memset(cont[:, 0:1], 0.0))
            step.up(tt(cont[:, 1:T], first_i[:, 1:T], last_i[:, 0:T - 1], ALU.is_equal))
            step.up(tt(run_sum[:], first_i, last_i, ALU.is_equal))
            settle()
            step.up(tt(chained[:], run_sum[:], cont[:], ALU.mult))

            settle()
            v.sem_inc(hot_ready, 1)
            v.wait_ge(ranks_in, 8)
            with v.Fori(0, TURNS) as i:
                for h in range(2):
                    v.wait_ge(hot_used, i * 2 + h + 1)
                    v.sem_inc(v_go, 1)
                    nc.vector.tensor_copy(kg[:, h, 0:2 * U], big[:, bass.ds((i * 2 + h) * (5 * U), 2 * U)]).then_inc(kg_ready, 1)
                    v.wait_ge(kg_ready, i * 2 + h + 1)
                    v.sem_inc(v_go, 1)
                    for u in range(U):
                        ins = ts(hot_lo[:, h, u], iota_h, kg[:, h, u:u + 1], None, ALU.is_equal)
                    for u in range(HI_POOL, U):
                        ins = ts(hot_hi[:, h, u], iota_h[:, 0:J], kg[:, h, U + u:U + u + 1], None, ALU.is_equal)
                    ins.then_inc(hot_ready, 1)

            v.wait_ge(counted, 1)
            step.up(ts(small[:, 0], ps_out[:, 0, 0:J], 1.0, None, ALU.add))
            step.up(nc.vector.tensor_copy(deg_dst[:], ps_out[:, 0, 0:J]))
            settle()
            v.sem_inc(deg_ready, 2)
            v.sem_inc(root_ready, 1)
            v.wait_ge(cum_ready, 1)
            step.up(nc.vector.memset(small[:, 2], 1.0))
            step.up(nc.vector.tensor_copy(small[:, 4], ps_last[:, 1, P:P + J]))
            settle()
            step.up(nc.vector.tensor_tensor_scan(small[:, 3], small[:, 2], small[:, 4], 0.0, ALU.mult, ALU.add))
            settle()
            step.up(tt(small[:, 3], small[:, 3], small[:, 4], ALU.subtract))
            settle()
            step.up(tt(small[:, 3], small[:, 3], ps_last[:, 1, 0:J], ALU.add))
            settle()
            cum_i = small[:, 5].bitcast(I32)
            tile_i = small[:, 6].bitcast(I32)
            step.up(ts(cum_i, small[:, 3], -1.0, 0.0, ALU.add, ALU.max))
            settle()
            step.up(ts(tile_i, cum_i, 7, None, ALU.logical_shift_right))
            settle()
            step.up(nc.vector.tensor_copy(small[:, 4], tile_i))

            v.wait_ge(root_in, 1)
            settle()
            step.up(nc.vector.reciprocal(small[:, 7], dinv[:]))
            settle()
            step.up(nc.vector.tensor_copy(dinv[:], small[:, 7]))
            settle()

            def place_sums():
                v.wait_ge(counted_all, 1)
                step.up(nc.vector.tensor_copy(small[:, 1], ps_out[:, 1, 0:J]))
                settle()
                step.up(ts(small[:, 2], small[:, 1], 0.0, None, ALU.is_gt))
                step.up(nc.vector.scalar_tensor_tensor(small[:, 3], small[:, 1], float(T), small[:, 4], ALU.mult, ALU.add))
                settle()
                step.up(ts(small[:, 5], small[:, 3], float(-T - ZERO_ROW), None, ALU.add))
                settle()
                step.up(tt(small[:, 6], small[:, 5], small[:, 2], ALU.mult))
                settle()
                step.up(ts(node_idx[:, 0:J], small[:, 6], float(ZERO_ROW), None, ALU.add))
                settle()

            def make_table(scaled):
                if scaled:
                    tt(split(own[:]), split(x_cur[:]), per_node(dinv, 0, J), ALU.mult).then_inc(own_ready, NC)
                else:
                    nc.vector.tensor_copy(own[:], x_cur[:]).then_inc(own_ready, NC)

            def count_hot(i, h):
                m = i * 2 + h
                step.up(nc.vector.tensor_copy(kg[:, h, 0:3 * U], big[:, bass.ds(m * (5 * U), 3 * U)]))
                settle()
                v.wait_ge(count_used, m + 1)
                v.sem_inc(v_go, 1)
                for u in range(U):
                    lo, hi, end = (kg[:, h, q * U + u:q * U + u + 1] for q in range(3))
                    ts(hot_end[:, h, u, 0:P], iota_h, lo, None, ALU.is_equal)
                    ins = ts(hot_end[:, h, u, P:P + J], iota_h[:, 0:J], hi, end, ALU.is_equal, ALU.mult)
                ins.then_inc(count_ready, 1)

            def pick_slots(k, weighted):
                with v.Fori(0, TURNS) as i:
                    step.enter(i, 6 if k == 0 else 4)
                    for h in range(2):
                        m = (i + TURNS * k) * 2 + h
                        at = bass.ds((i * 2 + h) * U, U)
                        v.wait_ge(group_done, m + 1)
                        v.sem_inc(v_go, 1)
                        nc.vector.tensor_copy(idx[:, h], src_idx[:, at]).then_inc(idx_ready, 1)
                        step.up(nc.vector.tensor_copy(w_g[:, h], (edge_w if weighted else rank)[:, at]))
                        step.up(nc.vector.tensor_copy(rank_g[:, h], rank[:, at]))
                        settle()
                        v.sem_inc(v_go, 1)
                        for u in range(U):
                            if weighted:
                                ins = ts(pick[:, h, u], iota_f[:], rank_g[:, h, u:u + 1], w_g[:, h, u:u + 1],
                                         ALU.is_equal, ALU.mult)
                            else:
                                ins = ts(pick[:, h, u], iota_f[:], rank_g[:, h, u:u + 1], None, ALU.is_equal)
                        ins.then_inc(pick_ready, 1)
                        if k == 0:
                            count_hot(i, h)
                    step.leave(TURNS)

            def carry_runs(k):
                v.wait_ge(sums_out, 2 * TURNS * (k + 1) + 2)
                step.up(nc.vector.tensor_tensor_scan(run_sum[0:F], chained[0:F], tile_sum[0:F], 0.0, ALU.mult, ALU.add))
                settle()
                step.up(nc.vector.memset(tile_sum[0:F, 0:1], 0.0))
                step.up(tt(tile_sum[0:F, 1:T], run_sum[0:F, 0:T - 1], cont[0:F, 1:T], ALU.mult))
                settle()
                v.sem_inc(carry_ready, 1)

            def finish_nodes(k):
                kind = KIND[k]
                per = {"wide": 1, "wide_skip": 1, "narrow": 3, "residual": 5, "conv": 1, "conv_out": 3, "gin": 0}[kind]
                for h in range(2):
                    nc.vector.tensor_copy(nidx[:, h], node_idx[:, h * C:(h + 1) * C]).then_inc(nidx_ready, 1)
                with v.Fori(0, CTURNS) as i:
                    step.enter(i, 2 * per)
                    for h in range(2):
                        c = i * 2 + h
                        chunk = bass.ds(c * (C * F), C * F)
                        if kind == "narrow":
                            v.wait_ge(own_ready, c + NC * (k + 1))
                        elif kind in ("residual", "conv_out"):
                            settle()
                        v.wait_ge(agg_in[h], (i + CTURNS * k) * (16 * C) + 16 * C)
                        v.sem_inc(v_go, 1)
                        if kind == "gin":
                            v.wait_ge(z_turned, c + (NC * TURNED.index(k) - 1))
                            v.sem_inc(v_go, 1)
                            tt(z[:, h], agg[:, h], own[:, chunk], ALU.add).then_inc(z_ready, 1)
                        else:
                            step.up(tt(tmp[:], agg[:, h], own[:, chunk], ALU.add))
                            settle()
                            v.sem_inc(v_go, 1)
                            ins = tt(split(z[:, h]), split(tmp[:]), per_node(dinv, c * C), ALU.mult)
                            if k in MATS:
                                ins.then_inc(z_ready, 1)
                            else:
                                step.up(ins)
                        nc.vector.tensor_copy(nidx[:, h], node_idx[:, bass.ds(c * C + 2 * C, C)]).then_inc(nidx_ready, 1)
                        if kind in ("narrow", "residual"):
                            bias = (W["b2"] if kind == "narrow" else W["b4"])[0][:]
                            settle()
                            v.sem_inc(v_go, 1)
                            step.up(tt(split(tmp[:]), split(z[:, h]), bias.unsqueeze(1).to_broadcast([P, C, F]), ALU.add))
                            settle()
                            v.sem_inc(v_go, 1)
                            if kind == "narrow":
                                nc.vector.scalar_tensor_tensor(split(own[:, chunk]), split(tmp[:]), 0.0,
                                                               per_node(dinv, c * C), ALU.max, ALU.mult).then_inc(own_ready, 1)
                            else:
                                step.up(nc.vector.scalar_tensor_tensor(z[:, h], tmp[:], 0.0, x_cur[:, chunk],
                                                                       ALU.max, ALU.add))
                                settle()
                                v.sem_inc(v_go, 1)
                                step.up(tt(x_cur[:, chunk], z[:, h], x_cur[:, chunk], ALU.add))
                            continue
                        m = (i + CTURNS * TURNED.index(k)) * 2 + h + 1
                        if kind == "gin":
                            continue
                        if kind == "wide_skip":
                            v.wait_ge(hT_ready, m + HT_EXTRA[k])
                            v.sem_inc(v_go, 1)
                            tt(hT[:], hT[:], big[:, bass.ds(c * (C * P), C * P)], ALU.add).then_inc(skip_ready, 1)
                        v.wait_ge(o_done, m + O_EXTRA[k])
                        v.sem_inc(v_go, 1)
                        product = ps_out[:, 0, 0:C * F]
                        if kind == "conv_out":
                            step.up(tt(split(tmp[:]), split(product), W["cbl"][0][:].unsqueeze(1).to_broadcast([P, C, F]), ALU.add))
                            settle()
                            v.sem_inc(v_go, 1)
                            step.up(tt(x_cur[:, chunk], tmp[:], x_cur[:, chunk], ALU.add))
                        else:
                            tt(split(own[:, chunk]), split(product), per_node(dinv, c * C), ALU.mult).then_inc(own_ready, 1)
                    step.leave(CTURNS)

            def norm_hidden(k):
                l = k - 6
                v.wait_ge(hT_ready, NC * (TURNED.index(k) + 1) + HT_EXTRA[k])
                for s in range(BN_PARTS):
                    ins = nc.vector.bn_stats(stats[:, s * 6:(s + 1) * 6], big[0:F, s * BN_LEN:(s + 1) * BN_LEN])
                step.up(ins)
                settle()
                step.up(nc.vector.bn_aggr(bn[:, 0:2], stats[:]))
                settle()
                ts(bn[:, 2:3], bn[:, 1:2], BN_EPS, None, ALU.add).then_inc(bn_var, 1)
                v.wait_ge(bn_root, l + 1)
                step.up(nc.vector.reciprocal(bn[:, 6:7], bn[:, 3:4]))
                settle()
                step.up(tt(bn[:, 4:5], bn[:, 6:7], W["gg"][0][:, l:l + 1], ALU.mult))
                settle()
                step.up(tt(bn[:, 7:8], bn[:, 0:1], bn[:, 4:5], ALU.mult))
                settle()
                tt(bn[:, 5:6], W["gbe"][0][:, l:l + 1], bn[:, 7:8], ALU.subtract).then_inc(bn_ready, 1)
                last = k == PHASES - 1
                with v.Fori(0, NC) as c:
                    step.enter(c, 1 if last else 0)
                    chunk = bass.ds(c * (C * F), C * F)
                    if last:
                        settle()
                    else:
                        v.wait_ge(own_ready, c + NC * (k + 1))
                    v.wait_ge(o_done, c + (NC * TURNED.index(k) + 1))
                    v.sem_inc(v_go, 1)
                    tt(split(tmp[:]), split(ps_out[:, 0, 0:C * F]), W["gb2"][0][:, l * F:(l + 1) * F].unsqueeze(1)
                       .to_broadcast([P, C, F]), ALU.add).then_inc(o_taken, 1)
                    v.wait_ge(o_taken, c + (NC * l + 2))
                    v.sem_inc(v_go, 1)
                    if last:
                        step.up(nc.vector.scalar_tensor_tensor(x_cur[:, chunk], tmp[:], 0.0, x_cur[:, chunk],
                                                               ALU.max, ALU.add))
                    else:
                        ts(own[:, chunk], tmp[:], 0.0, None, ALU.max).then_inc(own_ready, 1)
                    step.leave(NC)

            def norm_layer(last):
                xs, cs = split(x_cur[:]), split(own[:])
                settle()
                step.up(nc.vector.tensor_reduce(small[:, 0], xs, AX.X, ALU.add))
                settle()
                step.up(ts(small[:, 1], small[:, 0], 1.0 / F, None, ALU.mult))
                settle()
                step.up(tt(cs, xs, per_node(small[:, 1], 0, J), ALU.subtract))
                settle()
                step.up(tt(xs, cs, cs, ALU.mult))
                settle()
                step.up(nc.vector.tensor_reduce(small[:, 0], xs, AX.X, ALU.add))
                settle()
                ts(small[:, 2], small[:, 0], 1.0 / F, LN_EPS, ALU.mult, ALU.add).then_inc(ln_var, 1)
                norm_layer.n += 1
                v.wait_ge(ln_root, norm_layer.n)
                step.up(nc.vector.reciprocal(small[:, 4], small[:, 3]))
                settle()
                ins = tt(xs, cs, per_node(small[:, 4], 0, J), ALU.mult)
                if last:
                    ins.then_inc(result_ready, 1)
                else:
                    step.up(ins)
                    settle()
            norm_layer.n = 0

            def layer1():
                def spread(t, n=C):
                    return t.unsqueeze(1).to_broadcast([P, n, t.shape[1]])

                def settled():
                    settle()
                    v.sem_inc(v_go, 1)

                step.up(nc.vector.memset(times[:], 1.0))
                with v.Fori(0, CTURNS) as i:
                    for h in range(2):
                        c = i * 2 + h
                        nc.vector.tensor_copy(z[:, h], x_cur[:, bass.ds(c * (C * F), C * F)]).then_inc(x_ready, 1)
                        v.wait_ge(st_done, c + 1)
                        v.sem_inc(v_go, 1)
                        for t in range(C):
                            bank = ps_main[:, t // 2, (t % 2) * 2 * H:(t % 2 + 1) * 2 * H]
                            tt(new_s[:, t * H:(t + 1) * H], bank[:, 0:H], W["eb1"][0][:], ALU.add)
                            ins = nc.vector.tensor_copy(new_t[:, t * H:(t + 1) * H], bank[:, H:2 * H])
                        ins.then_inc(st_ready, 1)
                        v.wait_ge(st_out, c * 32 + 32)
                        v.sem_inc(v_go, 1)
                v.sem_inc(arg_ready, 1)
                with v.Fori(0, TURNS1) as i:
                    step.enter(i, 2 * 5)
                    for h in range(2):
                        m = i * 2 + h
                        at = bass.ds(m * U1, U1)
                        v.wait_ge(group1_done, m + 1)
                        v.sem_inc(v_go, 1)
                        nc.vector.tensor_copy(idx[:, h, 0:U1], src_idx[:, at])
                        nc.vector.tensor_copy(idx[:, h, U1:2 * U1], dst_idx[:, at]).then_inc(idx1_ready, 1)
                        step.up(nc.vector.tensor_copy(rank_g[:, h, 0:U1], rank[:, at]))
                        v.wait_ge(edge_in[h], i * 48 + 48)
                        v.sem_inc(v_go, 1)
                        step.up(ts(src_lo[:, h], src_c[:, h], P - 1, None, ALU.bitwise_and))
                        step.up(ts(src_hi[:, h], src_c[:, h], 7, None, ALU.logical_shift_right))
                        settled()
                        for u in range(U1):
                            one = src_c[:, h, u:u + 1]
                            ts(hot_src[:, h, u, 0:P], iota_h, src_lo[:, h, u:u + 1], None, ALU.is_equal)
                            ts(hot_src[:, h, u, P:P + J], iota_h[:, 0:J], src_hi[:, h, u:u + 1], None, ALU.is_equal)
                            ts(pick1[:, h, u], iota_f[:], rank_g[:, h, u:u + 1], None, ALU.is_equal)
                            ins = ts(same[:, h, u], src_b[:, h, u * P:(u + 1) * P], one, None, ALU.is_equal)
                        step.up(ins)
                        settled()
                        for u in range(U1):
                            ins = nc.vector.tensor_tensor_reduce(scratch[:, h, u * P:(u + 1) * P], same[:, h, u], low[:], 1.0, 0.0, ALU.mult, ALU.add,
                                                                 earlier[:, h, u:u + 1])
                        ins.then_inc(pick1_ready, 1)
                        v.wait_ge(pick1_ready, m + 1)
                        v.wait_ge(added_free, m + 1)
                        v.sem_inc(v_go, 1)
                        nc.vector.scalar_tensor_tensor(add_idx[:, h], earlier[:, h], float(2 * NPAD), idx[:, h, 0:U1],
                                                       ALU.mult, ALU.add).then_inc(add_idx_ready, 1)
                        v.wait_ge(rows1_in[h], i * (32 * U1) + 32 * U1)
                        v.wait_ge(t_ready, m + 2)
                        v.sem_inc(v_go, 1)
                        step.up(tt(rows_s[:, h], rows_s[:, h], rows_t[:, h], ALU.add))
                        settled()
                        tt(arg, rows_s[:, h], t_emb, ALU.add).then_inc(arg_ready, 1)
                    step.leave(TURNS1)
                v.wait_ge(sums1_out, 2 * TURNS1 + 2)
                step.up(nc.vector.tensor_tensor_scan(run_sum[:], chained[:], tile_sum[:], 0.0, ALU.mult, ALU.add))
                settle()
                step.up(nc.vector.memset(tile_sum[:, 0:1], 0.0))
                step.up(tt(tile_sum[:, 1:T], run_sum[:, 0:T - 1], cont[:, 1:T], ALU.mult))
                settle()
                v.sem_inc(carry1_ready, 1)
                v.wait_ge(src_counted, 1)
                step.up(nc.vector.tensor_copy(deg_src, ps_last[:, 1, 0:J]))
                settle()
                v.sem_inc(o1_taken, 1)
                for h in range(2):
                    nc.vector.tensor_copy(nidx[:, h], node_idx[:, h * C:(h + 1) * C]).then_inc(nidx1_ready, 1)
                with v.Fori(0, CTURNS) as i:
                    step.enter(i, 2 * 3)
                    for h in range(2):
                        c = i * 2 + h
                        chunk = bass.ds(c * (C * F), C * F)
                        settled()
                        step.up(tt(split(tmp[:]), spread(W["eb2"][0][:, 0:F]), per_node(deg_src, c * C), ALU.mult))
                        step.up(tt(split(z[:, h]), spread(W["eb2"][0][:, F:2 * F]), per_node(deg_dst, c * C), ALU.mult))
                        settled()
                        tt(tmp[:], tmp[:], z[:, h], ALU.add).then_inc(tmp_sum, 1)
                        v.wait_ge(sd_turned, c + 1)
                        v.sem_inc(v_go, 1)
                        nc.vector.tensor_copy(nidx[:, h], node_idx[:, bass.ds(c * C + 2 * C, C)]).then_inc(nidx1_ready, 1)
                        v.wait_ge(tmp_sum, c + 1)
                        v.wait_ge(o1_done, c + 1)
                        v.sem_inc(v_go, 1)
                        tt(z[:, h], tmp[:], ps_out[:, 0, 0:C * F], ALU.add).then_inc(o1_taken, 1)
                        v.wait_ge(o1_taken, c + 2)
                        v.sem_inc(v_go, 1)
                        step.up(tt(x_cur[:, chunk], z[:, h], x_cur[:, chunk], ALU.add))
                    step.leave(CTURNS)
                norm_layer(layers == 2)

            for k in range(PHASES):
                if k in (0, 4, 6):
                    make_table(scaled=k < 6)
                if k == 6:
                    v.sem_inc(o_taken, 1)
                    v.wait_ge(weights_in, 16)
                pick_slots(k, weighted=k >= 6)
                carry_runs(k)
                if k == 0:
                    place_sums()
                finish_nodes(k)
                if k >= 6:
                    norm_hidden(k)
                if k in LN_AFTER:
                    norm_layer(k == PHASES - 1 and layers != 2)
                if k == 3 and layers > 1:
                    layer1()


BY_HIDDEN = ("L3_gnn_b1", "L3_gnn_gamma", "L3_gnn_beta")


def kernel(x, src, dst, edge_weight, edge_weight1, **w):
    import numpy as np
    import concourse.bacc as bacc
    from concourse.bass_utils import run_bass_kernel_spmd as run

    def padded(a, n, value):
        a = np.asarray(a).reshape(len(a), -1)
        return np.concatenate([a, np.full((n - len(a), a.shape[1]), value, a.dtype)])

    def columns(a):
        return np.ascontiguousarray(a.reshape(T, P).T)

    nodes = padded(x, NPAD, 0).reshape(J, P, F).transpose(1, 0, 2).reshape(P, J * F)
    srcs = padded(src, EPAD, PAD_NODE).reshape(-1)
    dsts = padded(dst, EPAD, PAD_NODE).reshape(-1)
    times = padded(edge_weight, EPAD, 0).reshape(-1)
    ew = padded(edge_weight1, EPAD, 0).reshape(-1)
    by_tile = dsts.reshape(T, P)
    end = np.full(1, -1, dsts.dtype)
    arrays = {
        "x_nodes": np.ascontiguousarray(nodes),
        "src_cols": columns(srcs),
        "dst_cols": columns(dsts),
        "weight_cols": columns(ew),
        "dst_rows": np.ascontiguousarray(dsts.reshape(G, U * P)),
        "tile_first": np.concatenate([by_tile[:, 0], end]),
        "tile_last": np.ascontiguousarray(by_tile[:, -1]),
        "time_row": times.reshape(1, EPAD),
        "time_cols": columns(times),
        "src_row": srcs.reshape(1, EPAD),
    }
    for name, a in w.items():
        arrays[name] = np.ascontiguousarray(np.asarray(a).T if name in BY_HIDDEN else np.asarray(a))
    nc = bacc.Bacc("TRN2", target_bir_lowering=False, num_devices=1)
    ap = {n: nc.dram_tensor("in_" + n, a.shape, mybir.dt.from_np(a.dtype), kind="ExternalInput").ap() for n, a in arrays.items()}

    def mat(name):
        return (ap[name], list(ap[name].shape), "mat")

    def row(name):
        return (ap[name], [P, ap[name].shape[0]], "row")

    def col(name):
        return (ap[name].rearrange("(p o) -> p o", o=1), [ap[name].shape[0], 1], "col")

    weights = {"W1": mat("L0_gnn_W1"), "b1": col("L0_gnn_b1"), "W2": mat("L0_gnn_W2"), "b2": row("L0_gnn_b2"),
               "W3": mat("L0_gnn_W3"), "b3": col("L0_gnn_b3"), "W4": mat("L0_gnn_W4"), "b4": row("L0_gnn_b4")}
    if 4 > 1:
        weights.update({"eW1": (ap["L1_gnn_W1"].rearrange("(s k) m -> k s m", s=2), [F, 2, H], "mat"),
                        "eb1": row("L1_gnn_b1"), "eWt": ((ap["L1_gnn_Wt"], ap["L1_gnn_bt"].rearrange("(o m) -> o m", o=1)), [2, H], "rows"),
                        "eW2": mat("L1_gnn_W2"), "eb2": row("L1_gnn_b2")})
    if 4 > 2:
        weights.update({"cW1": mat("L2_gnn_W1"), "cb1": col("L2_gnn_b1"), "cW2": mat("L2_gnn_W2"), "cb2": col("L2_gnn_b2"),
                        "cWl": mat("L2_gnn_Wl"), "cbl": row("L2_gnn_bl")})
    if 4 > 3:
        def layers_in(name):
            return (ap[name].rearrange("l k m -> k l m"), [F, 3, F], "mat")

        def layer_cols(name):
            return (ap[name], [F, 3], "mat")

        weights.update({"gW1": layers_in("L3_gnn_W1"), "gW2": layers_in("L3_gnn_W2"), "gb1": layer_cols("L3_gnn_b1"),
                        "gg": layer_cols("L3_gnn_gamma"), "gbe": layer_cols("L3_gnn_beta"),
                        "gb2": (ap["L3_gnn_b2"].rearrange("l k -> (l k)"), [P, 3 * F], "row")})
    out = nc.dram_tensor("out_0_dram", (P, J * F), F32, kind="ExternalOutput").ap()
    gnn_program(nc, ap["x_nodes"], ap["src_cols"], ap["dst_cols"], ap["weight_cols"], ap["dst_rows"], ap["tile_first"],
                ap["tile_last"], ap["time_row"], ap["time_cols"], ap["src_row"], weights, out, layers=4)
    r = run(nc, [{"in_" + n: a for n, a in arrays.items()}], core_ids=[0])
    got = r.results[0]["out_0_dram"].reshape(P, J, F).transpose(1, 0, 2).reshape(NPAD, F)[:N]
    return np.ascontiguousarray(got)
```

```python
from contextlib import ExitStack

import concourse.bass as bass
from concourse import mybir

ALU = mybir.AluOpType
ACT = mybir.ActivationFunctionType
AX = mybir.AxisListType
F32 = mybir.dt.float32
BF16 = mybir.dt.bfloat16
I32 = mybir.dt.int32
U32 = mybir.dt.uint32

P = 128
N = 12500
E = 200000
F = 64
H = 128
J = -(-N // P)
NPAD = J * P
U = 16
T = -(-E // (P * 2 * U)) * 2 * U
G = T // U
EPAD = T * P
PAD_NODE = NPAD - 1
C = 7
NC = J // C
U1 = U // 2
TURNS = G // 2
TURNS1 = G
CTURNS = NC // 2
CW = C * P // 2
KIND = ["wide", "narrow", "wide_skip", "residual", "conv", "conv_out", "gin", "gin", "gin"]
PHASES = len(KIND)
LN_AFTER = {3: 1, 5: 3, 8: 4}
ZERO_ROW = P * T
HI_POOL, HI_ACT = 5, 8
BN_PARTS = 25
BN_LEN = N // BN_PARTS
LN_EPS = 1e-5
BN_EPS = 1e-5
assert BN_PARTS * BN_LEN == N and BN_LEN <= 512
assert NC * C == J and NC % 2 == 0 and G % 2 == 0 and PAD_NODE >= N


class Tally:

    def __init__(self, sem):
        self.sem, self.base, self.n = sem, 0, 0

    def up(self, ins, by=1):
        ins.then_inc(self.sem, by)
        self.n += by
        return ins

    def value(self):
        return self.base + self.n

    def enter(self, i, per_turn):
        self.start, self.per_turn = self.base + self.n, per_turn
        self.base, self.n = self.start + i * per_turn, 0

    def leave(self, turns):
        assert self.n == self.per_turn, (self.n, self.per_turn)
        self.base, self.n = self.start + turns * self.per_turn, 0


def gnn_program(nc, x_nodes, src_cols, dst_cols, weight_cols, dst_rows, tile_first, tile_last, time_cols, src_row,
                weights, out):
    with ExitStack() as ctx:
        def sb(name, shape, dt=F32):
            return ctx.enter_context(nc.sbuf_tensor(name, shape, dt))[:]

        def psum(name, shape):
            return ctx.enter_context(nc.psum_tensor(name, shape, F32))[:]

        def sem(name):
            return ctx.enter_context(nc.semaphore(name))

        table = nc.dram_tensor("table", (NPAD, F), F32).ap()
        partial = nc.dram_tensor("partial", (P * T + P, F), F32).ap()
        table_v = table.rearrange("(p j) f -> p (j f)", p=P)
        partial_v = partial[0:P * T, :].rearrange("(p t) f -> p (t f)", p=P)

        table_s = nc.dram_tensor("table_s", (NPAD, H), F32).ap()
        table_t = nc.dram_tensor("table_t", (NPAD + P, H), F32).ap()
        rank_line = nc.dram_tensor("rank_line", (1, EPAD), BF16).ap()
        partial1 = nc.dram_tensor("partial1", (P * T + P, H), F32).ap()
        partial1_v = partial1[0:P * T, :].rearrange("(p t) f -> p (t f)", p=P)
        by_src = [nc.dram_tensor("by_src%d" % u, (NPAD, H), F32).ap() for u in range(U1)]
        by_src_v = [a.rearrange("(p j) f -> p (j f)", p=P) for a in by_src]

        in_order = {"src_cols": nc.dram_tensor("sorted_src_cols", (P, T), I32).ap(),
                    "weight_cols": nc.dram_tensor("sorted_weight_cols", (P, T), F32).ap(),
                    "src_row": nc.dram_tensor("sorted_src_row", (1, EPAD), I32).ap(),
                    "time_cols": nc.dram_tensor("sorted_time_cols", (P, T), F32).ap()}
        dst_line = nc.dram_tensor("sorted_dst", (EPAD,), I32).ap()
        moved = [nc.dram_tensor("moved%d" % d, (EPAD, 4), F32).ap() for d in range(2)]

        ps_main = psum("ps_main", [P, 4, 512])
        ps_out = psum("ps_out", [P, 2, 512])
        ps_last = psum("ps_last", [P, 2, 512])

        x_cur = sb("x_cur", [P, J * F])
        own = sb("own", [P, J * F])
        big = sb("big", [P, NPAD])
        rank = sb("rank", [P, T])
        edge_w = sb("edge_w", [P, T])
        src_idx_pad = sb("src_idx", [P, T + 2 * U1], U32)
        src_idx = src_idx_pad[:, 0:T]
        chained = sb("chained", [P, T])
        cont = sb("cont", [P, T])
        tile_sum = sb("tile_sum", [P, T])
        run_sum = sb("run_sum", [P, T])
        rows = sb("rows", [P, 2, U * F])
        pick = sb("pick", [P, 2, U, P])
        stage = sb("stage", [P, 2, U * F])
        idx = sb("idx", [P, 2, U], U32)
        rank_g = sb("rank_g", [P, 2, U])
        w_g = sb("w_g", [P, 2, U])
        node_idx = sb("node_idx", [P, J + 2 * C], U32)
        nidx = sb("nidx", [P, 2, C], U32)
        agg = sb("agg", [P, 2, C * F])
        z = sb("z", [P, 2, C * F])
        tmp = sb("tmp", [P, C * F])
        zT = sb("zT", [F, C * P])
        hT = sb("hT", [P, C * P])
        bent = [hT[0:F, :], zT[:]]
        carry_rows = pick[:, 0].rearrange("p u c -> p (u c)")[:, 0:U * F]
        zeros = hT
        carry_idx = sb("carry_idx", [P, U], U32)
        deg_dst = sb("deg_dst", [P, J])
        deg_src = sb("deg_src", [P, J])
        dinv = sb("dinv", [P, J])
        iota_f = sb("iota_f", [P, P])
        iota_h = sb("iota_h", [P, P], BF16)
        iota_i = sb("iota_i", [P, P], I32)
        part_i = sb("part_i", [P, 1], I32)
        part_f = sb("part_f", [P, 1])
        ident = sb("ident", [P, P])
        tri = sb("tri", [P, P])
        ones = sb("ones", [P, P])
        hot_zero = sb("hot_zero", [P, P], BF16)
        low = sb("low", [P, P])
        src_c = sb("src_c", [P, 2, U1], I32)
        time_c = sb("time_c", [P, 2, U1])
        tile_at_g = sb("tile_at_g", [1, 2, U1], I32)
        src_lo = sb("src_lo", [P, 2, U1], I32)
        src_hi = sb("src_hi", [P, 2, U1], I32)
        earlier = sb("earlier", [P, 2, U1])
        add_idx = sb("add_idx", [P, 2, U1], U32)
        stats = sb("stats", [F, BN_PARTS * 6])
        bn = sb("bn", [F, 8])
        small = sb("small", [P, 8, J])
        tid_i = sb("tid_i", [P, U], I32)
        next_first = sb("next_first", [P, U], I32)

        W1G = U1 * H
        rows_s = rows
        rows_t = big[:, 0:2 * W1G].rearrange("p (h c) -> p h c", h=2)
        pick1, same = pick[:, :, 0:U1], pick[:, :, U1:2 * U1]
        hid = big[:, 2 * W1G:4 * W1G].rearrange("p (h c) -> p h c", h=2)
        merged = big[:, 4 * W1G:6 * W1G].rearrange("p (h c) -> p h c", h=2)
        src_b = big[:, 6 * W1G:8 * W1G].bitcast(I32).rearrange("p (h c) -> p h c", h=2)
        t_emb = big[:, 8 * W1G:9 * W1G]
        arg = big[:, 9 * W1G:10 * W1G]
        scratch = big[:, 6 * W1G:8 * W1G].rearrange("p (h c) -> p h c", h=2)
        tile_at = big[0:1, 10 * W1G:10 * W1G + T + 2 * U1].bitcast(I32)
        slot_hot = own[:, 2 * W1G:4 * W1G].rearrange("p (h c) -> p h c", h=2)
        rank_b = own[:, 4 * W1G:5 * W1G].bitcast(BF16).rearrange("p (h c) -> p h c", h=2)
        carry_rows1 = big[:, 0:U * H]
        parts_s = big[:, 2 * W1G:2 * W1G + U1 * C * H].rearrange("p (k c) -> p k c", k=U1)
        parts_all = big[:, 2 * W1G:2 * W1G + U1 * C * H]
        part_sums = pick.rearrange("p h u c -> p (h u c)")[:, 0:U1 // 2 * C * H]
        agg1 = big[:, 9 * W1G:9 * W1G + 2 * C * H].rearrange("p (h c) -> p h c", h=2)
        dT = big[:, 11 * W1G:11 * W1G + C * P]
        new_s = big[:, 0:2 * C * H].rearrange("p (h c) -> p h c", h=2)
        new_t = big[:, 2 * C * H:4 * C * H].rearrange("p (h c) -> p h c", h=2)
        node_pos = own[:, 5 * W1G:5 * W1G + J].bitcast(U32)
        hot_src = own[:, 0:U1 * (P + J)].bitcast(BF16).rearrange("p (h u c) -> p h u c", h=2, u=U1)
        dst_idx = edge_w[:].bitcast(U32)

        keys = big[:, 0:5 * T].rearrange("p (g q u) -> p g q u", q=5, u=U)
        hot_lo = pick.rearrange("p h u c -> p (h u c)")[:, 0:U * P].bitcast(BF16).rearrange("p (h u c) -> p h u c", h=2, u=U)
        hot_hi = big[:, 5 * T:7 * T].bitcast(BF16)[:, 0:2 * U * J].rearrange("p (h u c) -> p h u c", h=2, u=U)
        hot_end = big[:, 5 * T:8 * T].bitcast(BF16)[:, 0:2 * U * (P + J)].rearrange("p (h u c) -> p h u c", h=2, u=U)
        kg = z[:, :, 0:5 * U]
        row_dst = own[0:G, 0:U * P].bitcast(I32)
        row_chg = own[0:G, U * P:2 * U * P]
        row_pre = own[0:G, 2 * U * P:3 * U * P]
        row_rank_h = big[0:G, 7 * T:7 * T + U * P // 2].bitcast(BF16)
        row_rank = pick[0:G, 0].rearrange("p u c -> p (u c)")
        row_val = pick[0:G, 1].rearrange("p u c -> p (u c)")
        col_i = rows[:].rearrange("p h c -> p (h c)").bitcast(I32)[:, 0:T]
        dst_i = run_sum[:].bitcast(I32)
        src_i = tile_sum[:].bitcast(I32)
        first_b = chained
        last_b = stage[:].rearrange("p h c -> p (h c)")[:, 0:T]

        edges = own.rearrange("p (t q) -> p t q", q=4)
        digit = chained
        digit_hot, digit_sum, digit_tmp, digit_base = (pick[:, 0, q] for q in range(4))
        digit_col, digit_rank = rank_g[:, 0, 0:1], rank_g[:, 0, 1:2]
        move_idx, moving = idx[:, 0, 0:1], agg[:, 0, 0:4]
        out_of_order = sb("out_of_order", [P, 2])
        sort_flag = sb("sort_flag", [1, 1], I32)

        W = {}
        for name, (ap, shape, kind) in weights.items():
            W[name] = (sb("w_" + name, shape), ap, kind)

        inputs_in = sem("inputs_in")
        zero_in = sem("zero_in")
        zero_made = sem("zero_made")
        consts = sem("consts")
        v_step = Tally(sem("v_step"))
        ranks_out = sem("ranks_out")
        ranks_in = sem("ranks_in")
        keys_ready = sem("keys_ready")
        hot_ready = sem("hot_ready")
        kg_ready, hi_ready = sem("kg_ready"), sem("hi_ready")
        distance_ready, act_hi_ready = sem("distance_ready"), sem("act_hi_ready")
        count_ready, count_used = sem("count_ready"), sem("count_used")
        counted_all, src_counted = sem("counted_all"), sem("src_counted")
        hot_used = sem("hot_used")
        counted = sem("counted")
        deg_ready = sem("deg_ready")
        cum_ready = sem("cum_ready")
        root_ready = sem("root_ready")
        root_in = sem("root_in")
        own_ready = sem("own_ready")
        table_out = sem("table_out")
        idx_ready = sem("idx_ready")
        pool_go = sem("pool_go")
        rows_in = [[sem("rows_in%d_%d" % (s, h)) for h in range(2)] for s in range(-(-PHASES // 3))]
        pick_ready = sem("pick_ready")
        group_done = sem("group_done")
        sums_out = sem("sums_out")
        stored = [sem("stored0"), sem("stored1")]
        stage_free = sem("stage_free")
        carry_ready = sem("carry_ready")
        carry_turned = sem("carry_turned")
        carry_in = sem("carry_in")
        carry_added = sem("carry_added")
        nidx_ready = sem("nidx_ready")
        agg_in = [sem("agg_in0"), sem("agg_in1")]
        z_ready = sem("z_ready")
        z_turned = sem("z_turned")
        zT_ready = sem("zT_ready")
        h_done = sem("h_done")
        hT_ready = sem("hT_ready")
        bn_var, bn_root, bn_ready = sem("bn_var"), sem("bn_root"), sem("bn_ready")
        o_taken = sem("o_taken")
        v_go, pe_go, act_go = sem("v_go"), sem("pe_go"), sem("act_go")
        o_done = sem("o_done")
        skip_ready = sem("skip_ready")
        ln_var, ln_root = sem("ln_var"), sem("ln_root")
        result_ready = sem("result_ready")
        result_out = sem("result_out")
        order_summed, flag_ready, copies_in = sem("order_summed"), sem("flag_ready"), sem("copies_in")
        s_step = Tally(sem("s_step"))
        cols_in, edges_in, unpacked, lines_out, again_in = sem("cols_in"), sem("edges_in"), sem("unpacked"), sem("lines_out"), sem("again_in")
        digit_ready, digit_used, digit_counted, digit_zeroed = sem("digit_ready"), sem("digit_used"), sem("digit_counted"), sem("digit_zeroed")
        rank_ready, edge_moved, edge_free = sem("rank_ready"), sem("edge_moved"), sem("edge_free")

        zeroed = sem("zeroed")
        mask_ready, mask_summed = sem("mask_ready"), sem("mask_summed")
        pos_ready = sem("pos_ready")
        x_ready, x_turned = sem("x_ready"), sem("x_turned")
        xT_ready = sem("xT_ready")
        st_done = sem("st_done")
        new_s_ready, new_t_ready = sem("new_s_ready"), sem("new_t_ready")
        rank_h_ready, rank_line_out = sem("rank_h_ready"), sem("rank_line_out")
        tile_at_ready = sem("tile_at_ready")
        idx1_ready = sem("idx1_ready")
        slot_ready = sem("slot_ready")
        spread_done = sem("spread_done")
        pick1_ready, add_idx_ready = sem("pick1_ready"), sem("add_idx_ready")
        time_ready, t_ready = sem("time_ready"), sem("t_ready")
        arg_ready, hid_ready = sem("arg_ready"), sem("hid_ready")
        group1_done = sem("group1_done")
        sums1_out, stage1_free = sem("sums1_out"), sem("stage1_free")
        added, added_free = sem("added"), sem("added_free")
        carry1_ready, carry1_turned = sem("carry1_ready"), sem("carry1_turned")
        carry1_in, carry1_added = sem("carry1_in"), sem("carry1_added")
        nidx1_ready = sem("nidx1_ready")
        parts_in, parts_summed = sem("parts_in"), sem("parts_summed")
        parts_free = sem("parts_free")
        sd_turned, sd_ready = sem("sd_turned"), sem("sd_ready")
        o1_done, o1_taken = sem("o1_done"), sem("o1_taken")
        tmp_sum = sem("tmp_sum")
        weights_in = sem("weights_in")
        s_out, t_out = [sem("s_out0"), sem("s_out1")], [sem("t_out0"), sem("t_out1")]
        edge_in, rows1_in = [sem("edge_in0"), sem("edge_in1")], [sem("rows1_in0"), sem("rows1_in1")]
        stored1, agg1_in = [sem("stored1_0"), sem("stored1_1")], [sem("agg1_in0"), sem("agg1_in1")]
        t_free = sem("t_free")
        block = ctx.enter_context(nc.Block())

        MATS = {0: (W["W1"][0], W["b1"][0], W["W2"][0]), 2: (W["W3"][0], W["b3"][0], W["W4"][0])}
        MATS[4] = (W["cW1"][0], W["cb1"][0], ident[0:F, 0:F])
        MATS[5] = (W["cW2"][0], W["cb2"][0], W["cWl"][0])
        for l in range(PHASES - 6):
            MATS[6 + l] = (W["gW1"][0][:, l], W["gb1"][0][:, l:l + 1], W["gW2"][0][:, l])
        TURNED = sorted(MATS)
        HT_EXTRA = {k: NC * max(0, k - 6) for k in TURNED}

        LOADS = []
        LOADS += [(x_cur[:], x_nodes), (dst_i, dst_cols), (src_i, src_cols),
                  (row_dst, dst_rows), (first_b[:].bitcast(I32), tile_first[0:T].partition_broadcast(P)),
                  (last_b.bitcast(I32), tile_last.partition_broadcast(P)),
                  (next_first[0:G, :], tile_first[1:T + 1].rearrange("(g u) -> g u", u=U))]
        for name, (t, ap, kind) in W.items():
            LOADS.append((t[:], ap.partition_broadcast(P) if kind == "row" else ap))

        def if_unsorted(eng):
            eng.wait_ge(flag_ready, 1)
            return eng.If(eng.value_load(sort_flag[0:1, 0:1], min_val=0, max_val=1) > 0)

        @block.sync
        def _(sp):
            for dst, source in LOADS:
                sp.dma_start(dst, source).then_inc(inputs_in, 16)
            for name, source in (("src_cols", src_cols), ("weight_cols", weight_cols), ("src_row", src_row), ("time_cols", time_cols)):
                sp.dma_start(in_order[name], source).then_inc(copies_in, 16)
            with if_unsorted(sp):
                sp.dma_start(edge_w, weight_cols).then_inc(cols_in, 16)
                sp.dma_start(cont, time_cols).then_inc(cols_in, 16)
                for d in range(2):
                    sp.wait_ge(edge_moved, 16 * T * (d + 1))
                    sp.dma_start(edges, moved[d].rearrange("(t p) q -> p t q", p=P)).then_inc(edges_in, 16)
                sp.wait_ge(unpacked, 1)
                sp.wait_ge(copies_in, 64)
                with nc.allow_non_contiguous_dma(reason="only for inputs out of order"):
                    sp.dma_start(in_order["src_cols"], src_i).then_inc(lines_out, 16)
                    sp.dma_start(in_order["weight_cols"], edge_w).then_inc(lines_out, 16)
                    sp.dma_start(in_order["src_row"][0].rearrange("(t p) -> p t", p=P), src_i).then_inc(lines_out, 16)
                    sp.dma_start(in_order["time_cols"], cont).then_inc(lines_out, 16)
                    sp.dma_start(dst_line.rearrange("(t p) -> p t", p=P), dst_i).then_inc(lines_out, 16)
                    sp.wait_ge(lines_out, 80)
                    ends = dst_line.rearrange("(t p) -> t p", p=P)
                    sp.dma_start(row_dst, dst_line.rearrange("(g e) -> g e", g=G)).then_inc(again_in, 16)
                    sp.dma_start(first_b.bitcast(I32), ends[:, 0].partition_broadcast(P)).then_inc(again_in, 16)
                    sp.dma_start(last_b.bitcast(I32), ends[:, P - 1].partition_broadcast(P)).then_inc(again_in, 16)
                    starts = ends[:, 0].rearrange("(g u) -> g u", u=U)
                    sp.dma_start(next_first[0:G, 0:U - 1], starts[:, 1:U]).then_inc(again_in, 16)
                    sp.dma_start(next_first[0:G - 1, U - 1:U], starts[1:G, 0:1]).then_inc(again_in, 16)
            sp.wait_ge(zero_made, 1)
            sp.dma_start(partial[P * T:P * T + P, :], zeros[:, 0:F]).then_inc(zero_in, 16)
            sp.dma_start(partial1[P * T:P * T + P, :], zeros[:, 0:H]).then_inc(zero_in, 16)
            sp.dma_start(table_t[NPAD:NPAD + P, :], zeros[:, 0:H]).then_inc(zero_in, 16)
            sp.wait_ge(rank_h_ready, 1)
            sp.dma_start(rank_line[0].rearrange("(g e) -> g e", g=G), row_rank_h).then_inc(rank_line_out, 16)

            sp.sem_inc(stage_free, 2)

            def store_table(k):
                with sp.Fori(0, NC) as c:
                    sp.wait_ge(own_ready, c + NC * k + 1)
                    sp.dma_start(table_v[:, bass.ds(c * (C * F), C * F)], own[:, bass.ds(c * (C * F), C * F)]).then_inc(table_out, 16)

            def layer1():
                for h in range(2):
                    sp.sem_inc(s_out[h], 16)
                with sp.Fori(0, CTURNS) as i:
                    for h in range(2):
                        c = i * 2 + h
                        sp.wait_ge(new_s_ready, c + 1)
                        sp.dma_start(table_s.rearrange("(p j) f -> p (j f)", p=P)[:, bass.ds(c * (C * H), C * H)],
                                     new_s[:, h]).then_inc(s_out[h], 16)
                for h in range(2):
                    sp.wait_ge(s_out[h], 16 * CTURNS + 16)
                    sp.wait_ge(t_out[h], 16 * C * CTURNS)
                sp.wait_ge(copies_in, 64)
                sp.wait_ge(rank_line_out, 16)
                sp.sem_inc(stage1_free, 2)
                def load_group(m, h):
                    at = bass.ds(m * (U1 * P), U1 * P)
                    sp.wait_ge(tile_at_ready, m + 1)
                    sp.dma_start(rank_b[:, h, :], rank_line[0, at].partition_broadcast(P)).then_inc(edge_in[h], 16)
                    sp.dma_start(time_c[:, h, :], in_order["time_cols"][:, bass.ds(m * U1, U1)]).then_inc(edge_in[h], 16)
                    sp.dma_start(src_c[:, h, :], in_order["src_cols"][:, bass.ds(m * U1, U1)]).then_inc(edge_in[h], 16)
                    for u in range(U1):
                        first = sp.value_load(tile_at_g[0:1, h, u:u + 1], min_val=0, max_val=NPAD)
                        sp.dma_start(rows_t[:, h, u * H:(u + 1) * H], table_t[bass.ds(first, P), :]).then_inc(edge_in[h], 16)
                    sp.dma_start(src_b[:, h, :], in_order["src_row"][0, at].partition_broadcast(P)).then_inc(edge_in[h], 16)

                def store_group(m, h):
                    sp.wait_ge(sums1_out, m + 3)
                    sp.dma_start(partial1_v[:, bass.ds(m * W1G, W1G)], stage[:, h, :]).then_inc(stored1[h], 16)

                for h in range(2):
                    load_group(h, h)
                with sp.Fori(0, TURNS1 - 1) as i:
                    for h in range(2):
                        load_group(i * 2 + (h + 2), h)
                        store_group(i * 2 + h, h)
                    for h in range(2):
                        sp.wait_ge(stored1[h], i * 16 + 16)
                        sp.sem_inc(stage1_free, 1)
                for h in range(2):
                    store_group(2 * (TURNS1 - 1) + h, h)
                    sp.wait_ge(stored1[h], TURNS1 * 16)
                sp.wait_ge(added, 16 * U1 * 2 * TURNS1)
                with sp.Fori(0, NC) as c:
                    at = bass.ds(c * (C * H), C * H)
                    sp.wait_ge(parts_free, c + 1)
                    for u in range(U1):
                        sp.dma_start(parts_s[:, u, :], by_src_v[u][:, at]).then_inc(parts_in, 16)

            with sp.Fori(0, NC) as c:
                for a in by_src_v + [table_t[0:NPAD, :].rearrange("(p j) f -> p (j f)", p=P)]:
                    sp.dma_start(a[:, bass.ds(c * (C * H), C * H)], zeros[:, 0:C * H]).then_inc(zeroed, 16)

            for k in range(PHASES):
                if k == 4:
                    layer1()
                if k == 6:
                    sp.wait_ge(own_ready, NC * 6 + 1)
                    sp.dma_start(edge_w[:], in_order["weight_cols"]).then_inc(weights_in, 16)
                store_table(k)
                with sp.Fori(0, TURNS) as i:
                    n = i + TURNS * k
                    for h in range(2):
                        sp.wait_ge(sums_out, n * 2 + h + 3)
                        sp.dma_start(partial_v[:, bass.ds((i * 2 + h) * (U * F), U * F)], stage[:, h, :]).then_inc(stored[h], 16)
                    for h in range(2):
                        sp.wait_ge(stored[h], n * 16 + 16)
                        sp.sem_inc(stage_free, 1)
            with sp.Fori(0, NC) as c:
                at = bass.ds(c * (C * F), C * F)
                sp.wait_ge(result_ready, c + 1)
                sp.dma_start(out[:, at], x_cur[:, at]).then_inc(result_out, 16)
            sp.wait_ge(result_out, 16 * NC)
            sp.wait_ge(inputs_in, 16 * len(LOADS))
            sp.wait_ge(zero_in, 48)
            sp.wait_ge(zeroed, 16 * NC * (U1 + 1))
            sp.wait_ge(table_out, 16 * NC * PHASES)
            for h in range(2):
                sp.wait_ge(stored[h], 16 * TURNS * PHASES)

        @block.gpsimd
        def _(pool):
            nc.gpsimd.iota(iota_i[:], pattern=[[1, P]], base=0, channel_multiplier=0).then_inc(consts, 1)
            nc.gpsimd.iota(part_i[:], pattern=[[0, 1]], base=0, channel_multiplier=1).then_inc(consts, 1)
            nc.gpsimd.iota(tid_i[:], pattern=[[1, U]], base=0, channel_multiplier=U).then_inc(consts, 1)

            with if_unsorted(pool):
                pool.sem_inc(edge_free, 1)
                for d in range(2):
                    with pool.Fori(0, T) as t:
                        pool.wait_ge(rank_ready, t + (T * d + 1))
                        pool.sem_inc(pool_go, 1)
                        pool.indirect_dma_start(
                            out=moved[d], out_offset=bass.IndirectOffsetOnAxis(ap=move_idx, axis=0),
                            in_=moving, in_offset=None).then_inc(edge_moved, 16)
                        pool.wait_ge(edge_moved, t * 16 + (16 * T * d + 16))
                        pool.sem_inc(edge_free, 1)

            with pool.Fori(0, TURNS) as i:
                for h in range(2):
                    pool.wait_ge(kg_ready, i * 2 + h + 1)
                    pool.sem_inc(pool_go, 1)
                    for u in range(HI_POOL):
                        ins = nc.gpsimd.tensor_scalar(hot_hi[:, h, u], iota_h[:, 0:J], kg[:, h, U + u:U + u + 1], None, ALU.is_equal)
                    ins.then_inc(hi_ready, 1)

            def gather_edges(k):
                pool.wait_ge(table_out, 16 * NC * (k + 1))
                with pool.Fori(0, TURNS) as i:
                    for h in range(2):
                        pool.wait_ge(idx_ready, (i + TURNS * k) * 2 + h + 1)
                        pool.sem_inc(pool_go, 1)
                        for u in range(U):
                            pool.indirect_dma_start(
                                out=rows[:, h, u * F:(u + 1) * F], out_offset=None, in_=table,
                                in_offset=bass.IndirectOffsetOnAxis(ap=idx[:, h, u:u + 1], axis=0),
                            ).then_inc(rows_in[k // 3][h], 16)

            def add_carries(k):
                for h in range(2):
                    pool.wait_ge(stored[h], 16 * TURNS * (k + 1))
                pool.wait_ge(zero_in, 48)
                pool.wait_ge(zeroed, 16 * NC * (U1 + 1))
                pool.wait_ge(carry_in, k + 1)
                for u in range(U):
                    pool.indirect_dma_start(
                        out=partial, out_offset=bass.IndirectOffsetOnAxis(ap=carry_idx[0:G, u:u + 1], axis=0),
                        in_=carry_rows[0:G, u * F:(u + 1) * F], in_offset=None, compute_op=ALU.add,
                    ).then_inc(carry_added, 16)
                pool.wait_ge(carry_added, 16 * U * (k + 1))

            def gather_nodes(k):
                with pool.Fori(0, CTURNS) as i:
                    for h in range(2):
                        pool.wait_ge(nidx_ready, (i + (CTURNS + 1) * k) * 2 + h + 1)
                        pool.sem_inc(pool_go, 1)
                        for c in range(C):
                            pool.indirect_dma_start(
                                out=agg[:, h, c * F:(c + 1) * F], out_offset=None, in_=partial,
                                in_offset=bass.IndirectOffsetOnAxis(ap=nidx[:, h, c:c + 1], axis=0),
                            ).then_inc(agg_in[h], 16)

            def layer1():
                def gather(m, h):
                    pool.wait_ge(idx1_ready, m + 1)
                    pool.sem_inc(pool_go, 1)
                    for u in range(U1):
                        pool.indirect_dma_start(
                            out=rows_s[:, h, u * H:(u + 1) * H], out_offset=None, in_=table_s,
                            in_offset=bass.IndirectOffsetOnAxis(ap=idx[:, h, u:u + 1], axis=0),
                        ).then_inc(rows1_in[h], 16)

                def add(m, h, begun=True):
                    pool.wait_ge(sums1_out, m + 3)
                    pool.wait_ge(add_idx_ready, m + 1)
                    if begun:
                        pool.wait_ge(added, m * (16 * U1))
                        pool.sem_inc(added_free, 1)
                    for u in range(U1):
                        pool.indirect_dma_start(
                            out=by_src[u], out_offset=bass.IndirectOffsetOnAxis(ap=add_idx[:, h, u:u + 1], axis=0),
                            in_=merged[:, h, u * H:(u + 1) * H], in_offset=None, compute_op=ALU.add,
                            bounds_check=NPAD - 1, oob_is_err=False,
                        ).then_inc(added, 16)

                def place_targets(m, h):
                    pool.wait_ge(pos_ready, m + 1)
                    pool.wait_ge(new_t_ready, m + 1)
                    pool.sem_inc(pool_go, 1)
                    for c in range(C):
                        pool.indirect_dma_start(
                            out=table_t, out_offset=bass.IndirectOffsetOnAxis(ap=nidx[:, h, c:c + 1], axis=0),
                            in_=new_t[:, h, c * H:(c + 1) * H], in_offset=None,
                            bounds_check=NPAD - 1, oob_is_err=False,
                        ).then_inc(t_out[h], 16)

                pool.sem_inc(t_free, 2)
                for h in range(2):
                    place_targets(h, h)
                with pool.Fori(1, CTURNS) as i:
                    for h in range(2):
                        pool.wait_ge(t_out[h], i * (16 * C))
                        pool.sem_inc(t_free, 1)
                        place_targets(i * 2 + h, h)
                for h in range(2):
                    pool.wait_ge(s_out[h], 16 * CTURNS + 16)
                    pool.wait_ge(t_out[h], 16 * C * CTURNS)
                pool.sem_inc(added_free, 2)
                last = 2 * TURNS1 - 1
                gather(0, 0)
                gather(1, 1)
                gather(2, 0)
                add(0, 0, begun=False)
                gather(3, 1)
                add(1, 1)
                with pool.Fori(0, TURNS1 - 2) as i:
                    for h in range(2):
                        gather(i * 2 + (h + 4), h)
                        add(i * 2 + (h + 2), h)
                add(last - 1, 0)
                add(last, 1)
                for h in range(2):
                    pool.wait_ge(stored1[h], 16 * TURNS1)
                pool.wait_ge(carry1_in, 1)
                for u in range(U):
                    pool.indirect_dma_start(
                        out=partial1, out_offset=bass.IndirectOffsetOnAxis(ap=carry_idx[0:G, u:u + 1], axis=0),
                        in_=carry_rows1[0:G, u * H:(u + 1) * H], in_offset=None, compute_op=ALU.add,
                    ).then_inc(carry1_added, 16)
                pool.wait_ge(carry1_added, 16 * U)
                with pool.Fori(0, CTURNS) as i:
                    for h in range(2):
                        pool.wait_ge(nidx1_ready, i * 2 + h + 1)
                        pool.sem_inc(pool_go, 1)
                        for c in range(C):
                            pool.indirect_dma_start(
                                out=agg1[:, h, c * H:(c + 1) * H], out_offset=None, in_=partial1,
                                in_offset=bass.IndirectOffsetOnAxis(ap=nidx[:, h, c:c + 1], axis=0),
                            ).then_inc(agg1_in[h], 16)

            for k in range(PHASES):
                gather_edges(k)
                add_carries(k)
                gather_nodes(k)
                if k == 3:
                    layer1()

        @block.tensor
        def _(pe):
            pe.wait_ge(order_summed, 1)
            pe.matmul(ps_last[0:1, 0, 0:1], out_of_order[0:G, 0:1], ones[0:G, 0:1], start=True, stop=True).then_inc(order_summed, 1)
            with if_unsorted(pe):
                for d in range(2):
                    pe.wait_ge(digit_zeroed, d + 1)
                    pe.matmul(ps_main[:, 0, 0:P], ones, digit_sum, start=True, stop=False, skip_group_check=True)
                    pe.sem_inc(digit_used, 1)
                    with pe.Fori(0, T) as t:
                        pe.wait_ge(digit_ready, t + (2 * T * d + 1))
                        pe.sem_inc(pe_go, 1)
                        pe.matmul(ps_main[:, 0, 0:P], ones, digit_hot, start=False, stop=False,
                                  skip_group_check=True).then_inc(digit_used, 1)
                    pe.matmul(ps_main[:, 0, 0:P], ones, digit_sum, start=False, stop=True,
                              skip_group_check=True).then_inc(digit_counted, 1)
                    with pe.Fori(0, T) as t:
                        pe.wait_ge(digit_ready, t + (2 * T * d + T + 1))
                        pe.sem_inc(pe_go, 1)
                        pe.matmul(ps_main[:, 1, 0:P], tri, digit_hot, start=True, stop=True)
                        pe.matmul(ps_main[:, 2, 0:P], ones, digit_hot, start=True, stop=True).then_inc(digit_counted, 1)

            def turn_rows(source, ready, n):
                pe.wait_ge(ready, n)
                for u in range(U):
                    ins = pe.transpose(ps_main[:, u // 4, (u % 4) * P:(u % 4) * P + G],
                                       source[:, u * P:(u + 1) * P], ident[0:G, 0:G])
                ins.then_inc(ranks_out, 1)

            turn_rows(row_rank, keys_ready, 1)
            pe.wait_ge(ranks_in, 4)
            turn_rows(row_val, keys_ready, 1)

            pe.wait_ge(hot_ready, 1)
            zero_lo, zero_hi = hot_zero[:, 0:P], hot_zero[:, 0:J]

            def clear(counts):
                pe.matmul(counts, zero_lo, zero_hi, start=True, stop=False, skip_group_check=True)

            def close(counts):
                return pe.matmul(counts, zero_lo, zero_hi, start=False, stop=True, skip_group_check=True)

            dst_counts, end_counts, src_counts = ps_out[:, 0, 0:J], ps_out[:, 1, 0:J], ps_last[:, 1, 0:J]
            clear(dst_counts)
            pe.sem_inc(hot_used, 2)
            with pe.Fori(0, TURNS) as i:
                for h in range(2):
                    pe.wait_ge(hot_ready, i * 2 + h + 2)
                    pe.wait_ge(hi_ready, i * 2 + h + 1)
                    pe.wait_ge(act_hi_ready, i * 2 + h + 1)
                    pe.sem_inc(pe_go, 1)
                    for u in range(U):
                        ins = pe.matmul(dst_counts, hot_lo[:, h, u], hot_hi[:, h, u],
                                        start=False, stop=False, skip_group_check=True)
                    ins.then_inc(hot_used, 1)
            close(dst_counts).then_inc(counted, 1)

            pe.wait_ge(deg_ready, 1)
            pe.matmul(ps_last[:, 1, 0:J], tri[:], deg_dst[:], start=True, stop=True)
            pe.matmul(ps_last[:, 1, P:P + J], ones[:], deg_dst[:], start=True, stop=True).then_inc(cum_ready, 1)

            pe.sem_inc(group_done, 2)

            def sum_runs(k):
                if k == 0:
                    pe.wait_ge(deg_ready, 2)
                    clear(end_counts)
                    pe.sem_inc(count_used, 2)
                with pe.Fori(0, TURNS) as i:
                    for h in range(2):
                        n = i + TURNS * k
                        pe.wait_ge(rows_in[k // 3][h], (i + TURNS * (k % 3)) * (16 * U) + 16 * U)
                        pe.wait_ge(pick_ready, n * 2 + h + 1)
                        pe.wait_ge(sums_out, n * 2 + h + 1)
                        for u in range(U):
                            got = rows[:, h, u * F:(u + 1) * F]
                            pe.matmul(ps_main[:, h * 2 + u // 8, (u % 8) * F:(u % 8 + 1) * F], pick[:, h, u], got,
                                      start=True, stop=True)
                            ins = pe.matmul(ps_last[0:F, h, u:u + 1], got, pick[:, h, u, 0:1],
                                            start=True, stop=True)
                        ins.then_inc(group_done, 1)
                        if k == 0:
                            count_ends(n * 2, h)
                if k == 0:
                    close(end_counts).then_inc(counted_all, 1)

            def count_ends(m, h):
                pe.wait_ge(count_ready, m + h + 1)
                pe.sem_inc(pe_go, 1)
                for u in range(U):
                    ins = pe.matmul(end_counts, hot_end[:, h, u, 0:P], hot_end[:, h, u, P:P + J], start=False, stop=False,
                                    skip_group_check=True)
                ins.then_inc(count_used, 1)

            def turn_carries(k):
                pe.wait_ge(carry_ready, k + 1)
                for u in range(U):
                    ins = pe.transpose(ps_main[0:G, u // 8, (u % 8) * F:(u % 8 + 1) * F],
                                       tile_sum[0:F, u:T:U], ident[0:F, 0:F])
                ins.then_inc(carry_turned, 1)

            def transform_nodes(k):
                first, _, second = MATS[k]
                wide = first.shape[1]
                gin = KIND[k] == "gin"
                with pe.Fori(0, CTURNS) as i:
                    for h in range(2):
                        m = (i + CTURNS * TURNED.index(k)) * 2 + h + 1
                        pe.wait_ge(z_ready, m)
                        pe.sem_inc(pe_go, 1)
                        for c in range(C):
                            ins = pe.transpose(ps_main[0:F, c // 4, (c % 4) * P:(c % 4 + 1) * P],
                                               z[:, h, c * F:(c + 1) * F], ident[:])
                        ins.then_inc(z_turned, 1)
                        pe.wait_ge(zT_ready, m)
                        pe.sem_inc(pe_go, 1)
                        for b in range(2):
                            ins = pe.matmul(ps_main[0:wide, 2 + b, 0:CW], first, zT[:, b * CW:(b + 1) * CW],
                                            start=True, stop=True)
                        ins.then_inc(h_done, 1)
                        if gin:
                            pe.wait_ge(hT_ready, m + HT_EXTRA[k])
                            pe.sem_inc(pe_go, 1)
                            continue
                        if KIND[k] == "wide_skip":
                            pe.wait_ge(skip_ready, i * 2 + h + 1)
                            pe.sem_inc(pe_go, 1)
                        else:
                            pe.wait_ge(hT_ready, m + HT_EXTRA[k])
                            pe.sem_inc(pe_go, 1)
                        for c in range(C):
                            ins = pe.matmul(ps_out[:, 0, c * F:(c + 1) * F], hT[0:wide, c * P:(c + 1) * P], second,
                                            start=True, stop=True)
                        ins.then_inc(o_done, 1)
                if gin:
                    with pe.Fori(0, CTURNS) as i:
                        for h in range(2):
                            c = i * 2 + h
                            pe.wait_ge(hT_ready, c + (NC * (TURNED.index(k) + 1) + HT_EXTRA[k] + 1))
                            pe.wait_ge(o_taken, c + (NC * (k - 6) + 1))
                            pe.sem_inc(pe_go, 1)
                            for t in range(C):
                                ins = pe.matmul(ps_out[:, h, t * F:(t + 1) * F], bent[h][:, t * P:(t + 1) * P], second,
                                                start=True, stop=True)
                            ins.then_inc(o_done, 1)

            def layer1():
                pe.wait_ge(mask_ready, 1)
                pe.matmul(ps_last[:, 1, 0:J], tri[:], small[:, 0], start=True, stop=True)
                pe.matmul(ps_last[:, 1, P:P + J], ones[:], small[:, 0], start=True, stop=True).then_inc(mask_summed, 1)
                for_s, for_t = W["eW1"][0][:, 0], W["eW1"][0][:, 1]

                def project(m, h, wait_free):
                    pe.wait_ge(x_ready, m + 1)
                    pe.sem_inc(pe_go, 1)
                    for c in range(C):
                        ins = pe.transpose(ps_out[0:F, c // 4, (c % 4) * P:(c % 4 + 1) * P],
                                           z[:, h, c * F:(c + 1) * F], ident[:])
                    ins.then_inc(x_turned, 1)
                    pe.wait_ge(xT_ready, m + 1)
                    if wait_free:
                        pe.wait_ge(new_s_ready, m)
                        pe.wait_ge(new_t_ready, m)
                    pe.sem_inc(pe_go, 1)
                    for c in range(C):
                        at = slice((c % 4) * P, (c % 4 + 1) * P)
                        pe.matmul(ps_main[:, c // 4, at], zT[:, c * P:(c + 1) * P], for_s, start=True, stop=True)
                        ins = pe.matmul(ps_main[:, 2 + c // 4, at], zT[:, c * P:(c + 1) * P], for_t, start=True, stop=True)
                    ins.then_inc(st_done, 1)

                project(0, 0, False)
                project(1, 1, True)
                with pe.Fori(1, CTURNS) as i:
                    for h in range(2):
                        project(i * 2 + h, h, True)
                pe.wait_ge(new_s_ready, NC)
                pe.wait_ge(new_t_ready, NC)
                clear(src_counts)
                pe.sem_inc(group1_done, 2)

                def spread_runs(m, h):
                    pe.wait_ge(slot_ready, m + 1)
                    pe.wait_ge(arg_ready, m + 2)
                    pe.sem_inc(pe_go, 1)
                    for u in range(U1):
                        at = slice(u * H, (u + 1) * H)
                        ins = pe.matmul(ps_out[:, u // 4, (u % 4) * H:(u % 4 + 1) * H], slot_hot[:, h, at], rows_t[:, h, at],
                                        start=True, stop=True)
                    ins.then_inc(spread_done, 1)

                def sum_hidden(m, h):
                    pe.wait_ge(hid_ready, m + 1)
                    pe.wait_ge(pick1_ready, m + 1)
                    pe.wait_ge(sums1_out, m + 2)
                    pe.sem_inc(pe_go, 1)
                    for u in range(U1):
                        got = hid[:, h, u * H:(u + 1) * H]
                        at = slice((u % 4) * H, (u % 4 + 1) * H)
                        pe.matmul(ps_main[:, u // 4, at], pick1[:, h, u], got, start=True, stop=True)
                        pe.matmul(ps_main[:, 2 + u // 4, at], same[:, h, u], got, start=True, stop=True)
                        pe.matmul(ps_last[:, 0, u:u + 1], got, pick1[:, h, u, 0:1], start=True, stop=True)
                        ins = pe.matmul(src_counts, hot_src[:, h, u, 0:P], hot_src[:, h, u, P:P + J],
                                        start=False, stop=False, skip_group_check=True)
                    ins.then_inc(group1_done, 1)

                last = 2 * TURNS1 - 1
                spread_runs(0, 0)
                with pe.Fori(0, TURNS1 - 1) as i:
                    for h in range(2):
                        spread_runs(i * 2 + (h + 1), 1 - h)
                        sum_hidden(i * 2 + h, h)
                spread_runs(last, 1)
                sum_hidden(last - 1, 0)
                sum_hidden(last, 1)
                close(src_counts).then_inc(src_counted, 1)
                pe.wait_ge(carry1_ready, 1)
                for u in range(U):
                    ins = pe.transpose(ps_main[0:G, u // 4, (u % 4) * P:(u % 4 + 1) * P], tile_sum[:, u:T:U], ident[:])
                ins.then_inc(carry1_turned, 1)
                pe.wait_ge(carry1_in, 1)
                pe.sem_inc(sd_turned, 1)
                with pe.Fori(0, CTURNS) as i:
                    for h in range(2):
                        m = i * 2 + h + 1
                        pe.wait_ge(parts_summed, m)
                        pe.wait_ge(agg1_in[h], i * (16 * C) + 16 * C)
                        pe.sem_inc(pe_go, 1)
                        for c in range(C):
                            at = slice((c % 4) * P, (c % 4 + 1) * P)
                            for half in range(2):
                                part = part_sums[:, (half * C + c) * H:(half * C + c + 1) * H]
                                pe.matmul(ps_main[:, c // 4, at], part, ident[:], start=half == 0, stop=half == 1)
                            ins = pe.transpose(ps_main[:, 2 + c // 4, at], agg1[:, h, c * H:(c + 1) * H], ident[:])
                        ins.then_inc(sd_turned, 1)
                        pe.wait_ge(sd_ready, m)
                        pe.wait_ge(o1_taken, m)
                        pe.sem_inc(pe_go, 1)
                        for c in range(C):
                            at = slice(c * F, (c + 1) * F)
                            pe.matmul(ps_out[:, 0, at], hT[:, c * P:(c + 1) * P], W["eW2"][0][:, 0:F], start=True, stop=False)
                            ins = pe.matmul(ps_out[:, 0, at], dT[:, c * P:(c + 1) * P], W["eW2"][0][:, F:2 * F],
                                            start=False, stop=True)
                        ins.then_inc(o1_done, 1)

            for k in range(PHASES):
                sum_runs(k)
                turn_carries(k)
                if k in MATS:
                    transform_nodes(k)
                if k == 3:
                    layer1()

        @block.scalar
        def _(act):
            with if_unsorted(act):
                act.sem_inc(act_go, 1)

            def take_rows(target, n):
                act.wait_ge(ranks_out, n)
                for b in range(4):
                    ins = nc.scalar.copy(target(b), ps_main[:, b].rearrange("p (u g) -> p u g", u=4)[:, :, 0:G])
                ins.then_inc(ranks_in, 4)

            take_rows(lambda b: rank[:].rearrange("p (g u) -> p u g", u=U)[:, 4 * b:4 * b + 4], 1)
            take_rows(lambda b: keys[:, :, 2].rearrange("p g u -> p u g")[:, 4 * b:4 * b + 4], 2)

            mine = slice(HI_POOL, HI_POOL + HI_ACT)
            with act.Fori(0, TURNS) as i:
                for h in range(2):
                    act.wait_ge(kg_ready, i * 2 + h + 1)
                    act.sem_inc(act_go, 1)
                    for u in range(HI_POOL, HI_POOL + HI_ACT):
                        ins = nc.scalar.activation(hot_hi[:, h, u], iota_h[:, 0:J], ACT.Abs, bias=kg[:, h, U + u:U + u + 1], scale=-1.0)
                    ins.then_inc(distance_ready, 1)
                    act.wait_ge(distance_ready, i * 2 + h + 1)
                    act.sem_inc(act_go, 1)
                    nc.scalar.activation(hot_hi[:, h, mine], hot_hi[:, h, mine], ACT.Relu, bias=ones[:, 0:1],
                                         scale=-1.0).then_inc(act_hi_ready, 1)

            act.wait_ge(root_ready, 1)
            nc.scalar.activation(dinv[:], small[:, 0], ACT.Sqrt).then_inc(root_in, 1)
            act.sem_inc(sums_out, 2)

            def take_sums(k):
                with act.Fori(0, TURNS) as i:
                    for h in range(2):
                        m = (i + TURNS * k) * 2 + h
                        act.wait_ge(group_done, m + 3)
                        act.wait_ge(stage_free, m + 1)
                        act.sem_inc(act_go, 1)
                        for b in range(2):
                            nc.scalar.copy(stage[:, h, b * 512:(b + 1) * 512], ps_main[:, h * 2 + b])
                        nc.scalar.copy(tile_sum[0:F, bass.ds((i * 2 + h) * U, U)],
                                       ps_last[0:F, h, 0:U]).then_inc(sums_out, 1)

            def take_carries(k):
                act.wait_ge(carry_turned, k + 1)
                for b in range(2):
                    ins = nc.scalar.copy(carry_rows[0:G, b * 512:(b + 1) * 512], ps_main[0:G, b])
                ins.then_inc(carry_in, 1)

            def bend_nodes(k):
                first, bias, _ = MATS[k]
                wide = first.shape[1]
                kind = KIND[k]
                bend = ACT.Identity if kind in ("conv_out", "gin") else ACT.Relu
                with act.Fori(0, CTURNS) as i:
                    for h in range(2):
                        m = (i + CTURNS * TURNED.index(k)) * 2 + h + 1
                        act.wait_ge(z_turned, m)
                        act.sem_inc(act_go, 1)
                        nc.scalar.copy(zT[:, 0:512], ps_main[0:F, 0])
                        nc.scalar.copy(zT[:, 512:C * P], ps_main[0:F, 1, 0:C * P - 512]).then_inc(zT_ready, 1)
                        act.wait_ge(h_done, m)
                        act.sem_inc(act_go, 1)
                        if kind in ("gin", "wide"):
                            for b in range(2):
                                ins = nc.scalar.activation(big[0:wide, bass.ds((i * 2 + h) * (C * P) + b * CW, CW)],
                                                           ps_main[0:wide, 2 + b, 0:CW], bend, bias=bias)
                        if kind != "gin":
                            for b in range(2):
                                ins = nc.scalar.activation(hT[0:wide, b * CW:(b + 1) * CW],
                                                           ps_main[0:wide, 2 + b, 0:CW], bend, bias=bias)
                        ins.then_inc(hT_ready, 1)
                if kind == "gin":
                    act.wait_ge(bn_var, k - 5)
                    nc.scalar.activation(bn[:, 3:4], bn[:, 2:3], ACT.Sqrt).then_inc(bn_root, 1)
                    act.wait_ge(bn_ready, k - 5)
                    with act.Fori(0, CTURNS) as i:
                        for h in range(2):
                            c = i * 2 + h
                            act.wait_ge(o_done, c + (NC * TURNED.index(k) - 1))
                            act.sem_inc(act_go, 1)
                            nc.scalar.activation(bent[h], big[0:F, bass.ds(c * (C * P), C * P)], ACT.Relu,
                                                 bias=bn[:, 5:6], scale=bn[:, 4:5]).then_inc(hT_ready, 1)

            def root(n):
                act.wait_ge(ln_var, n)
                nc.scalar.activation(small[:, 3], small[:, 2], ACT.Sqrt).then_inc(ln_root, 1)

            def layer1():
                def turn_features(m):
                    act.wait_ge(x_turned, m + 1)
                    act.sem_inc(act_go, 1)
                    nc.scalar.copy(zT[:, 0:512], ps_out[0:F, 0])
                    nc.scalar.copy(zT[:, 512:C * P], ps_out[0:F, 1, 0:C * P - 512]).then_inc(xT_ready, 1)

                def take_targets(m, h):
                    act.wait_ge(st_done, m + 1)
                    act.wait_ge(t_free, m + 1)
                    act.sem_inc(act_go, 1)
                    nc.scalar.copy(new_t[:, h, 0:512], ps_main[:, 2])
                    nc.scalar.copy(new_t[:, h, 512:C * H], ps_main[:, 3, 0:C * H - 512]).then_inc(new_t_ready, 1)

                with act.Fori(0, CTURNS) as i:
                    for h in range(2):
                        turn_features(i * 2 + h)
                        take_targets(i * 2 + h, h)
                act.sem_inc(sums1_out, 2)

                def bend_hidden(m, h):
                    act.wait_ge(time_ready, m + 1)
                    act.sem_inc(act_go, 1)
                    nc.scalar.activation(t_emb, t_emb, ACT.Silu).then_inc(t_ready, 1)
                    act.wait_ge(arg_ready, m + 3)
                    act.sem_inc(act_go, 1)
                    nc.scalar.activation(hid[:, h], arg, ACT.Silu).then_inc(hid_ready, 1)

                def take_hidden_sums(m, h):
                    act.wait_ge(group1_done, m + 3)
                    act.wait_ge(stage1_free, m + 1)
                    act.wait_ge(added_free, m + 1)
                    act.sem_inc(act_go, 1)
                    for b in range(2):
                        nc.scalar.copy(stage[:, h, b * 512:(b + 1) * 512], ps_main[:, b])
                        nc.scalar.copy(merged[:, h, b * 512:(b + 1) * 512], ps_main[:, 2 + b])
                    nc.scalar.copy(tile_sum[:, bass.ds(m * U1, U1)], ps_last[:, 0, 0:U1]).then_inc(sums1_out, 1)

                last = 2 * TURNS1 - 1
                bend_hidden(0, 0)
                with act.Fori(0, TURNS1 - 1) as i:
                    for h in range(2):
                        bend_hidden(i * 2 + (h + 1), 1 - h)
                        take_hidden_sums(i * 2 + h, h)
                bend_hidden(last, 1)
                take_hidden_sums(last - 1, 0)
                take_hidden_sums(last, 1)
                act.wait_ge(carry1_turned, 1)
                for b in range(4):
                    ins = nc.scalar.copy(carry_rows1[0:G, b * 512:(b + 1) * 512], ps_main[0:G, b])
                ins.then_inc(carry1_in, 1)
                act.wait_ge(added, 16 * U1 * 2 * TURNS1)
                act.sem_inc(parts_free, 1)
                with act.Fori(0, NC) as c:
                    act.wait_ge(sd_turned, c + 2)
                    for b, (start, end) in enumerate(((0, 512), (512, C * P))):
                        nc.scalar.copy(hT[:, start:end], ps_main[:, b, 0:end - start])
                        ins = nc.scalar.copy(dT[:, start:end], ps_main[:, 2 + b, 0:end - start])
                    ins.then_inc(sd_ready, 1)

            for k in range(PHASES):
                take_sums(k)
                take_carries(k)
                if k in MATS:
                    bend_nodes(k)
                if k in LN_AFTER:
                    root(LN_AFTER[k])
                if k == 3:
                    layer1()
                    root(2)

        @block.vector
        def _(v):
            tt, ts = nc.vector.tensor_tensor, nc.vector.tensor_scalar
            step = v_step

            def settle():
                v.wait_ge(step.sem, step.value())

            def per_node(t, j0, n=C):
                return t[:, bass.ds(j0, n)].unsqueeze(2).to_broadcast([P, n, F])

            def split(t):
                return t.rearrange("p (j f) -> p j f", f=F)

            def sort_edges():
                def then(ins):
                    s_step.up(ins)
                    v.wait_ge(s_step.sem, s_step.value())

                def tile_hot(t):
                    v.wait_ge(digit_used, s_used[0])
                    v.sem_inc(v_go, 1)
                    then(nc.vector.tensor_copy(digit_col, digit[:, bass.ds(t, 1)]))
                    ts(digit_hot, iota_f, digit_col, None, ALU.is_equal).then_inc(digit_ready, 1)

                v.wait_ge(cols_in, 32)
                for q, source in enumerate((src_i, dst_i, edge_w, cont)):
                    then(nc.vector.tensor_copy(edges[:, :, q], source))
                for d in range(2):
                    then(nc.vector.tensor_copy(col_i, edges[:, :, 1]))
                    then(ts(col_i, col_i, *((P - 1, None, ALU.bitwise_and) if d == 0 else (7, None, ALU.logical_shift_right))))
                    then(nc.vector.tensor_copy(digit, col_i))
                    then(nc.vector.memset(digit_sum, 0.0))
                    v.sem_inc(digit_zeroed, 1)
                    used = (T + 1) * d
                    with v.Fori(0, T) as t:
                        s_step.enter(t, 1)
                        s_used = [t + (used + 1)]
                        tile_hot(t)
                        s_step.leave(T)
                    v.wait_ge(digit_counted, (T + 1) * d + 1)
                    then(nc.vector.tensor_copy(digit_sum, ps_main[:, 0, 0:P]))
                    then(nc.vector.memset(digit_tmp, 1.0))
                    then(nc.vector.tensor_tensor_scan(digit_base, digit_tmp, digit_sum, 0.0, ALU.mult, ALU.add))
                    then(tt(digit_base, digit_base, digit_sum, ALU.subtract))
                    then(ts(digit_base, digit_base, -1.0, None, ALU.add))
                    with v.Fori(0, T) as t:
                        s_step.enter(t, 5)
                        s_used = [used + T + 1]
                        tile_hot(t)
                        v.wait_ge(digit_counted, t + ((T + 1) * d + 2))
                        v.sem_inc(v_go, 1)
                        then(tt(digit_tmp, digit_base, ps_main[:, 1, 0:P], ALU.add))
                        then(nc.vector.tensor_tensor_reduce(digit_sum, digit_tmp, digit_hot, 1.0, 0.0, ALU.mult, ALU.add, digit_rank))
                        then(tt(digit_base, digit_base, ps_main[:, 2, 0:P], ALU.add))
                        v.wait_ge(edge_free, t + (T * d + 1))
                        v.sem_inc(v_go, 1)
                        then(nc.vector.tensor_copy(moving, edges[:, bass.ds(t, 1)].rearrange("p t q -> p (t q)")))
                        nc.vector.tensor_copy(move_idx, digit_rank).then_inc(rank_ready, 1)
                        v.wait_ge(rank_ready, t + (T * d + 1))
                        v.sem_inc(v_go, 1)
                        s_step.leave(T)
                    v.wait_ge(edges_in, 16 * (d + 1))
                for q, target in enumerate((src_i, dst_i, edge_w, cont)):
                    then(nc.vector.tensor_copy(target, edges[:, :, q]))
                v.sem_inc(unpacked, 1)
                v.wait_ge(again_in, 80)

            step.up(nc.vector.memset(zeros[:], 0.0))
            step.up(nc.vector.memset(hot_zero[:], 0.0))
            step.up(nc.vector.memset(ones[:], 1.0))
            step.up(nc.vector.memset(node_idx[:, J:J + 2 * C], 0))
            step.up(nc.vector.memset(src_idx_pad[:, T:T + 2 * U1], 0))
            settle()
            nc.vector.memset(row_chg, 0.0).then_inc(zero_made, 1)
            v.wait_ge(consts, 3)
            step.up(nc.vector.tensor_copy(iota_f[:], iota_i[:]))
            step.up(nc.vector.tensor_copy(iota_h[:], iota_i[:]))
            step.up(nc.vector.tensor_copy(part_f[:], part_i[:]))
            settle()
            step.up(ts(ident[:], iota_f[:], part_f[:], None, ALU.is_equal))
            step.up(ts(tri[:], iota_f[:], part_f[:], None, ALU.is_ge))
            step.up(ts(low[:], iota_f[:], part_f[:], None, ALU.is_lt))
            v.wait_ge(inputs_in, 16 * len(LOADS))
            v.wait_ge(zero_made, 1)

            step.up(nc.vector.memset(out_of_order, 0.0))
            settle()
            step.up(tt(row_chg[:, 1:U * P], row_dst[:, 1:U * P], row_dst[:, 0:U * P - 1], ALU.is_lt))
            step.up(tt(out_of_order[0:G - 1, 1:2], next_first[0:G - 1, U - 1:U], row_dst[0:G - 1, U * P - 1:U * P], ALU.is_lt))
            settle()
            step.up(nc.vector.tensor_reduce(out_of_order[0:G, 0:1], row_chg, AX.X, ALU.add))
            settle()
            tt(out_of_order[:, 0:1], out_of_order[:, 0:1], out_of_order[:, 1:2], ALU.add).then_inc(order_summed, 1)
            v.wait_ge(order_summed, 2)
            ts(sort_flag, ps_last[0:1, 0, 0:1], 1.0, None, ALU.min).then_inc(flag_ready, 1)
            with if_unsorted(v):
                sort_edges()
            step.up(nc.vector.memset(row_chg, 0.0))
            settle()

            def tiles(t):
                return t.rearrange("g (u e) -> g u e", u=U)

            chg, pre = tiles(row_chg), tiles(row_pre)
            step.up(tt(chg[:, :, 1:P], tiles(row_dst)[:, :, 1:P], tiles(row_dst)[:, :, 0:P - 1], ALU.not_equal))
            step.up(nc.vector.memset(row_rank, 1.0))
            settle()
            step.up(nc.vector.memset(tiles(row_rank)[:, :, 0:1], 0.0))
            settle()
            step.up(nc.vector.tensor_tensor_scan(row_pre, row_rank, row_chg, 0.0, ALU.mult, ALU.add))
            settle()
            in_tile = pre[:, :, P - 1:P]
            step.up(tt(tiles(row_rank), in_tile.to_broadcast([G, U, P]), pre, ALU.subtract))
            step.up(nc.vector.tensor_copy(tiles(row_val)[:, :, 0:P - 1], chg[:, :, 1:P]))
            step.up(tt(tiles(row_val)[:, :, P - 1], tiles(row_dst)[:, :, P - 1], next_first[0:G], ALU.not_equal))
            step.up(nc.vector.tensor_copy(small[0:G, 1, 0:U], tid_i[0:G, :]))
            settle()
            step.up(nc.vector.scalar_tensor_tensor(carry_idx[0:G, :], pre[:, :, P - 1], float(T), small[0:G, 1, 0:U],
                                                   ALU.mult, ALU.add))
            nc.vector.scalar_tensor_tensor(row_val, row_rank, 1.0, row_val, ALU.add, ALU.mult).then_inc(keys_ready, 1)
            nc.vector.tensor_copy(row_rank_h, row_rank).then_inc(rank_h_ready, 1)

            def parts(source, lo, hi):
                step.up(ts(col_i, source, P - 1, None, ALU.bitwise_and))
                settle()
                step.up(nc.vector.tensor_copy(keys[:, :, lo], col_i.rearrange("p (g u) -> p g u", u=U)))
                settle()
                step.up(ts(col_i, source, 7, None, ALU.logical_shift_right))
                settle()
                step.up(nc.vector.tensor_copy(keys[:, :, hi], col_i.rearrange("p (g u) -> p g u", u=U)))
                settle()

            parts(dst_i, 0, 1)
            parts(src_i, 3, 4)
            step.up(nc.vector.scalar_tensor_tensor(src_idx[:].rearrange("p (g u) -> p g u", u=U), keys[:, :, 3],
                                                   float(J), keys[:, :, 4], ALU.mult, ALU.add))
            step.up(nc.vector.scalar_tensor_tensor(dst_idx.rearrange("p (g u) -> p g u", u=U), keys[:, :, 0],
                                                   float(J), keys[:, :, 1], ALU.mult, ALU.add))
            first_i = first_b[:].bitcast(I32)
            last_i = last_b.bitcast(I32)
            step.up(nc.vector.memset(cont[:, 0:1], 0.0))
            step.up(tt(cont[:, 1:T], first_i[:, 1:T], last_i[:, 0:T - 1], ALU.is_equal))
            step.up(tt(run_sum[:], first_i, last_i, ALU.is_equal))
            settle()
            step.up(tt(chained[:], run_sum[:], cont[:], ALU.mult))

            settle()
            v.sem_inc(hot_ready, 1)
            v.wait_ge(ranks_in, 8)
            with v.Fori(0, TURNS) as i:
                for h in range(2):
                    v.wait_ge(hot_used, i * 2 + h + 1)
                    v.sem_inc(v_go, 1)
                    nc.vector.tensor_copy(kg[:, h, 0:2 * U], big[:, bass.ds((i * 2 + h) * (5 * U), 2 * U)]).then_inc(kg_ready, 1)
                    v.wait_ge(kg_ready, i * 2 + h + 1)
                    v.sem_inc(v_go, 1)
                    for u in range(U):
                        ins = ts(hot_lo[:, h, u], iota_h, kg[:, h, u:u + 1], None, ALU.is_equal)
                    for u in range(HI_POOL + HI_ACT, U):
                        ins = ts(hot_hi[:, h, u], iota_h[:, 0:J], kg[:, h, U + u:U + u + 1], None, ALU.is_equal)
                    ins.then_inc(hot_ready, 1)

            v.wait_ge(counted, 1)
            step.up(ts(small[:, 0], ps_out[:, 0, 0:J], 1.0, None, ALU.add))
            step.up(nc.vector.tensor_copy(deg_dst[:], ps_out[:, 0, 0:J]))
            settle()
            v.sem_inc(deg_ready, 2)
            v.sem_inc(root_ready, 1)
            v.wait_ge(cum_ready, 1)
            step.up(nc.vector.memset(small[:, 2], 1.0))
            step.up(nc.vector.tensor_copy(small[:, 4], ps_last[:, 1, P:P + J]))
            settle()
            step.up(nc.vector.tensor_tensor_scan(small[:, 3], small[:, 2], small[:, 4], 0.0, ALU.mult, ALU.add))
            settle()
            step.up(tt(small[:, 3], small[:, 3], small[:, 4], ALU.subtract))
            settle()
            step.up(tt(small[:, 3], small[:, 3], ps_last[:, 1, 0:J], ALU.add))
            settle()
            cum_i = small[:, 5].bitcast(I32)
            tile_i = small[:, 6].bitcast(I32)
            step.up(ts(cum_i, small[:, 3], -1.0, 0.0, ALU.add, ALU.max))
            settle()
            step.up(ts(tile_i, cum_i, 7, None, ALU.logical_shift_right))
            settle()
            step.up(nc.vector.tensor_copy(small[:, 4], tile_i))

            v.wait_ge(root_in, 1)
            settle()
            step.up(nc.vector.reciprocal(small[:, 7], dinv[:]))
            settle()
            step.up(nc.vector.tensor_copy(dinv[:], small[:, 7]))
            settle()

            def place_sums():
                v.wait_ge(counted_all, 1)
                step.up(nc.vector.tensor_copy(small[:, 1], ps_out[:, 1, 0:J]))
                settle()
                step.up(ts(small[:, 2], small[:, 1], 0.0, None, ALU.is_gt))
                step.up(nc.vector.scalar_tensor_tensor(small[:, 3], small[:, 1], float(T), small[:, 4], ALU.mult, ALU.add))
                settle()
                step.up(ts(small[:, 5], small[:, 3], float(-T - ZERO_ROW), None, ALU.add))
                settle()
                step.up(tt(small[:, 6], small[:, 5], small[:, 2], ALU.mult))
                settle()
                step.up(ts(node_idx[:, 0:J], small[:, 6], float(ZERO_ROW), None, ALU.add))
                settle()

            def place_targets():
                step.up(ts(small[:, 0], deg_dst, 0.0, None, ALU.is_gt))
                settle()
                v.sem_inc(mask_ready, 1)
                ups, so_far = tile_sum[0:1], big[0:1, 5 * W1G:5 * W1G + T]
                step.up(nc.vector.memset(ups, 1.0))
                step.up(nc.vector.memset(tile_at[:, T:T + 2 * U1], 0))
                step.up(nc.vector.scalar_tensor_tensor(run_sum[0:1], rank[0:1], 1.0, cont[0:1], ALU.add, ALU.subtract))
                settle()
                step.up(nc.vector.tensor_tensor_scan(so_far, ups, run_sum[0:1], 0.0, ALU.mult, ALU.add))
                settle()
                step.up(ts(tile_at[:, 0:T], so_far, -1.0, so_far[:, T - 1:T], ALU.mult, ALU.add))
                step.up(nc.vector.memset(small[:, 2], 1.0))
                v.wait_ge(mask_summed, 1)
                step.up(nc.vector.tensor_copy(small[:, 4], ps_last[:, 1, P:P + J]))
                settle()
                step.up(nc.vector.tensor_tensor_scan(small[:, 3], small[:, 2], small[:, 4], 0.0, ALU.mult, ALU.add))
                settle()
                step.up(tt(small[:, 5], small[:, 4], small[:, 3], ALU.subtract))
                settle()
                step.up(tt(small[:, 6], small[:, 5], ps_last[:, 1, 0:J], ALU.subtract))
                step.up(ts(small[:, 1], small[:, 0], float(-2 * NPAD), float(2 * NPAD), ALU.mult, ALU.add))
                settle()
                step.up(nc.vector.scalar_tensor_tensor(node_pos, small[:, 6], small[:, 3, J - 1:J], small[:, 1], ALU.add, ALU.add))
                settle()

            def make_table(kind, chunk, c):
                if kind == "scaled":
                    tt(split(own[:, chunk]), split(x_cur[:, chunk]), per_node(dinv, c * C), ALU.mult).then_inc(own_ready, 1)
                else:
                    nc.vector.tensor_copy(own[:, chunk], x_cur[:, chunk]).then_inc(own_ready, 1)

            CENTER_STEPS = 5

            def center(c):
                def on():
                    settle()
                    v.sem_inc(v_go, 1)

                at, nodes = bass.ds(c * (C * F), C * F), bass.ds(c * C, C)
                on()
                step.up(nc.vector.tensor_reduce(small[:, 0][:, nodes], split(x_cur[:, at]), AX.X, ALU.add))
                on()
                step.up(ts(small[:, 1][:, nodes], small[:, 0][:, nodes], 1.0 / F, None, ALU.mult))
                on()
                step.up(tt(split(own[:, at]), split(x_cur[:, at]), per_node(small[:, 1], c * C), ALU.subtract))
                on()
                step.up(tt(tmp[:], own[:, at], own[:, at], ALU.mult))
                on()
                step.up(nc.vector.tensor_reduce(small[:, 0][:, nodes], split(tmp[:]), AX.X, ALU.add))

            def count_hot(i, h):
                m = i * 2 + h
                step.up(nc.vector.tensor_copy(kg[:, h, 0:3 * U], big[:, bass.ds(m * (5 * U), 3 * U)]))
                settle()
                v.wait_ge(count_used, m + 1)
                v.sem_inc(v_go, 1)
                for u in range(U):
                    lo, hi, end = (kg[:, h, q * U + u:q * U + u + 1] for q in range(3))
                    ts(hot_end[:, h, u, 0:P], iota_h, lo, None, ALU.is_equal)
                    ins = ts(hot_end[:, h, u, P:P + J], iota_h[:, 0:J], hi, end, ALU.is_equal, ALU.mult)
                ins.then_inc(count_ready, 1)

            v.wait_ge(rank_line_out, 16)

            def pick_slots(k, weighted):
                with v.Fori(0, TURNS) as i:
                    step.enter(i, 6 if k == 0 else 4)
                    for h in range(2):
                        m = (i + TURNS * k) * 2 + h
                        at = bass.ds((i * 2 + h) * U, U)
                        v.wait_ge(group_done, m + 1)
                        v.sem_inc(v_go, 1)
                        nc.vector.tensor_copy(idx[:, h], src_idx[:, at]).then_inc(idx_ready, 1)
                        step.up(nc.vector.tensor_copy(w_g[:, h], (edge_w if weighted else rank)[:, at]))
                        step.up(nc.vector.tensor_copy(rank_g[:, h], rank[:, at]))
                        settle()
                        v.sem_inc(v_go, 1)
                        for u in range(U):
                            if weighted:
                                ins = ts(pick[:, h, u], iota_f[:], rank_g[:, h, u:u + 1], w_g[:, h, u:u + 1],
                                         ALU.is_equal, ALU.mult)
                            else:
                                ins = ts(pick[:, h, u], iota_f[:], rank_g[:, h, u:u + 1], None, ALU.is_equal)
                        ins.then_inc(pick_ready, 1)
                        if k == 0:
                            count_hot(i, h)
                    step.leave(TURNS)

            def carry_runs(k):
                v.wait_ge(sums_out, 2 * TURNS * (k + 1) + 2)
                step.up(nc.vector.tensor_tensor_scan(run_sum[0:F], chained[0:F], tile_sum[0:F], 0.0, ALU.mult, ALU.add))
                settle()
                step.up(nc.vector.memset(tile_sum[0:F, 0:1], 0.0))
                step.up(tt(tile_sum[0:F, 1:T], run_sum[0:F, 0:T - 1], cont[0:F, 1:T], ALU.mult))
                settle()
                v.sem_inc(carry_ready, 1)

            def finish_nodes(k):
                kind = KIND[k]
                per = {"wide": 1, "wide_skip": 1, "narrow": 3, "residual": 5 + CENTER_STEPS, "conv": 1, "conv_out": 3 + CENTER_STEPS, "gin": 0}[kind]
                for h in range(2):
                    nc.vector.tensor_copy(nidx[:, h], node_idx[:, h * C:(h + 1) * C]).then_inc(nidx_ready, 1)
                with v.Fori(0, CTURNS) as i:
                    step.enter(i, 2 * per)
                    for h in range(2):
                        c = i * 2 + h
                        chunk = bass.ds(c * (C * F), C * F)
                        if kind == "narrow":
                            v.wait_ge(own_ready, c + NC * (k + 1))
                        elif kind in ("residual", "conv_out"):
                            settle()
                        v.wait_ge(agg_in[h], (i + CTURNS * k) * (16 * C) + 16 * C)
                        v.sem_inc(v_go, 1)
                        if kind == "gin":
                            v.wait_ge(z_turned, c + (NC * TURNED.index(k) - 1))
                            v.sem_inc(v_go, 1)
                            tt(z[:, h], agg[:, h], own[:, chunk], ALU.add).then_inc(z_ready, 1)
                        else:
                            step.up(tt(tmp[:], agg[:, h], own[:, chunk], ALU.add))
                            settle()
                            v.sem_inc(v_go, 1)
                            ins = tt(split(z[:, h]), split(tmp[:]), per_node(dinv, c * C), ALU.mult)
                            if k in MATS:
                                ins.then_inc(z_ready, 1)
                            else:
                                step.up(ins)
                        nc.vector.tensor_copy(nidx[:, h], node_idx[:, bass.ds(c * C + 2 * C, C)]).then_inc(nidx_ready, 1)
                        if kind in ("narrow", "residual"):
                            bias = (W["b2"] if kind == "narrow" else W["b4"])[0][:]
                            settle()
                            v.sem_inc(v_go, 1)
                            step.up(tt(split(tmp[:]), split(z[:, h]), bias.unsqueeze(1).to_broadcast([P, C, F]), ALU.add))
                            settle()
                            v.sem_inc(v_go, 1)
                            if kind == "narrow":
                                nc.vector.scalar_tensor_tensor(split(own[:, chunk]), split(tmp[:]), 0.0,
                                                               per_node(dinv, c * C), ALU.max, ALU.mult).then_inc(own_ready, 1)
                            else:
                                step.up(nc.vector.scalar_tensor_tensor(z[:, h], tmp[:], 0.0, x_cur[:, chunk],
                                                                       ALU.max, ALU.add))
                                settle()
                                v.sem_inc(v_go, 1)
                                step.up(tt(x_cur[:, chunk], z[:, h], x_cur[:, chunk], ALU.add))
                                center(c)
                            continue
                        m = (i + CTURNS * TURNED.index(k)) * 2 + h + 1
                        if kind == "gin":
                            continue
                        if kind == "wide_skip":
                            v.wait_ge(hT_ready, m + HT_EXTRA[k])
                            v.sem_inc(v_go, 1)
                            tt(hT[:], hT[:], big[:, bass.ds(c * (C * P), C * P)], ALU.add).then_inc(skip_ready, 1)
                        v.wait_ge(o_done, m)
                        v.sem_inc(v_go, 1)
                        product = ps_out[:, 0, 0:C * F]
                        if kind == "conv_out":
                            step.up(tt(split(tmp[:]), split(product), W["cbl"][0][:].unsqueeze(1).to_broadcast([P, C, F]), ALU.add))
                            settle()
                            v.sem_inc(v_go, 1)
                            step.up(tt(x_cur[:, chunk], tmp[:], x_cur[:, chunk], ALU.add))
                            center(c)
                        else:
                            tt(split(own[:, chunk]), split(product), per_node(dinv, c * C), ALU.mult).then_inc(own_ready, 1)
                    step.leave(CTURNS)

            def norm_hidden(k):
                l = k - 6
                v.wait_ge(hT_ready, NC * (TURNED.index(k) + 1) + HT_EXTRA[k])
                for s in range(BN_PARTS):
                    ins = nc.vector.bn_stats(stats[:, s * 6:(s + 1) * 6], big[0:F, s * BN_LEN:(s + 1) * BN_LEN])
                step.up(ins)
                settle()
                step.up(nc.vector.bn_aggr(bn[:, 0:2], stats[:]))
                settle()
                ts(bn[:, 2:3], bn[:, 1:2], BN_EPS, None, ALU.add).then_inc(bn_var, 1)
                v.wait_ge(bn_root, l + 1)
                step.up(nc.vector.reciprocal(bn[:, 6:7], bn[:, 3:4]))
                settle()
                step.up(tt(bn[:, 4:5], bn[:, 6:7], W["gg"][0][:, l:l + 1], ALU.mult))
                settle()
                step.up(tt(bn[:, 7:8], bn[:, 0:1], bn[:, 4:5], ALU.mult))
                settle()
                tt(bn[:, 5:6], W["gbe"][0][:, l:l + 1], bn[:, 7:8], ALU.subtract).then_inc(bn_ready, 1)
                last = k == PHASES - 1
                with v.Fori(0, CTURNS) as i:
                    step.enter(i, 2 * (1 + CENTER_STEPS) if last else 0)
                    for h in range(2):
                        c = i * 2 + h
                        chunk = bass.ds(c * (C * F), C * F)
                        if last:
                            settle()
                        else:
                            v.wait_ge(own_ready, c + (NC * (k + 1) - 1))
                        v.wait_ge(o_done, c + (NC * TURNED.index(k) + 1))
                        v.sem_inc(v_go, 1)
                        tt(split(z[:, h]), split(ps_out[:, h, 0:C * F]), W["gb2"][0][:, l * F:(l + 1) * F].unsqueeze(1)
                           .to_broadcast([P, C, F]), ALU.add).then_inc(o_taken, 1)
                        v.wait_ge(o_taken, c + (NC * l + 3))
                        v.sem_inc(v_go, 1)
                        if last:
                            step.up(nc.vector.scalar_tensor_tensor(x_cur[:, chunk], z[:, h], 0.0, x_cur[:, chunk],
                                                                   ALU.max, ALU.add))
                            center(c)
                        else:
                            ts(own[:, chunk], z[:, h], 0.0, None, ALU.max).then_inc(own_ready, 1)
                    step.leave(CTURNS)

            def norm_layer(table, last=False):
                settle()
                ts(small[:, 2], small[:, 0], 1.0 / F, LN_EPS, ALU.mult, ALU.add).then_inc(ln_var, 1)
                norm_layer.n += 1
                v.wait_ge(ln_root, norm_layer.n)
                step.up(nc.vector.reciprocal(small[:, 4], small[:, 3]))
                settle()
                with v.Fori(0, NC) as c:
                    step.enter(c, 0 if last else 1)
                    chunk = bass.ds(c * (C * F), C * F)
                    ins = tt(split(x_cur[:, chunk]), split(own[:, chunk]), per_node(small[:, 4], c * C), ALU.mult)
                    if last:
                        ins.then_inc(result_ready, 1)
                    else:
                        step.up(ins)
                    if table is not None:
                        settle()
                        v.sem_inc(v_go, 1)
                        make_table(table, chunk, c)
                    step.leave(NC)
                settle()
            norm_layer.n = 0

            def layer1():
                def spread(t, n=C):
                    return t.unsqueeze(1).to_broadcast([P, n, t.shape[1]])

                def settled():
                    settle()
                    v.sem_inc(v_go, 1)

                place_targets()
                for h in range(2):
                    nc.vector.tensor_copy(z[:, h], x_cur[:, h * (C * F):(h + 1) * (C * F)]).then_inc(x_ready, 1)
                def take_sources(c, h, turn, more):
                    v.wait_ge(t_free, c + 1)
                    v.sem_inc(v_go, 1)
                    nc.vector.tensor_copy(nidx[:, h], node_pos[:, bass.ds(c * C, C)]).then_inc(pos_ready, 1)
                    v.wait_ge(st_done, c + 1)
                    v.wait_ge(s_out[h], turn * 16 + 16)
                    v.sem_inc(v_go, 1)
                    for b, n in ((0, 4), (1, C - 4)):
                        ins = tt(new_s[:, h, b * 4 * H:(b * 4 + n) * H].rearrange("p (t m) -> p t m", m=H),
                                 ps_main[:, b, 0:n * H].rearrange("p (t m) -> p t m", m=H),
                                 spread(W["eb1"][0][:], n), ALU.add)
                    ins.then_inc(new_s_ready, 1)
                    if more:
                        nc.vector.tensor_copy(z[:, h], x_cur[:, bass.ds(c * (C * F) + 2 * C * F, C * F)]).then_inc(x_ready, 1)

                with v.Fori(0, CTURNS - 1) as i:
                    for h in range(2):
                        take_sources(i * 2 + h, h, i, True)
                for h in range(2):
                    take_sources(2 * (CTURNS - 1) + h, h, CTURNS - 1, False)

                def place_group(m, h):
                    nc.vector.tensor_copy(idx[:, h, 0:U1], src_idx_pad[:, bass.ds(m * U1, U1)]).then_inc(idx1_ready, 1)
                    nc.vector.tensor_copy(tile_at_g[:, h], tile_at[:, bass.ds(m * U1, U1)]).then_inc(tile_at_ready, 1)

                for h in range(2):
                    place_group(h, h)
                v.sem_inc(arg_ready, 2)
                with v.Fori(0, TURNS1) as i:
                    step.enter(i, 2 * 5)
                    for h in range(2):
                        m = i * 2 + h
                        at = bass.ds(m * U1, U1)
                        v.wait_ge(edge_in[h], i * (16 * (U1 + 4)) + 16 * (U1 + 4))
                        v.wait_ge(arg_ready, m + 2)
                        v.sem_inc(v_go, 1)
                        ts(slot_hot[:, h], rank_b[:, h], part_f, None, ALU.is_equal).then_inc(slot_ready, 1)
                        for u in range(U1):
                            ins = nc.vector.scalar_tensor_tensor(t_emb[:, u * H:(u + 1) * H], W["eWt"][0], time_c[:, h, u:u + 1],
                                                                 W["ebt"][0], ALU.mult, ALU.add)
                        ins.then_inc(time_ready, 1)
                        v.wait_ge(group1_done, m + 1)
                        v.sem_inc(v_go, 1)
                        step.up(nc.vector.tensor_copy(rank_g[:, h, 0:U1], rank[:, at]))
                        step.up(ts(src_lo[:, h], src_c[:, h], P - 1, None, ALU.bitwise_and))
                        step.up(ts(src_hi[:, h], src_c[:, h], 7, None, ALU.logical_shift_right))
                        settled()
                        for u in range(U1):
                            one = src_c[:, h, u:u + 1]
                            ts(hot_src[:, h, u, 0:P], iota_h, src_lo[:, h, u:u + 1], None, ALU.is_equal)
                            ts(hot_src[:, h, u, P:P + J], iota_h[:, 0:J], src_hi[:, h, u:u + 1], None, ALU.is_equal)
                            ts(pick1[:, h, u], iota_f[:], rank_g[:, h, u:u + 1], None, ALU.is_equal)
                            ins = ts(same[:, h, u], src_b[:, h, u * P:(u + 1) * P], one, None, ALU.is_equal)
                        step.up(ins)
                        settled()
                        for u in range(U1):
                            ins = nc.vector.tensor_tensor_reduce(scratch[:, h, u * P:(u + 1) * P], same[:, h, u], low[:], 1.0, 0.0, ALU.mult, ALU.add,
                                                                 earlier[:, h, u:u + 1])
                        ins.then_inc(pick1_ready, 1)
                        v.wait_ge(rows1_in[h], i * (16 * U1) + 16 * U1)
                        v.wait_ge(spread_done, m + 1)
                        v.wait_ge(t_ready, m + 1)
                        v.sem_inc(v_go, 1)
                        step.up(tt(rows_s[:, h], rows_s[:, h], ps_out.rearrange("p b c -> p (b c)"), ALU.add))
                        settled()
                        tt(arg, rows_s[:, h], t_emb, ALU.add).then_inc(arg_ready, 1)
                        v.wait_ge(pick1_ready, m + 1)
                        v.wait_ge(arg_ready, m + 3)
                        v.sem_inc(v_go, 1)
                        place_group(m + 2, h)
                        v.wait_ge(added_free, m + 1)
                        v.sem_inc(v_go, 1)
                        nc.vector.scalar_tensor_tensor(add_idx[:, h], earlier[:, h], float(2 * NPAD), src_idx[:, at],
                                                       ALU.mult, ALU.add).then_inc(add_idx_ready, 1)
                    step.leave(TURNS1)
                v.wait_ge(sums1_out, 2 * TURNS1 + 2)
                step.up(nc.vector.tensor_tensor_scan(run_sum[:], chained[:], tile_sum[:], 0.0, ALU.mult, ALU.add))
                settle()
                step.up(nc.vector.memset(tile_sum[:, 0:1], 0.0))
                step.up(tt(tile_sum[:, 1:T], run_sum[:, 0:T - 1], cont[:, 1:T], ALU.mult))
                settle()
                v.sem_inc(carry1_ready, 1)
                v.wait_ge(src_counted, 1)
                step.up(nc.vector.tensor_copy(deg_src, ps_last[:, 1, 0:J]))
                settle()
                v.sem_inc(o1_taken, 1)
                for h in range(2):
                    nc.vector.tensor_copy(nidx[:, h], node_idx[:, h * C:(h + 1) * C]).then_inc(nidx1_ready, 1)
                with v.Fori(0, CTURNS) as i:
                    step.enter(i, 2 * (4 + CENTER_STEPS))
                    for h in range(2):
                        c = i * 2 + h
                        chunk = bass.ds(c * (C * F), C * F)
                        v.wait_ge(parts_in, c * (16 * U1) + 16 * U1)
                        v.wait_ge(sd_turned, c + 1)
                        v.sem_inc(v_go, 1)
                        quarter = U1 // 4 * C * H
                        step.up(tt(part_sums, parts_all[:, 0:2 * quarter], parts_all[:, 2 * quarter:4 * quarter], ALU.add))
                        settle()
                        v.sem_inc(parts_free, 1)
                        tt(part_sums[:, 0:quarter], part_sums[:, 0:quarter], part_sums[:, quarter:2 * quarter],
                           ALU.add).then_inc(parts_summed, 1)
                        settled()
                        step.up(tt(split(tmp[:]), spread(W["eb2"][0][:, 0:F]), per_node(deg_src, c * C), ALU.mult))
                        step.up(tt(split(z[:, h]), spread(W["eb2"][0][:, F:2 * F]), per_node(deg_dst, c * C), ALU.mult))
                        settled()
                        tt(tmp[:], tmp[:], z[:, h], ALU.add).then_inc(tmp_sum, 1)
                        v.wait_ge(sd_turned, c + 2)
                        v.sem_inc(v_go, 1)
                        nc.vector.tensor_copy(nidx[:, h], node_idx[:, bass.ds(c * C + 2 * C, C)]).then_inc(nidx1_ready, 1)
                        v.wait_ge(tmp_sum, c + 1)
                        v.wait_ge(o1_done, c + 1)
                        v.sem_inc(v_go, 1)
                        tt(z[:, h], tmp[:], ps_out[:, 0, 0:C * F], ALU.add).then_inc(o1_taken, 1)
                        v.wait_ge(o1_taken, c + 2)
                        v.sem_inc(v_go, 1)
                        step.up(tt(x_cur[:, chunk], z[:, h], x_cur[:, chunk], ALU.add))
                        center(c)
                    step.leave(CTURNS)
                norm_layer("scaled")

            for k in range(PHASES):
                if k == 0:
                    with v.Fori(0, NC) as c:
                        make_table("scaled", bass.ds(c * (C * F), C * F), c)
                if k == 6:
                    v.sem_inc(o_taken, 2)
                    v.wait_ge(weights_in, 16)
                pick_slots(k, weighted=k >= 6)
                carry_runs(k)
                if k == 0:
                    place_sums()
                finish_nodes(k)
                if k >= 6:
                    norm_hidden(k)
                if k in LN_AFTER:
                    norm_layer("copied" if k == 5 else None, last=k == PHASES - 1)
                if k == 3:
                    layer1()


BY_HIDDEN = ("L3_gnn_b1", "L3_gnn_gamma", "L3_gnn_beta")


def kernel(x, src, dst, edge_weight, edge_weight1, **w):
    import numpy as np
    import concourse.bacc as bacc
    from concourse.bass_utils import run_bass_kernel_spmd as run

    def padded(a, n, value):
        a = np.asarray(a).reshape(len(a), -1)
        return np.concatenate([a, np.full((n - len(a), a.shape[1]), value, a.dtype)])

    def columns(a):
        return np.ascontiguousarray(a.reshape(T, P).T)

    nodes = padded(x, NPAD, 0).reshape(J, P, F).transpose(1, 0, 2).reshape(P, J * F)
    srcs = padded(src, EPAD, PAD_NODE).reshape(-1)
    dsts = padded(dst, EPAD, PAD_NODE).reshape(-1)
    times = padded(edge_weight, EPAD, 0).reshape(-1)
    ew = padded(edge_weight1, EPAD, 0).reshape(-1)
    by_tile = dsts.reshape(T, P)
    end = np.full(1, -1, dsts.dtype)
    arrays = {
        "x_nodes": np.ascontiguousarray(nodes),
        "src_cols": columns(srcs),
        "dst_cols": columns(dsts),
        "weight_cols": columns(ew),
        "dst_rows": np.ascontiguousarray(dsts.reshape(G, U * P)),
        "tile_first": np.concatenate([by_tile[:, 0], end]),
        "tile_last": np.ascontiguousarray(by_tile[:, -1]),
        "time_cols": columns(times),
        "src_row": srcs.reshape(1, EPAD),
    }
    for name, a in w.items():
        arrays[name] = np.ascontiguousarray(np.asarray(a).T if name in BY_HIDDEN else np.asarray(a))
    nc = bacc.Bacc("TRN2", target_bir_lowering=False, num_devices=1)
    ap = {n: nc.dram_tensor("in_" + n, a.shape, mybir.dt.from_np(a.dtype), kind="ExternalInput").ap() for n, a in arrays.items()}

    def mat(name):
        return (ap[name], list(ap[name].shape), "mat")

    def row(name):
        return (ap[name], [P, ap[name].shape[0]], "row")

    def col(name):
        return (ap[name].rearrange("(p o) -> p o", o=1), [ap[name].shape[0], 1], "col")

    weights = {"W1": mat("L0_gnn_W1"), "b1": col("L0_gnn_b1"), "W2": mat("L0_gnn_W2"), "b2": row("L0_gnn_b2"),
               "W3": mat("L0_gnn_W3"), "b3": col("L0_gnn_b3"), "W4": mat("L0_gnn_W4"), "b4": row("L0_gnn_b4")}
    weights.update({"eW1": (ap["L1_gnn_W1"].rearrange("(s k) m -> k s m", s=2), [F, 2, H], "mat"),
                    "eb1": row("L1_gnn_b1"), "eWt": (ap["L1_gnn_Wt"].rearrange("o m -> (o m)"), [P, H], "row"), "ebt": row("L1_gnn_bt"),
                    "eW2": mat("L1_gnn_W2"), "eb2": row("L1_gnn_b2")})
    weights.update({"cW1": mat("L2_gnn_W1"), "cb1": col("L2_gnn_b1"), "cW2": mat("L2_gnn_W2"), "cb2": col("L2_gnn_b2"),
                    "cWl": mat("L2_gnn_Wl"), "cbl": row("L2_gnn_bl")})

    def layers_in(name):
        return (ap[name].rearrange("l k m -> k l m"), [F, 3, F], "mat")

    def layer_cols(name):
        return (ap[name], [F, 3], "mat")

    weights.update({"gW1": layers_in("L3_gnn_W1"), "gW2": layers_in("L3_gnn_W2"), "gb1": layer_cols("L3_gnn_b1"),
                    "gg": layer_cols("L3_gnn_gamma"), "gbe": layer_cols("L3_gnn_beta"),
                    "gb2": (ap["L3_gnn_b2"].rearrange("l k -> (l k)"), [P, 3 * F], "row")})
    out = nc.dram_tensor("out_0_dram", (P, J * F), F32, kind="ExternalOutput").ap()
    gnn_program(nc, ap["x_nodes"], ap["src_cols"], ap["dst_cols"], ap["weight_cols"], ap["dst_rows"], ap["tile_first"],
                ap["tile_last"], ap["time_cols"], ap["src_row"], weights, out)
    r = run(nc, [{"in_" + n: a for n, a in arrays.items()}], core_ids=[0])
    got = r.results[0]["out_0_dram"].reshape(P, J, F).transpose(1, 0, 2).reshape(NPAD, F)[:N]
    return np.ascontiguousarray(got)
```
